# Optimizing a Trainium2 kernel written in Bass

```python
import numpy as np
import jax
import jax.numpy as jnp

def _softmax(x, axis=-1):
    return jax.nn.softmax(x, axis=axis)

def _gelu(x):
    return jax.nn.gelu(x, approximate=True)

def _silu(x):
    return jax.nn.silu(x)

def _sigmoid(x):
    return jax.nn.sigmoid(x)

def _layernorm(x, axis=-1, eps=1e-05):
    m = jnp.mean(x, axis=axis, keepdims=True)
    v = jnp.var(x, axis=axis, keepdims=True)
    return (x - m) / jnp.sqrt(v + eps)

def _scatter_add(tgt, idx, src, axis=0):
    return tgt.at[idx].add(src)

def _segment_sum(src, seg, n):
    return jax.ops.segment_sum(src, seg, n)
kernel_name = 'mk_prb_d1_jaxref_r8_e626aa'

def setup_inputs(seed: int=0):
    np.random.seed(seed)
    _w = jnp.asarray

    def _L0_attn_setup():
        import jax, jax.numpy as jnp
        import numpy as np
        EMBED_DIM = 128
        NUM_HEADS = 16
        HEAD_DIM = EMBED_DIM // NUM_HEADS
        SEQ_LEN = 128
        BATCH = 4
        MAX_REL_POS = 2

        def _rel_index(length_q, length_k):
            q = jnp.arange(length_q)[:, None]
            k = jnp.arange(length_k)[None, :]
            return jnp.clip(k - q, -MAX_REL_POS, MAX_REL_POS) + MAX_REL_POS
        key = jax.random.key(seed)
        ks = jax.random.split(key, 12)
        s = 1.0 / np.sqrt(EMBED_DIM)
        x = jax.random.normal(ks[0], (BATCH, SEQ_LEN, EMBED_DIM), dtype=jnp.float32)
        W_q = jax.random.normal(ks[1], (EMBED_DIM, EMBED_DIM), dtype=jnp.float32) * s
        b_q = jnp.zeros((EMBED_DIM,), dtype=jnp.float32)
        W_k = jax.random.normal(ks[2], (EMBED_DIM, EMBED_DIM), dtype=jnp.float32) * s
        b_k = jnp.zeros((EMBED_DIM,), dtype=jnp.float32)
        W_v = jax.random.normal(ks[3], (EMBED_DIM, EMBED_DIM), dtype=jnp.float32) * s
        b_v = jnp.zeros((EMBED_DIM,), dtype=jnp.float32)
        W_o = jax.random.normal(ks[4], (EMBED_DIM, EMBED_DIM), dtype=jnp.float32) * s
        b_o = jnp.zeros((EMBED_DIM,), dtype=jnp.float32)
        lim = float(np.sqrt(6.0 / (2 * MAX_REL_POS + 1 + HEAD_DIM)))
        rel_k_table = jax.random.uniform(ks[5], (2 * MAX_REL_POS + 1, HEAD_DIM), jnp.float32, -lim, lim)
        rel_v_table = jax.random.uniform(ks[6], (2 * MAX_REL_POS + 1, HEAD_DIM), jnp.float32, -lim, lim)
        return {'x': x, 'W_q': W_q, 'b_q': b_q, 'W_k': W_k, 'b_k': b_k, 'W_v': W_v, 'b_v': b_v, 'W_o': W_o, 'b_o': b_o, 'rel_k_table': rel_k_table, 'rel_v_table': rel_v_table}
    _L0_attn_in = _L0_attn_setup()

    def _L0_ffn_setup():
        import jax, jax.numpy as jnp
        import numpy as np
        DIM = 128
        DEPTH = 6
        HEADS = 16
        DIM_HEAD = 64
        WINDOW = 32
        INNER = HEADS * DIM_HEAD
        DIM_INNER = int(DIM * 4 * 2 / 3)
        QK_SCALE = 8.0

        def shift_tokens(t):
            a, s = jnp.split(t, 2, -1)
            s = jnp.pad(s, ((0, 0), (1, 0), (0, 0)))[:, :-1]
            return jnp.concatenate([a, s], -1)

        def l2norm(t):
            return t / jnp.maximum(jnp.linalg.norm(t, axis=-1, keepdims=True), 1e-12)

        def rotate_half(x):
            x1, x2 = jnp.split(x, 2, -1)
            return jnp.concatenate([-x2, x1], -1)

        def rotary_tables(n):
            half = jnp.arange(0, DIM_HEAD, 2, dtype=jnp.float32)
            inv_freq = 1.0 / 10000.0 ** (half / DIM_HEAD)
            t = jnp.arange(n, dtype=jnp.float32)
            freqs = t[:, None] * inv_freq[None, :]
            freqs = jnp.concatenate([freqs, freqs], -1)
            base_scale = (half + 0.4 * DIM_HEAD) / (1.4 * DIM_HEAD)
            power = (t - n // 2) / (WINDOW // 2)
            scale = base_scale[None, :] ** power[:, None]
            scale = jnp.concatenate([scale, scale], -1)
            return (freqs, scale)

        def local_attention(q, k, v):
            b, h, n, d = q.shape
            w = WINDOW
            nw = n // w
            bq = q.reshape(b, h, nw, w, d)
            bk = k.reshape(b, h, nw, w, d)
            bv = v.reshape(b, h, nw, w, d)

            def look(t):
                p = jnp.pad(t, ((0, 0), (0, 0), (1, 0), (0, 0), (0, 0)))
                return jnp.concatenate([p[:, :, :nw], p[:, :, 1:]], axis=3)
            bk2, bv2 = (look(bk), look(bv))
            seq = jnp.arange(n).reshape(nw, w)
            seq_p = jnp.pad(seq, ((1, 0), (0, 0)), constant_values=-1)
            jt = jnp.concatenate([seq_p[:nw], seq_p[1:]], axis=1)
            it = seq[:, :, None]
            jb = jt[:, None, :]
            mask = (it < jb) | (it > jb + w) | (jb == -1)
            sim = jnp.einsum('bhwie,bhwje->bhwij', bq, bk2) * QK_SCALE
            sim = jnp.where(mask, -jnp.finfo(sim.dtype).max, sim)
            attn = jax.nn.softmax(sim, -1)
            out = jnp.einsum('bhwij,bhwje->bhwie', attn, bv2)
            return out.reshape(b, h, n, d)

        def attn_layer(x, Wqkv, qs, ksc, Wo):
            b, n, _ = x.shape
            qkv = x @ Wqkv
            q, k, v = jnp.split(qkv, 3, -1)
            sh = lambda t: t.reshape(b, n, HEADS, DIM_HEAD).transpose(0, 2, 1, 3)
            q, k, v = (sh(q), sh(k), sh(v))
            q = l2norm(q) * qs
            k = l2norm(k) * ksc
            freqs, scale = rotary_tables(n)
            cos, sin = (jnp.cos(freqs), jnp.sin(freqs))
            q = q * cos * scale + rotate_half(q) * sin * scale
            inv = 1.0 / scale
            k = k * cos * inv + rotate_half(k) * sin * inv
            out = local_attention(q, k, v)
            out = out.transpose(0, 2, 1, 3).reshape(b, n, INNER)
            return out @ Wo

        def ffn_layer(x, g, bln, W1, b1, W2, b2):
            mu = x.mean(-1, keepdims=True)
            var = ((x - mu) ** 2).mean(-1, keepdims=True)
            xn = (x - mu) / jnp.sqrt(var + 1e-05) * g + bln
            hg = xn @ W1 + b1
            a, gate = jnp.split(hg, 2, -1)
            return a * jax.nn.gelu(gate, approximate=False) @ W2 + b2
        key = jax.random.key(seed)
        ks = jax.random.split(key, 8)
        B, N = (2, 256)
        init = lambda k, shape: jax.random.normal(k, shape, jnp.float32) * 0.02
        return {'x': jax.random.normal(ks[0], (B, N, DIM), jnp.float32), 'Wqkv': init(ks[1], (DEPTH, DIM, 3 * INNER)), 'q_scale': jnp.ones((DEPTH, DIM_HEAD), jnp.float32), 'k_scale': jnp.ones((DEPTH, DIM_HEAD), jnp.float32), 'Wo': init(ks[2], (DEPTH, INNER, DIM)), 'ln_g': jnp.ones((DEPTH, DIM), jnp.float32), 'ln_b': jnp.zeros((DEPTH, DIM), jnp.float32), 'W1': init(ks[3], (DEPTH, DIM, 2 * DIM_INNER)), 'b1': jnp.zeros((DEPTH, 2 * DIM_INNER), jnp.float32), 'W2': init(ks[4], (DEPTH, DIM_INNER, DIM)), 'b2': jnp.zeros((DEPTH, DIM), jnp.float32)}
    _L0_ffn_in = _L0_ffn_setup()
    _d = {'L0_attn_x': _L0_attn_in['x'], 'L0_attn_W_q': _L0_attn_in['W_q'], 'L0_attn_b_q': _L0_attn_in['b_q'], 'L0_attn_W_k': _L0_attn_in['W_k'], 'L0_attn_b_k': _L0_attn_in['b_k'], 'L0_attn_W_v': _L0_attn_in['W_v'], 'L0_attn_b_v': _L0_attn_in['b_v'], 'L0_attn_W_o': _L0_attn_in['W_o'], 'L0_attn_b_o': _L0_attn_in['b_o'], 'L0_attn_rel_k_table': _L0_attn_in['rel_k_table'], 'L0_attn_rel_v_table': _L0_attn_in['rel_v_table'], 'L0_ffn_Wqkv': _L0_ffn_in['Wqkv'], 'L0_ffn_q_scale': _L0_ffn_in['q_scale'], 'L0_ffn_k_scale': _L0_ffn_in['k_scale'], 'L0_ffn_Wo': _L0_ffn_in['Wo'], 'L0_ffn_ln_g': _L0_ffn_in['ln_g'], 'L0_ffn_ln_b': _L0_ffn_in['ln_b'], 'L0_ffn_W1': _L0_ffn_in['W1'], 'L0_ffn_b1': _L0_ffn_in['b1'], 'L0_ffn_W2': _L0_ffn_in['W2'], 'L0_ffn_b2': _L0_ffn_in['b2']}
    _x0 = _d['L0_attn_x']
    _d['L0_attn_x'] = jax.random.normal(jax.random.fold_in(jax.random.key(seed), 1), (8, 512, 128), dtype=_x0.dtype)
    del _x0
    return _d

def reference(L0_attn_x, L0_attn_W_q, L0_attn_b_q, L0_attn_W_k, L0_attn_b_k, L0_attn_W_v, L0_attn_b_v, L0_attn_W_o, L0_attn_b_o, L0_attn_rel_k_table, L0_attn_rel_v_table, L0_ffn_Wqkv, L0_ffn_q_scale, L0_ffn_k_scale, L0_ffn_Wo, L0_ffn_ln_g, L0_ffn_ln_b, L0_ffn_W1, L0_ffn_b1, L0_ffn_W2, L0_ffn_b2):

    def _L0_attn_ref(x, W_q, b_q, W_k, b_k, W_v, b_v, W_o, b_o, rel_k_table, rel_v_table):
        import jax, jax.numpy as jnp
        import numpy as np
        EMBED_DIM = 128
        NUM_HEADS = 16
        HEAD_DIM = EMBED_DIM // NUM_HEADS
        SEQ_LEN = 128
        BATCH = 4
        MAX_REL_POS = 2

        def _rel_index(length_q, length_k):
            q = jnp.arange(length_q)[:, None]
            k = jnp.arange(length_k)[None, :]
            return jnp.clip(k - q, -MAX_REL_POS, MAX_REL_POS) + MAX_REL_POS
        B, S, E = x.shape
        H, D = (NUM_HEADS, HEAD_DIM)
        scale = jnp.sqrt(jnp.asarray(D, x.dtype))
        Q = x @ W_q + b_q
        K = x @ W_k + b_k
        V = x @ W_v + b_v
        Qh = Q.reshape(B, S, H, D).transpose(0, 2, 1, 3)
        Kh = K.reshape(B, S, H, D).transpose(0, 2, 1, 3)
        Vh = V.reshape(B, S, H, D).transpose(0, 2, 1, 3)
        scores = jnp.einsum('bhqd,bhkd->bhqk', Qh, Kh)
        idx = _rel_index(S, S)
        rel_k = rel_k_table[idx]
        scores = (scores + jnp.einsum('bhqd,qkd->bhqk', Qh, rel_k)) / scale
        causal = jnp.tril(jnp.ones((S, S), dtype=bool))
        scores = jnp.where(causal[None, None], scores, jnp.asarray(-1000000000.0, scores.dtype))
        attn = jax.nn.softmax(scores, axis=-1)
        out = jnp.einsum('bhqk,bhkd->bhqd', attn, Vh)
        rel_v = rel_v_table[idx]
        out = out + jnp.einsum('bhqk,qkd->bhqd', attn, rel_v)
        out = out.transpose(0, 2, 1, 3).reshape(B, S, E)
        return out @ W_o + b_o

    def _L0_ffn_ref(x, Wqkv, q_scale, k_scale, Wo, ln_g, ln_b, W1, b1, W2, b2):
        import jax, jax.numpy as jnp
        import numpy as np
        DIM = 128
        DEPTH = 6
        HEADS = 16
        DIM_HEAD = 64
        WINDOW = 32
        INNER = HEADS * DIM_HEAD
        DIM_INNER = int(DIM * 4 * 2 / 3)
        QK_SCALE = 8.0

        def shift_tokens(t):
            a, s = jnp.split(t, 2, -1)
            s = jnp.pad(s, ((0, 0), (1, 0), (0, 0)))[:, :-1]
            return jnp.concatenate([a, s], -1)

        def l2norm(t):
            return t / jnp.maximum(jnp.linalg.norm(t, axis=-1, keepdims=True), 1e-12)

        def rotate_half(x):
            x1, x2 = jnp.split(x, 2, -1)
            return jnp.concatenate([-x2, x1], -1)

        def rotary_tables(n):
            half = jnp.arange(0, DIM_HEAD, 2, dtype=jnp.float32)
            inv_freq = 1.0 / 10000.0 ** (half / DIM_HEAD)
            t = jnp.arange(n, dtype=jnp.float32)
            freqs = t[:, None] * inv_freq[None, :]
            freqs = jnp.concatenate([freqs, freqs], -1)
            base_scale = (half + 0.4 * DIM_HEAD) / (1.4 * DIM_HEAD)
            power = (t - n // 2) / (WINDOW // 2)
            scale = base_scale[None, :] ** power[:, None]
            scale = jnp.concatenate([scale, scale], -1)
            return (freqs, scale)

        def local_attention(q, k, v):
            b, h, n, d = q.shape
            w = WINDOW
            nw = n // w
            bq = q.reshape(b, h, nw, w, d)
            bk = k.reshape(b, h, nw, w, d)
            bv = v.reshape(b, h, nw, w, d)

            def look(t):
                p = jnp.pad(t, ((0, 0), (0, 0), (1, 0), (0, 0), (0, 0)))
                return jnp.concatenate([p[:, :, :nw], p[:, :, 1:]], axis=3)
            bk2, bv2 = (look(bk), look(bv))
            seq = jnp.arange(n).reshape(nw, w)
            seq_p = jnp.pad(seq, ((1, 0), (0, 0)), constant_values=-1)
            jt = jnp.concatenate([seq_p[:nw], seq_p[1:]], axis=1)
            it = seq[:, :, None]
            jb = jt[:, None, :]
            mask = (it < jb) | (it > jb + w) | (jb == -1)
            sim = jnp.einsum('bhwie,bhwje->bhwij', bq, bk2) * QK_SCALE
            sim = jnp.where(mask, -jnp.finfo(sim.dtype).max, sim)
            attn = jax.nn.softmax(sim, -1)
            out = jnp.einsum('bhwij,bhwje->bhwie', attn, bv2)
            return out.reshape(b, h, n, d)

        def attn_layer(x, Wqkv, qs, ksc, Wo):
            b, n, _ = x.shape
            qkv = x @ Wqkv
            q, k, v = jnp.split(qkv, 3, -1)
            sh = lambda t: t.reshape(b, n, HEADS, DIM_HEAD).transpose(0, 2, 1, 3)
            q, k, v = (sh(q), sh(k), sh(v))
            q = l2norm(q) * qs
            k = l2norm(k) * ksc
            freqs, scale = rotary_tables(n)
            cos, sin = (jnp.cos(freqs), jnp.sin(freqs))
            q = q * cos * scale + rotate_half(q) * sin * scale
            inv = 1.0 / scale
            k = k * cos * inv + rotate_half(k) * sin * inv
            out = local_attention(q, k, v)
            out = out.transpose(0, 2, 1, 3).reshape(b, n, INNER)
            return out @ Wo

        def ffn_layer(x, g, bln, W1, b1, W2, b2):
            mu = x.mean(-1, keepdims=True)
            var = ((x - mu) ** 2).mean(-1, keepdims=True)
            xn = (x - mu) / jnp.sqrt(var + 1e-05) * g + bln
            hg = xn @ W1 + b1
            a, gate = jnp.split(hg, 2, -1)
            return a * jax.nn.gelu(gate, approximate=False) @ W2 + b2
        for i in range(DEPTH):
            x = attn_layer(shift_tokens(x), Wqkv[i], q_scale[i], k_scale[i], Wo[i]) + x
            x = ffn_layer(shift_tokens(x), ln_g[i], ln_b[i], W1[i], b1[i], W2[i], b2[i]) + x
        return x
    x = L0_attn_x
    xn = _layernorm(x, axis=-1)
    x = x + _L0_attn_ref(xn, L0_attn_W_q, L0_attn_b_q, L0_attn_W_k, L0_attn_b_k, L0_attn_W_v, L0_attn_b_v, L0_attn_W_o, L0_attn_b_o, L0_attn_rel_k_table, L0_attn_rel_v_table) + _L0_ffn_ref(xn, L0_ffn_Wqkv, L0_ffn_q_scale, L0_ffn_k_scale, L0_ffn_Wo, L0_ffn_ln_g, L0_ffn_ln_b, L0_ffn_W1, L0_ffn_b1, L0_ffn_W2, L0_ffn_b2)
    return x

_drawn_inputs = setup_inputs


def setup_inputs(seed=0):
    import zlib

    import numpy as np

    out = dict(_drawn_inputs(seed))
    spreads = {'L0_attn_b_q': (0.0, 2.0),
     'L0_attn_b_k': (0.0, 2.0),
     'L0_attn_b_v': (0.0, 0.466),
     'L0_attn_b_o': (0.0, 0.482),
     'L0_ffn_q_scale': (1.0, 0.6),
     'L0_ffn_k_scale': (1.0, 0.6),
     'L0_ffn_ln_g': (1.0, 0.6),
     'L0_ffn_ln_b': (0.0, 0.8),
     'L0_ffn_b1': (0.0, 0.8),
     'L0_ffn_b2': (0.0, 0.1)}
    factors = {'L0_attn_rel_k_table': 3.393, 'L0_ffn_W1': 3.701, 'L0_ffn_W2': 3.635}
    for name, (base, spread) in spreads.items():
        noise = np.random.default_rng([zlib.crc32(name.encode()), seed]).standard_normal(out[name].shape)
        drawn = base * np.exp(spread * noise) if base else spread * noise
        out[name] = jnp.asarray(drawn.astype(out[name].dtype))
    for name, factor in factors.items():
        out[name] = (out[name] * factor).astype(out[name].dtype)
    return out
```

```python
from contextlib import ExitStack

import numpy as np

import concourse.bass as bass
from concourse import mybir
from concourse.alu_op_type import AluOpType as ALU

F32 = mybir.dt.float32
F32R = mybir.dt.float32r
BF16 = mybir.dt.bfloat16
I32 = mybir.dt.int32
ACT = mybir.ActivationFunctionType
X = mybir.AxisListType.X

P = 128
B, N, D = 8, 512, 128
TPS = N // P
H = 16
HA = D // H
HB = 64
INNER = H * HB
W = 32
NW = P // W
PAIRS = H // 2
LAYERS = 6
FF = int(D * 4 * 2 / 3)
FC = [(0, 128), (128, 128), (256, FF - 256)]
MASKED = -1.0e30
SCALE_A = float(np.float32(1.0) / np.sqrt(np.float32(HA)))
RSQRT_SEED = float(0x5F3759DF)
HPB = [(0, 6), (6, 6), (12, 4)]
HB1 = HB + 1

C_ID = 0
C_ROPE = C_ID + P
C_MQ = C_ROPE + 4 * TPS * HB
C_MQ0 = C_MQ + 2 * W
C_MT = C_MQ0 + 2 * W
C_MT0 = C_MT + 2 * W
C_FAR = C_MT0 + 2 * W
C_NEAR = C_FAR + P + 1
NCONST = C_NEAR + H


def constants():
    c = np.zeros((P, NCONST), np.float32)
    c[:, C_ID:C_ID + P] = np.eye(P, dtype=np.float32)
    half = np.arange(0, HB, 2, dtype=np.float32)
    inv_freq = (np.float32(1.0) / np.float32(10000.0) ** (half / np.float32(HB))).astype(np.float32)
    t = np.arange(N, dtype=np.float32)
    freqs = (t[:, None] * inv_freq[None, :]).astype(np.float32)
    base = ((half + np.float32(0.4 * HB)) / np.float32(1.4 * HB)).astype(np.float32)
    power = ((t - N // 2) / np.float32(W // 2)).astype(np.float32)
    scale = (base[None, :] ** power[:, None]).astype(np.float32)
    cos, sin = np.cos(freqs.astype(np.float64)), np.sin(freqs.astype(np.float64))
    q = 8.0 * scale.astype(np.float64)
    k = 1.0 / scale.astype(np.float64)
    tables = []
    for s in (q, k):
        tables += [np.concatenate([cos * s, cos * s], 1), np.concatenate([-sin * s, sin * s], 1)]
    rope = np.stack(tables).astype(np.float32).reshape(4, TPS, P, HB).transpose(2, 0, 1, 3)
    c[:, C_ROPE:C_MQ] = rope.reshape(P, -1)
    r, k2 = np.arange(P)[:, None] % W, np.arange(2 * W)[None, :]
    shut = np.where((k2 < r) | (k2 > r + W), MASKED, 0.0)
    c[:, C_MQ:C_MQ + 2 * W] = shut
    first = (np.arange(P)[:, None] < W) & (k2 < W)
    c[:, C_MQ0:C_MQ0 + 2 * W] = np.where(first, MASKED, shut)
    k2, r = np.arange(P)[:, None] % (2 * W), np.arange(2 * W)[None, :] % W
    shut = np.where((k2 < r) | (k2 > r + W), MASKED, 0.0)
    c[:, C_MT:C_MT + 2 * W] = shut
    first = (np.arange(P)[:, None] < W) & (np.arange(2 * W)[None, :] < W)
    c[:, C_MT0:C_MT0 + 2 * W] = np.where(first, MASKED, shut)
    far = np.arange(P + 1)[None, :] - 1 >= np.arange(P)[:, None] - 1
    c[:, C_FAR:C_FAR + P + 1] = np.where(far, MASKED, 0.0)
    c[0, C_NEAR:C_NEAR + H] = MASKED
    return c


def bc(ap, where, n):
    ap = ap.unsqueeze(where)
    return ap.broadcast_to([n if i == where else m for i, m in enumerate(ap.shape)])


def rsqrt_steps(dve, sem, count, y, x, half_x, tmp):
    def step(instruction):
        nonlocal count
        count = count + 1
        instruction.then_inc(sem, 1)
        dve.wait_ge(sem, count)

    step(dve.tensor_scalar(y.bitcast(I32), x.bitcast(I32), 1, None, ALU.arith_shift_right))
    step(dve.tensor_scalar(y.bitcast(I32), y.bitcast(I32), -1.0, RSQRT_SEED, ALU.mult, ALU.add))
    step(dve.tensor_scalar(half_x, x, -0.5, None, ALU.mult))
    for _ in range(3):
        step(dve.tensor_tensor(tmp, y, y, ALU.mult))
        step(dve.tensor_tensor(tmp, tmp, half_x, ALU.mult))
        step(dve.scalar_tensor_tensor(y, tmp, 1.5, y, ALU.add, ALU.mult))
    return count


RSQRT_OPS = 3 + 3 * 3


def norm_and_constants(nc, x, const, state, rank, eps):
    with ExitStack() as ctx:
        sb = lambda n, s, d=F32: ctx.enter_context(nc.sbuf_tensor(n, s, d))
        sem = lambda n: ctx.enter_context(nc.semaphore(n))
        NT = B * TPS
        stats = sb("n_stats", [P, NT, 6])
        mv = sb("n_mv", [P, NT, 2])
        var = sb("n_var", [P, NT])
        half_x = sb("n_half", [P, NT])
        tmp = sb("n_tmp", [P, NT])
        rstd = sb("n_rstd", [P, NT])
        x_in, const_in = sem("n_x_in"), sem("n_const_in")
        const_made, chain, stats_made, mv_made, normed = (
            sem("n_const_made"), sem("n_chain"), sem("n_stats_made"), sem("n_mv_made"), sem("n_normed"))
        tiles = state[:].rearrange("p s t d -> p (s t) d")
        block = ctx.enter_context(nc.Block())

        @block.sync
        def _(sp):
            sp.dma_start(tiles, x.rearrange("s (t p) d -> p (s t) d", p=P)).then_inc(x_in, 16)
            sp.dma_start(rank["const"][:], const).then_inc(const_in, 16)

        @block.gpsimd
        def _(pool):
            pool.memset(rank["mean_w"][:], 1.0 / D).then_inc(const_made, 1)
            pool.wait_ge(const_in, 16)
            pool.tensor_copy(rank["id_bf"][:], rank["const"][:, C_ID:C_ID + P]).then_inc(const_made, 1)
            pool.tensor_copy(rank["mask_bf"][:], rank["const"][:, C_MQ:C_NEAR]).then_inc(const_made, 1)
            pool.wait_ge(const_made, 3)

        @block.vector
        def _(dve):
            dve.wait_ge(x_in, 16)
            for i in range(NT):
                dve.bn_stats(stats[:, i, :], tiles[:, i, :]).then_inc(stats_made, 1)
            for i in range(NT):
                if i == 0:
                    dve.wait_ge(stats_made, NT)
                dve.bn_aggr(mv[:, i, :], stats[:, i, :]).then_inc(mv_made, 1)
            dve.wait_ge(mv_made, NT)
            dve.tensor_scalar(var[:], mv[:, :, 1], eps, None, ALU.add).then_inc(chain, 1)
            dve.wait_ge(chain, 1)
            rsqrt_steps(dve, chain, 1, rstd[:], var[:], half_x[:], tmp[:])
            for i in range(NT):
                dve.tensor_scalar(tiles[:, i, :], tiles[:, i, :], mv[:, i, 0:1], rstd[:, i:i + 1],
                                  ALU.subtract, ALU.mult).then_inc(normed, 1)
            dve.wait_ge(normed, NT)


def relative_attention(nc, x, Wq, bq, Wk, bk, Wv, bv, Wo, bo, rel_k, rel_v, state, total, rank):
    with ExitStack() as ctx:
        sb = lambda n, s, d=F32: ctx.enter_context(nc.sbuf_tensor(n, s, d))
        sem = lambda n: ctx.enter_context(nc.semaphore(n))
        G = 4
        NG = H // G
        w_pad = sb("a_w_pad", [P, 2, H, 32])
        b_pad = sb("a_b_pad", [P, 2, NG])
        r_pad = sb("a_r_pad", [P, 1])
        w_all = sb("a_w_all", [P, 3 * D])
        wo = sb("a_wo", [P, D])
        bias = sb("a_bias", [P, 4, D])
        rel = sb("a_rel", [P, 2, 3, HA])
        kv_bias = sb("a_kv_bias", [P, 2, 3, D])
        xa = sb("a_xa", [P, TPS, D])
        xo = sb("a_xo", [P, TPS, D])
        xT = sb("a_xT", [P, N + 1])
        qkT = sb("a_qkT", [P, 2, NG, N])
        va = sb("a_va", [P, TPS, H, HA + 1])
        near = sb("a_near", [P, 5, D])
        prod = sb("a_prod", [P, 2, D])
        s01 = sb("a_s01", [P, 2, H])
        sm = sb("a_sm", [P, H])
        far_max = sb("a_far_max", [P, H])
        nm = sb("a_nm", [P, H])
        d01 = sb("a_d01", [P, 2, H])
        p01 = sb("a_p01", [P, 2, H])
        p_sum = sb("a_p_sum", [P, H])
        pv_near = sb("a_pv_near", [P, 2, D])
        probs = sb("a_probs", [P, 4, N])
        probsT = sb("a_probsT", [P, 2, N])
        num = sb("a_num", [P, D])
        den = sb("a_den", [P, H])
        rden = sb("a_rden", [P, H])
        on = sb("a_on", [P, D])
        oT = sb("a_oT", [P, P])
        S = ctx.enter_context(nc.psum_tensor("a_S", [P, 4, 512], F32))
        PT = ctx.enter_context(nc.psum_tensor("a_PT", [P, 2, 512], F32))
        O = ctx.enter_context(nc.psum_tensor("a_O", [P, 512], F32))
        M = ctx.enter_context(nc.psum_tensor("a_M", [P, 512], F32))
        ident = rank["const"][:, C_ID:C_ID + P]
        near_mask = rank["const"][:, C_NEAR:C_NEAR + H]
        far_mask = rank["mask_bf"][:, C_FAR - C_MQ:C_FAR - C_MQ + P + 1]

        par_in, zeroed = sem("a_par_in"), sem("a_zeroed")
        bias_made = sem("a_bias_made")
        xa_in, xo_in = sem("a_xa_in"), sem("a_xo_in")
        seq_done = sem("a_seq_done")
        turned = sem("a_turned")
        xT_ready = sem("a_xT_ready")
        proj = sem("a_proj")
        qkT_ready = sem("a_qkT_ready")
        near_mm = sem("a_near_mm")
        near_ready = sem("a_near_ready")
        prods = sem("a_prods")
        s01_ready = sem("a_s01_ready")
        sm_ready = sem("a_sm_ready")
        scored = sem("a_scored")
        far_maxed = sem("a_far_maxed")
        nm_ready = sem("a_nm_ready")
        exped = sem("a_exped")
        flipped = sem("a_flipped")
        flip_dve, flip_act = sem("a_flip_dve"), sem("a_flip_act")
        summed = sem("a_summed")
        d01_ready, p01_ready = sem("a_d01_ready"), sem("a_p01_ready")
        pool_chain = sem("a_pool_chain")
        fin = sem("a_fin")
        on_T, oT_ready, y_mm = sem("a_on_T"), sem("a_oT_ready"), sem("a_y_mm")
        block = ctx.enter_context(nc.Block())
        NPAIR = TPS * PAIRS

        def region(qt):
            return (0, P, 1) if qt == 0 else (P * qt - 1, P + 1, 0)

        @block.sync
        def _(sp):
            sp.wait_ge(zeroed, 4)
            for i, w in enumerate((Wq, Wk)):
                sp.dma_start(w_pad[:, i, :, 0:HA], w.rearrange("c (h d) -> c h d", h=H)).then_inc(par_in, 16)
            for i, b in enumerate((bq, bk)):
                for g in range(G):
                    sp.dma_start(b_pad[32 * g:32 * g + HA, i, :],
                                 b.rearrange("(n g d) -> g d n", g=G, d=HA)[g],
                                 allow_slow_non_contiguous=True).then_inc(par_in, 16)
            for g in range(G):
                sp.dma_start(r_pad[32 * g:32 * g + HA, :],
                             rel_k[0:1, :].rearrange("a d -> d a"),
                             allow_slow_non_contiguous=True).then_inc(par_in, 16)
            for i, w in enumerate((Wq, Wk, Wv)):
                sp.dma_start(w_all[:, D * i:D * (i + 1)], w).then_inc(par_in, 16)
            sp.dma_start(wo[:], Wo).then_inc(par_in, 16)
            for i, b in enumerate((bq, bk, bv, bo)):
                sp.dma_start(bias[:, i, :], bc(b, 0, P)).then_inc(par_in, 16)
            for i, r in enumerate((rel_k, rel_v)):
                sp.dma_start(rel[:, i, :, :], bc(r[0:3, :], 0, P)).then_inc(par_in, 16)
            with sp.Fori(0, B) as s:
                sp.wait_ge(seq_done, s * TPS)
                sp.dma_start(xa[:], state[:, bass.ds(s, 1), :, :].rearrange("p a t d -> p (a t) d")).then_inc(xa_in, 16)
                sp.dma_start(xo[:], x[bass.ds(s, 1), :, :].rearrange("a (t p) d -> p (a t) d", p=P)).then_inc(xo_in, 16)

        PAR = 16 * (2 + 2 * G + G + 3 + 1 + 4 + 2)

        @block.gpsimd
        def _(pool):
            pool.memset(w_pad[:], 0.0).then_inc(zeroed, 1)
            pool.memset(b_pad[:], 0.0).then_inc(zeroed, 1)
            pool.memset(r_pad[:], 0.0).then_inc(zeroed, 1)
            pool.memset(xT[:, 0:1], 0.0).then_inc(zeroed, 1)
            pool.memset(va[:, :, :, HA:HA + 1], 1.0).then_inc(zeroed, 1)
            pool.wait_ge(par_in, PAR)
            for i in range(2):
                for r in range(3):
                    pool.tensor_tensor(kv_bias[:, i, r, :].rearrange("p (h d) -> p h d", h=H),
                                       bias[:, 1 + i, :].rearrange("p (h d) -> p h d", h=H),
                                       bc(rel[:, i, r, :], 1, H), ALU.add).then_inc(bias_made, 1)
            pool.tensor_tensor(b_pad[:, 1, :], b_pad[:, 1, :], r_pad[:].broadcast_to([P, NG]), ALU.add).then_inc(bias_made, 1)
            with pool.Fori(0, B) as s:
                pool.wait_ge(xo_in, 16 * s + 16)
                pool.tensor_tensor(xo[:], xo[:], bc(bias[:, 3, :], 1, TPS), ALU.add).then_inc(bias_made, 1)
                for qt in range(TPS):
                    u = s * TPS + qt
                    pool.wait_ge(near_ready, 6 * u + 3)
                    pool.wait_ge(s01_ready, 2 * u)
                    pool.tensor_tensor(prod[:, 0, :], near[:, 0, :], near[:, 1, :], ALU.mult).then_inc(prods, 1)
                    pool.tensor_tensor(prod[:, 1, :], near[:, 0, :], near[:, 2, :], ALU.mult).then_inc(prods, 1)
                    pool.wait_ge(near_ready, 6 * u + 6)
                    pool.wait_ge(p01_ready, u + 1)
                    for i in range(2):
                        pool.tensor_tensor(pv_near[:, i, :].rearrange("p (h d) -> p h d", h=H),
                                           near[:, 3 + i, :].rearrange("p (h d) -> p h d", h=H),
                                           bc(p01[:, i, :], 2, HA), ALU.mult).then_inc(pool_chain, 1)
                    pool.tensor_tensor(p_sum[:], p01[:, 0, :], p01[:, 1, :], ALU.add).then_inc(pool_chain, 1)
                    pool.wait_ge(pool_chain, 4 * u + 2)
                    pool.tensor_tensor(pv_near[:, 0, :], pv_near[:, 0, :], pv_near[:, 1, :], ALU.add).then_inc(pool_chain, 1)

        @block.tensor
        def _(pe):
            def scores(s, n):
                qt, pr = divmod(n, PAIRS)
                lo, width, skip = region(qt)
                if n >= 2:
                    pe.wait_ge(exped, 2 * (s * NPAIR + n - 1))
                for j in range(2):
                    h = 2 * pr + j
                    g, r = h // G, 32 * (h % G)
                    bank = S[:, 2 * (n % 2) + j, :]
                    pe.matmul(bank[:, lo:lo + width], rank["id_bf"][:], far_mask[:, skip:],
                              start=True, stop=False, skip_group_check=True)
                    last = pe.matmul(bank[:, 0:P * (qt + 1)], qkT[r:r + 32, 0, g, P * qt:P * (qt + 1)],
                                     qkT[r:r + 32, 1, g, 0:P * (qt + 1)], start=False, stop=True,
                                     skip_group_check=True)
                last.then_inc(scored, 1)

            def weights(s, n):
                qt, pr = divmod(n, PAIRS)
                for j in range(2):
                    pe.wait_ge(exped, 2 * (s * NPAIR + n) + j + 1)
                    pe.wait_ge((flip_dve, flip_act)[j], s * NPAIR + n)
                    for kt in range(qt + 1):
                        last = pe.transpose(PT[:, j, P * kt:P * (kt + 1)],
                                            probs[:, 2 * (n % 2) + j, P * kt:P * (kt + 1)], ident)
                    last.then_inc(flipped, 1)

            def values(s, n):
                qt, pr = divmod(n, PAIRS)
                for j in range(2):
                    h = 2 * pr + j
                    pe.wait_ge((flip_dve, flip_act)[j], s * NPAIR + n + 1)
                    for kt in range(qt + 1):
                        last = pe.matmul(O[:, 9 * h:9 * h + 9], probsT[:, j, P * kt:P * (kt + 1)],
                                         va[:, kt, h, :], start=(kt == 0), stop=(kt == qt),
                                         skip_group_check=True)
                last.then_inc(summed, 1)

            def near_products(s, qt):
                u = s * TPS + qt
                pe.wait_ge(seq_done, u)
                pe.matmul(M[:, 0:3 * D], xT[:, 1 + P * qt:1 + P * (qt + 1)], w_all[:], start=True, stop=True)
                pe.matmul(PT[:, 0, 0:2 * D], xT[:, P * qt:P * (qt + 1)], w_all[:, D:3 * D],
                          start=True, stop=True).then_inc(near_mm, 1)

            def output(s, qt):
                u = s * TPS + qt
                pe.wait_ge(fin, 4 * u + 4)
                pe.transpose(M[:, 0:P], on[:], ident).then_inc(on_T, 1)
                pe.wait_ge(oT_ready, u + 1)
                pe.matmul(M[:, P:2 * P], oT[:], wo[:], start=True, stop=True).then_inc(y_mm, 1)

            pe.wait_ge(bias_made, 7)
            pe.wait_ge(zeroed, 5)
            with pe.Fori(0, B) as s:
                pe.wait_ge(xa_in, 16 * s + 16)
                pe.wait_ge(seq_done, s * TPS)
                for t in range(TPS):
                    last = pe.transpose(M[:, P * t:P * (t + 1)], xa[:, t, :], ident)
                last.then_inc(turned, 1)
                pe.wait_ge(xT_ready, s + 1)
                for i in range(2):
                    for g in range(NG):
                        c = i * NG + g
                        if c >= 2:
                            pe.wait_ge(qkT_ready, 2 * NG * s + c - 1)
                        pe.matmul(S[:, c % 2, :], w_pad[:, i, G * g:G * (g + 1), :].rearrange("p h d -> p (h d)"),
                                  xT[:, 1:N + 1], start=True, stop=True).then_inc(proj, 1)
                pe.wait_ge(qkT_ready, 2 * NG * s + 2 * NG)
                for qt in range(TPS):
                    near_products(s, qt)
                    pe.wait_ge(near_ready, 6 * (s * TPS + qt) + 6)
                    for n in range(qt * PAIRS, (qt + 1) * PAIRS):
                        if n % PAIRS == 0:
                            scores(s, n)
                        if (n + 1) % PAIRS:
                            scores(s, n + 1)
                        weights(s, n)
                        values(s, n)
                    output(s, qt)

        @block.scalar
        def _(act):
            with act.Fori(0, B) as s:
                act.wait_ge(turned, s + 1)
                act.activation(xT[:, 1:N + 1], M[:], ACT.Copy).then_inc(xT_ready, 1)
                for i in range(2):
                    for g in range(NG):
                        c = i * NG + g
                        act.wait_ge(proj, 2 * NG * s + c + 1)
                        act.activation(qkT[:, i, g, :], S[:, c % 2, :], ACT.Identity,
                                       bias=b_pad[:, i, g:g + 1]).then_inc(qkT_ready, 1)
                for qt in range(TPS):
                    u = s * TPS + qt
                    for n in range(qt * PAIRS, (qt + 1) * PAIRS):
                        k = s * NPAIR + n
                        for j in range(2):
                            h = 2 * (n % PAIRS) + j
                            act.wait_ge(nm_ready, k + 1)
                            act.activation(probs[:, 2 * (n % 2) + j, 0:P * (qt + 1)],
                                           S[:, 2 * (n % 2) + j, 0:P * (qt + 1)], ACT.Exp,
                                           bias=nm[:, h:h + 1], scale=SCALE_A).then_inc(exped, 1)
                        act.wait_ge(flipped, 2 * k + 2)
                        if n:
                            act.wait_ge(summed, k)
                        act.activation(probsT[:, 1, 0:P * (qt + 1)], PT[:, 1, 0:P * (qt + 1)],
                                       ACT.Copy).then_inc(flip_act, 1)
                    act.wait_ge(d01_ready, 2 * u + 2)
                    act.activation(p01[:], d01[:], ACT.Exp, scale=1.0).then_inc(p01_ready, 1)
                    act.wait_ge(on_T, u + 1)
                    act.activation(oT[:], M[:, 0:P], ACT.Copy).then_inc(oT_ready, 1)

        @block.vector
        def _(dve):
            with dve.Fori(0, B) as s:
                for qt in range(TPS):
                    u = s * TPS + qt
                    dve.wait_ge(near_mm, u + 1)
                    dve.wait_ge(pool_chain, 4 * u)
                    for out, src, b in ((near[:, 0, :], M[:, 0:D], bias[:, 0, :]),
                                        (near[:, 1, :], M[:, D:2 * D], kv_bias[:, 0, 2, :]),
                                        (near[:, 2, :], PT[:, 0, 0:D], kv_bias[:, 0, 1, :]),
                                        (near[:, 3, :], M[:, 2 * D:3 * D], kv_bias[:, 1, 2, :]),
                                        (near[:, 4, :], PT[:, 0, D:2 * D], kv_bias[:, 1, 1, :])):
                        dve.tensor_tensor(out, src, b, ALU.add).then_inc(near_ready, 1)
                    dve.tensor_tensor(va[:, qt, :, 0:HA], M[:, 2 * D:3 * D].rearrange("p (h d) -> p h d", h=H),
                                      kv_bias[:, 1, 0, :].rearrange("p (h d) -> p h d", h=H),
                                      ALU.add).then_inc(near_ready, 1)
                    for i in range(2):
                        dve.wait_ge(prods, 2 * u + i + 1)
                        dve.tensor_reduce(s01[:, i, :], prod[:, i, :].rearrange("p (h d) -> p h d", h=H),
                                          X, ALU.add).then_inc(s01_ready, 1)
                    dve.wait_ge(s01_ready, 2 * u + 2)
                    c = s * (2 * TPS + 1) + (2 * qt + 1 if qt else 0)
                    if qt == 0:
                        dve.tensor_tensor(s01[:, 1, :], s01[:, 1, :], near_mask, ALU.add).then_inc(sm_ready, 1)
                        dve.wait_ge(sm_ready, c + 1)
                        c = c + 1
                    dve.tensor_tensor(sm[:], s01[:, 0, :], s01[:, 1, :], ALU.max).then_inc(sm_ready, 1)
                    dve.wait_ge(sm_ready, c + 1)
                    dve.tensor_scalar(sm[:], sm[:], -SCALE_A, None, ALU.mult).then_inc(sm_ready, 1)
                    dve.wait_ge(sm_ready, c + 2)

                    def maxima(n):
                        k = s * NPAIR + n
                        h = 2 * (n % PAIRS)
                        dve.wait_ge(scored, k + 1)
                        dve.tensor_reduce(far_max[:, h:h + 2], S[:, 2 * (n % 2):2 * (n % 2) + 2, 0:P * (qt + 1)],
                                          X, ALU.max).then_inc(far_maxed, 1)
                        dve.wait_ge(far_maxed, k + 1)
                        dve.scalar_tensor_tensor(nm[:, h:h + 2], far_max[:, h:h + 2], -SCALE_A, sm[:, h:h + 2],
                                                 ALU.mult, ALU.min).then_inc(nm_ready, 1)

                    def flip(n):
                        k = s * NPAIR + n
                        dve.wait_ge(flipped, 2 * k + 1)
                        if n:
                            dve.wait_ge(summed, k)
                        dve.tensor_copy(probsT[:, 0, 0:P * (qt + 1)],
                                        PT[:, 0, 0:P * (qt + 1)]).then_inc(flip_dve, 1)

                    first = qt * PAIRS
                    maxima(first)
                    for n in range(first, first + PAIRS):
                        if (n + 1) % PAIRS:
                            maxima(n + 1)
                        flip(n)
                    dve.wait_ge(nm_ready, s * NPAIR + first + PAIRS)
                    for i in range(2):
                        dve.scalar_tensor_tensor(d01[:, i, :], s01[:, i, :], SCALE_A, nm[:],
                                                 ALU.mult, ALU.add).then_inc(d01_ready, 1)
                    dve.wait_ge(pool_chain, 4 * u + 4)
                    dve.wait_ge(summed, s * NPAIR + first + PAIRS)
                    o = O[:, 0:9 * H].rearrange("p (h d) -> p h d", h=H)
                    dve.tensor_tensor(den[:], o[:, :, HA], p_sum[:], ALU.add).then_inc(fin, 1)
                    dve.tensor_tensor(num[:].rearrange("p (h d) -> p h d", h=H), o[:, :, 0:HA],
                                      pv_near[:, 0, :].rearrange("p (h d) -> p h d", h=H), ALU.add).then_inc(fin, 1)
                    dve.wait_ge(fin, 4 * u + 2)
                    dve.reciprocal(rden[:], den[:]).then_inc(fin, 1)
                    dve.wait_ge(fin, 4 * u + 3)
                    dve.tensor_tensor(on[:].rearrange("p (h d) -> p h d", h=H),
                                      num[:].rearrange("p (h d) -> p h d", h=H), bc(rden[:], 2, HA),
                                      ALU.mult).then_inc(fin, 1)
                    dve.wait_ge(y_mm, u + 1)
                    dve.wait_ge(bias_made, 7 + 1 + s)
                    dve.tensor_tensor(total[:, bass.ds(s, 1), qt, :],
                                      M[:, P:2 * P].unsqueeze(1),
                                      xo[:, qt, :].unsqueeze(1), ALU.add).then_inc(seq_done, 1)
            dve.wait_ge(seq_done, B * TPS)


def windowed_layers(nc, Wqkv, qs, ks, Wout, ln_g, ln_b, W1, b1, W2, b2, state, total, rank, out):
    with ExitStack() as ctx:
        sb = lambda n, s, d=F32: ctx.enter_context(nc.sbuf_tensor(n, s, d))
        sem = lambda n: ctx.enter_context(nc.semaphore(n))
        w_raw = sb("w_raw", [P, 3 * INNER])
        w_hi, w_lo = sb("w_hi", [P, 3 * INNER], F32R), sb("w_lo", [P, 3 * INNER], F32R)
        w_out = sb("w_out", [P, PAIRS, D])
        qk_scale = sb("qk_scale", [P, 4, HB])
        rope = sb("rope", [P, 4, TPS, HB])
        w1_raw = sb("w1_raw", [P, 2 * FF])
        w1_hi, w1_lo = sb("w1_hi", [P, 2 * FF], F32R), sb("w1_lo", [P, 2 * FF], F32R)
        w2 = sb("w2", [P, 3, D])
        b1c = sb("b1c", [P, 2, 3])
        gbc = sb("gbc", [P, 2])
        b2r = sb("b2r", [P, D])
        xcur = sb("xcur", [P, TPS, D])
        xsf = sb("xsf", [P, 2, P + 1])
        xh, xl = sb("xh", [P, 2, P], F32R), sb("xl", [P, 2, P], F32R)
        sq = sb("sq", [P, INNER])
        t1 = sb("t1", [P, 2, INNER])
        t2 = sb("t2", [P, 2, INNER])
        ss = sb("ss", [P, 2 * H])
        rn = sb("rn", [P, 2 * H])
        half_ss, rn_tmp = sb("half_ss", [P, 2 * H]), sb("rn_tmp", [P, 2 * H])
        qT = sb("qT", [P, PAIRS, P])
        kT = sb("kT", [P, 2, PAIRS, W + P])
        va = sb("va", [P, 2, H, HB1])
        vb = sb("vb", [P, 2, H, HB1])
        m_neg = sb("m_neg", [P, H], BF16)
        pT = sb("pT", [P, 2, 2, PAIRS, W])
        rden = sb("rden", [P, H])
        on = sb("on", [P, H, HB])
        oT = sb("oT", [P, PAIRS, P])
        credit = sb("credit", [P, 8])
        zeros = sb("zeros", [P, PAIRS, W])
        xf = sb("xf", [P, 2, TPS, D])
        fsf = sb("fsf", [P, 2, N + 1])
        cen = sb("cen", [P, 2, N])
        sqf = sb("sqf", [P, 2, N])
        var, rstd = sb("f_var", [P, 2, TPS]), sb("f_rstd", [P, 2, TPS])
        half_v, f_tmp = sb("f_half", [P, 2, TPS]), sb("f_tmp", [P, 2, TPS])
        fh, fl = sb("fh", [P, 2, N], F32R), sb("fl", [P, 2, N], F32R)
        gel = sb("gel", [P, 2, N])
        hT = sb("hT", [P, 2, 3, N])
        PS = ctx.enter_context(nc.psum_tensor("PS", [P, 8, 512], F32))
        ident = rank["const"][:, C_ID:C_ID + P]
        id_bf, mask_bf, mean_w = rank["id_bf"], rank["mask_bf"], rank["mean_w"]
        mask_q = {t: mask_bf[:, 2 * W * (t == 0):2 * W * (t == 0) + 2 * W] for t in range(TPS)}
        mask_t = {t: mask_bf[:, 4 * W + 2 * W * (t == 0):6 * W + 2 * W * (t == 0)] for t in range(TPS)}

        RN_OPS = RSQRT_OPS + 1
        FFW_IN = 16 * (1 + 3 * 3 + 2 + 1)

        made = sem("made")
        raw_in, wout_in, scale_in, ffw_in = sem("raw_in"), sem("wout_in"), sem("scale_in"), sem("ffw_in")
        x_in = [sem(f"x_in{t}") for t in range(TPS)]
        vb_in = [sem("vb_in0"), sem("vb_in1")]
        xf_in = [sem("xf_in0"), sem("xf_in1")]
        out_done = sem("out_done")
        hi_made, lo_made, rope_made = sem("hi_made"), sem("lo_made"), sem("rope_made")
        hi1_made, lo1_made = sem("hi1_made"), sem("lo1_made")
        xt_mm = sem("xt_mm")
        xsf_made = sem("xsf_made")
        xh_made, xl_made = sem("xh_made"), sem("xl_made")
        q_mm, k_mm, v_mm = sem("q_mm"), sem("k_mm"), sem("v_mm")
        sq_made = sem("sq_made")
        t_made = sem("t_made")
        ss_made = sem("ss_made")
        rn_chain = sem("rn_chain")
        added = sem("added")
        qn_made, kn_made = sem("qn_made"), sem("kn_made")
        carried = sem("carried")
        qt_mm, kt_mm = sem("qt_mm"), sem("kt_mm")
        qT_made, kT_made = sem("qT_made"), sem("kT_made")
        v_made = sem("v_made")
        s_mm = sem("s_mm")
        m_made = sem("m_made")
        st_mm = sem("st_mm")
        pt_made = sem("pt_made")
        xf_begun = sem("xf_begun")
        pv_begun = sem("pv_begun")
        pv_mm = sem("pv_mm")
        rden_made, on_made = sem("rden_made"), sem("on_made")
        ot_mm = sem("ot_mm")
        oT_made = sem("oT_made")
        y_mm = sem("y_mm")
        attn_done = sem("attn_done")
        ft_mm, fsf_made, mean_mm, cen_made = sem("ft_mm"), sem("fsf_made"), sem("mean_mm"), sem("cen_made")
        sqf_made, var_mm, f_chain, rb_mm = sem("sqf_made"), sem("var_mm"), sem("f_chain"), sem("rb_mm")
        xn_made, fh_made, fl_made, b2_made = sem("xn_made"), sem("fh_made"), sem("fl_made"), sem("b2_made")
        g_mm, a_mm = sem("g_mm"), sem("a_mm")
        gel_made, h_made = sem("gel_made"), sem("h_made")
        y2_mm = sem("y2_mm")
        ffn_done = sem("ffn_done")
        totaled = sem("totaled")
        block = ctx.enter_context(nc.Block())

        def attention(eng, lay, slot):
            for t in range(TPS):
                slot(lay, 0, t, True, t > 0)
            with eng.Fori(1, B) as s:
                for t in range(TPS):
                    slot(lay, s, t, True, True)
            slot(lay, B, 0, False, True)

        def number(lay, s, t):
            return lay * (B * TPS) + s * TPS + t

        def before(s, t):
            return (s, t - 1) if t else (s - 1, TPS - 1)

        def pairs_of_sequences(eng, body):
            with eng.Fori(0, B // 2) as pr:
                body(pr)

        @block.sync
        def _(sp):
            def load_attention(lay):
                sp.dma_start(w_raw[:], Wqkv[bass.ds(lay, 1), :, :].rearrange("a c n -> (a c) n")).then_inc(raw_in, 16)
                sp.dma_start(w_out[:], Wout[bass.ds(lay, 1), :, :].rearrange("a (j p) d -> p (a j) d", p=P)).then_inc(wout_in, 16)
                for i, v in enumerate((qs, ks)):
                    v = v[bass.ds(lay, 1), :]
                    wide = v.broadcast_to([P, HB])
                    sp.dma_start(qk_scale[:, 2 * i, :], wide).then_inc(scale_in, 16)
                    sp.dma_start(qk_scale[:, 2 * i + 1, 0:32], wide[:, 32:64]).then_inc(scale_in, 16)
                    sp.dma_start(qk_scale[:, 2 * i + 1, 32:64], wide[:, 0:32]).then_inc(scale_in, 16)

            def load_ffn(lay):
                sp.dma_start(w1_raw[:], W1[bass.ds(lay, 1), :, :].rearrange("a c n -> (a c) n")).then_inc(ffw_in, 16)
                for j, (o, w) in enumerate(FC):
                    sp.dma_start(w2[0:w, j, :], W2[bass.ds(lay, 1), o:o + w, :].rearrange("a c n -> (a c) n")).then_inc(ffw_in, 16)
                    for i in range(2):
                        sp.dma_start(b1c[0:w, i, j:j + 1],
                                     b1[bass.ds(lay, 1), FF * i + o:FF * i + o + w].rearrange("a c -> c a"),
                                     allow_slow_non_contiguous=True).then_inc(ffw_in, 16)
                for i, v in enumerate((ln_g, ln_b)):
                    sp.dma_start(gbc[:, i:i + 1], v[bass.ds(lay, 1), :].rearrange("a c -> c a"),
                                 allow_slow_non_contiguous=True).then_inc(ffw_in, 16)
                sp.dma_start(b2r[:], b2[bass.ds(lay, 1), :].broadcast_to([P, D])).then_inc(ffw_in, 16)

            def layer(lay, prefetch):
                sp.wait_ge(ffn_done, lay * B + B)
                load_ffn(lay)

                def slot(lay, s, t, has_p, has_a):
                    T = number(lay, s, t)
                    if not has_p:
                        return
                    if t == 0:
                        sp.wait_ge(ffn_done, lay * B + s + 1)
                    sp.wait_ge(attn_done, T + 1)
                    src = state[:, bass.ds(s, 1), t, :].rearrange("p a d -> p (a d)")
                    sp.dma_start(xcur[:, t, :], src).then_inc(x_in[t], 16)
                    sp.wait_ge(v_made, 2 * T + 2)
                    sp.wait_ge(pv_mm, T + 1)
                    sp.dma_start(vb[0:W, t % 2, :, :], va[P - W:P, 1 - t % 2, :, :]).then_inc(vb_in[t % 2], 16)
                    sp.dma_start(vb[W:P, t % 2, :, :], va[0:P - W, t % 2, :, :]).then_inc(vb_in[t % 2], 16)

                attention(sp, lay, slot)
                if prefetch:
                    sp.wait_ge(attn_done, lay * (B * TPS) + B * TPS + TPS)
                    load_attention(lay + 1)

                def ffn(pr):
                    sp.wait_ge(attn_done, lay * (B * TPS) + B * TPS + TPS)
                    sp.sem_inc(xf_begun, 1)
                    for a in range(2):
                        sp.wait_ge(ffn_done, lay * B + pr * 2 + a + B - 1)
                        sp.dma_start(xf[:, a, :, :],
                                     state[:, bass.ds(pr * 2 + a, 1), :, :].rearrange("p a t d -> p (a t) d")
                                     ).then_inc(xf_in[a], 16)
                pairs_of_sequences(sp, ffn)

            sp.wait_ge(made, 5)
            load_attention(0)
            with sp.Fori(0, LAYERS - 1) as lay:
                layer(lay, True)
            layer(LAYERS - 1, False)
            for s in range(B):
                sp.wait_ge(totaled, s + 1)
                sp.dma_start(out[s].rearrange("(t p) d -> p t d", p=P), total[:, s, :, :]).then_inc(out_done, 16)
            sp.wait_ge(out_done, 16 * B)

        @block.gpsimd
        def _(pool):
            pool.memset(zeros[:], 0.0).then_inc(made, 1)
            pool.memset(va[:, :, :, :], 1.0).then_inc(made, 1)
            pool.memset(fsf[:, :, 0:1], 0.0).then_inc(made, 1)
            pool.memset(kT[:], 0.0).then_inc(made, 1)
            pool.memset(b1c[:], 0.0).then_inc(made, 1)

            def layer(lay):
                pool.wait_ge(scale_in, 96 * lay + 96)
                pool.wait_ge(attn_done, lay * (B * TPS) + TPS)
                for i in range(4):
                    pool.tensor_tensor(rope[:, i, :, :],
                                       rank["const"][:, C_ROPE + i * TPS * HB:C_ROPE + (i + 1) * TPS * HB].rearrange("p (t d) -> p t d", t=TPS),
                                       bc(qk_scale[:, i, :], 1, TPS), ALU.mult).then_inc(rope_made, 1)

                def slot(lay, s, t, has_p, has_a):
                    T = number(lay, s, t)
                    if not has_p:
                        return
                    pool.wait_ge(kT_made, 2 * T)
                    left = zeros[:] if t == 0 else kT[:, 1 - t % 2, :, P:P + W]
                    pool.tensor_tensor(kT[:, t % 2, :, 0:W], left, zeros[:], ALU.add).then_inc(carried, 1)
                    for i in range(2):
                        pool.wait_ge(t_made, 4 * T + 2 * i + 2)
                        pool.tensor_tensor(t1[:, i, :], t1[:, i, :], t2[:, i, :], ALU.add).then_inc(added, 1)
                    pool.wait_ge(rn_chain, (T + 1) * RN_OPS)
                    for i, done in enumerate((qn_made, kn_made)):
                        pool.wait_ge(added, 2 * T + i + 1)
                        h = t1[:, i, :].rearrange("p (h d) -> p h d", h=H)
                        pool.tensor_tensor(h, h, bc(rn[:, H * i:H * (i + 1)], 2, HB), ALU.mult).then_inc(done, 1)
                attention(pool, lay, slot)

                def ffn(pr):
                    pool.wait_ge(ffw_in, FFW_IN * lay + FFW_IN)
                    for a in range(2):
                        pool.wait_ge(ft_mm, lay * B + pr * 2 + a + 1)
                        pool.tensor_tensor(xf[:, a, :, :], xf[:, a, :, :], bc(b2r[:], 1, TPS), ALU.add).then_inc(b2_made, 1)
                pairs_of_sequences(pool, ffn)

            with pool.Fori(0, LAYERS) as lay:
                layer(lay)

        @block.tensor
        def _(pe):
            def split_matmul(out, hi, lo, w_hi, w_lo):
                pe.matmul(out, hi, w_hi, start=True, stop=False)
                pe.matmul(out, lo, w_hi, start=False, stop=False)
                return pe.matmul(out, hi, w_lo, start=False, stop=True)

            def project(i, bank, t, done):
                for c in range(2):
                    cols = slice(INNER * i + 512 * c, INNER * i + 512 * (c + 1))
                    last = split_matmul(PS[:, bank + c, :], xh[:, t % 2, :], xl[:, t % 2, :], w_hi[:, cols], w_lo[:, cols])
                last.then_inc(done, 1)

            def slot(lay, s, t, has_p, has_a):
                T = number(lay, s, t)
                Ta = T - 1
                sa, ta = before(s, t)
                if has_p:
                    pe.wait_ge(x_in[t], 16 * (lay * B + s) + 16)
                    pe.wait_ge(attn_done, T + TPS - 1)
                    pe.transpose(PS[:, 7, 0:P], xcur[:, t, :], ident).then_inc(xt_mm, 1)
                if has_a:
                    pe.wait_ge(qT_made, 2 * T)
                    pe.wait_ge(carried, T)
                    pe.wait_ge(kT_made, 2 * T)
                    for par in range(2):
                        pe.matmul(PS[:, 4 + par, :], id_bf[:], bc(mask_q[ta], 1, PAIRS),
                                  start=True, stop=False, skip_group_check=True)
                    for pair in range(PAIRS):
                        for par in range(2):
                            rows = slice(HB * par, HB * (par + 1))
                            for w in range(NW):
                                last = pe.matmul(PS[W * w:W * (w + 1), 4 + par, 2 * W * pair:2 * W * (pair + 1)],
                                                 qT[rows, pair, W * w:W * (w + 1)],
                                                 kT[rows, ta % 2, pair, W * w:W * (w + 2)],
                                                 start=False, stop=True, skip_group_check=True)
                    last.then_inc(s_mm, 1)
                if has_p:
                    pe.wait_ge(xl_made, T + 3)
                    pe.wait_ge(qT_made, 2 * T)
                    project(0, 0, t, q_mm)
                if has_a:
                    pe.wait_ge(oT_made, 2 * Ta)
                    for par in range(2):
                        pe.matmul(PS[:, 2 + par, :], id_bf[:],
                                  bc(mask_t[ta].rearrange("p (w q) -> p w q", w=2), 2, PAIRS),
                                  start=True, stop=False, skip_group_check=True)
                    for pair in range(PAIRS):
                        for par in range(2):
                            rows = slice(HB * par, HB * (par + 1))
                            for w in range(NW):
                                half = slice(2 * W * (w // 2), 2 * W * (w // 2 + 1))
                                at = (w % 2) * PAIRS * W + W * pair
                                pe.matmul(PS[half, 2 + par, at:at + W],
                                          kT[rows, ta % 2, pair, W * w:W * (w + 2)],
                                          qT[rows, pair, W * w:W * (w + 1)],
                                          start=False, stop=False, skip_group_check=True)
                    pe.wait_ge(m_made, T)
                    for pair in range(PAIRS):
                        for par in range(2):
                            lhs = m_neg[:, PAIRS * par + pair:PAIRS * par + pair + 1].broadcast_to([P, 2 * W])
                            for half in range(2):
                                rows = slice(2 * W * half, 2 * W * (half + 1))
                                o = PS[rows, 2 + par, :].rearrange("p (w j q) -> p w j q", w=2, j=PAIRS)[:, :, pair, :]
                                last = pe.matmul(o, lhs, id_bf[:, rows].rearrange("p (w q) -> p w q", w=2),
                                                 start=False, stop=True, skip_group_check=True)
                    last.then_inc(st_mm, 1)
                if has_p:
                    pe.wait_ge(m_made, T)
                    pe.wait_ge(kT_made, 2 * T)
                    project(1, 4, t, k_mm)
                if has_a:
                    if has_p:
                        pe.wait_ge(xsf_made, 3 * T + 3)
                    pe.wait_ge(attn_done, T + TPS - 1)
                    pe.wait_ge(v_made, 2 * T)
                    pe.wait_ge(vb_in[ta % 2], 32 * (lay * (B * 2) + sa * 2 + ta // 2) + 32)
                    pe.wait_ge(pt_made, 2 * T)
                    pe.sem_inc(pv_begun, 1)
                    for h in range(H):
                        par, pair = h % 2, h // 2
                        bank, h0 = [(6, 0), (7, 6), (2, 12)][h // 6]
                        for w in range(NW):
                            half = slice(2 * W * (w // 2), 2 * W * (w // 2 + 1))
                            v = (vb if w % 2 == 0 else va)[half, ta % 2, h, :]
                            last = pe.matmul(PS[W * w:W * (w + 1), bank, HB1 * (h - h0):HB1 * (h - h0 + 1)],
                                             pT[half, par, w % 2, pair, :], v, start=True, stop=True,
                                             skip_group_check=True)
                    last.then_inc(pv_mm, 1)
                if has_p:
                    pe.wait_ge(t_made, 4 * T + 2)
                    project(2, 0, t, v_mm)
                if has_a:
                    pe.wait_ge(on_made, 2 * T)
                    for c in range(2):
                        for j in range(4):
                            pair = 4 * c + j
                            last = pe.transpose(PS[:, (3, 6)[c], P * j:P * (j + 1)],
                                                on[:, 2 * pair:2 * pair + 2, :].rearrange("p h d -> p (h d)"), ident)
                        last.then_inc(ot_mm, 1)
                    pe.wait_ge(oT_made, 2 * T)
                    for pair in range(PAIRS):
                        last = pe.matmul(PS[:, 7, 0:D], oT[:, pair, :], w_out[:, pair, :],
                                         start=(pair == 0), stop=(pair == PAIRS - 1))
                    last.then_inc(y_mm, 1)
                if has_p:
                    for i, (bank, ready, out_of, done) in enumerate(((0, qn_made, v_made, qt_mm), (4, kn_made, t_made, kt_mm))):
                        pe.wait_ge(out_of, 2 * T + 2 if i == 0 else 4 * T + 4)
                        pe.wait_ge(ready, T + 1)
                        for j in range(PAIRS):
                            last = pe.transpose(PS[:, bank + j // 4, P * (j % 4):P * (j % 4 + 1)],
                                                t1[:, i, P * j:P * (j + 1)], ident)
                        last.then_inc(done, 1)

            def ffn_pair(lay, pr):
                pe.wait_ge(attn_done, lay * (B * TPS) + B * TPS + TPS)
                pe.wait_ge(hi1_made, lay + 1)
                pe.wait_ge(lo1_made, lay + 1)
                for a in range(2):
                    U = lay * B + pr * 2 + a
                    first = (0, 6)[a]
                    pe.wait_ge(xf_in[a], 16 * (lay * (B // 2) + pr) + 16)
                    pe.wait_ge(ffn_done, U + B - 1)
                    for t in range(TPS):
                        last = pe.transpose(PS[:, first, P * t:P * (t + 1)], xf[:, a, t, :], ident)
                    last.then_inc(ft_mm, 1)
                for a in range(2):
                    pe.wait_ge(fsf_made, 2 * (lay * B + pr * 2 + a) + 2)
                    pe.matmul(PS[:, (1, 7)[a], :], mean_w[:], fsf[:, a, 0:N], start=True, stop=True).then_inc(mean_mm, 1)
                for a in range(2):
                    pe.wait_ge(sqf_made, lay * B + pr * 2 + a + 1)
                    for t in range(TPS):
                        last = pe.matmul(PS[:, (1, 7)[a], t:t + 1], sqf[:, a, P * t:P * (t + 1)], mean_w[:, 0:1],
                                         start=True, stop=True, skip_group_check=True)
                    last.then_inc(var_mm, 1)
                for a in range(2):
                    pe.wait_ge(f_chain, (lay * B + pr * 2 + a + 1) * RN_OPS)
                    for t in range(TPS):
                        last = pe.matmul(PS[:, (1, 7)[a], P * t:P * (t + 1)], rstd[:, a, t:t + 1].broadcast_to([P, P]),
                                         ident, start=True, stop=True, skip_group_check=True)
                    last.then_inc(rb_mm, 1)
                pe.wait_ge(ffw_in, FFW_IN * lay + FFW_IN)
                for a in range(2):
                    U = lay * B + pr * 2 + a
                    pe.wait_ge(fl_made, U + 1)
                    for j, (o, w) in enumerate(FC):
                        for i, (sem_read, done) in enumerate(((gel_made, g_mm), (h_made, a_mm))):
                            bank = 2 + (6 * a + 2 * j + i) % 4
                            pe.wait_ge(sem_read, 3 * U + j)
                            cols = slice(FF * (1 - i) + o, FF * (1 - i) + o + w)
                            split_matmul(PS[0:w, bank, :], w1_hi[:, cols], w1_lo[:, cols], fh[:, a, :], fl[:, a, :]).then_inc(done, 1)
                    pe.wait_ge(h_made, 3 * U + 4)
                    for t in range(TPS):
                        for j, (o, w) in enumerate(FC):
                            last = pe.matmul(PS[:, (0, 6)[a], P * t:P * (t + 1)], hT[0:w, a, j, P * t:P * (t + 1)],
                                             w2[0:w, j, :], start=(j == 0), stop=(j == 2), skip_group_check=True)
                    last.then_inc(y2_mm, 1)

            pe.wait_ge(made, 5)
            with pe.Fori(0, LAYERS) as lay:
                pe.wait_ge(ffn_done, lay * B + B)
                pe.wait_ge(hi_made, 3 * lay + 3)
                pe.wait_ge(lo_made, 3 * lay + 3)
                pe.wait_ge(wout_in, 16 * lay + 16)

                attention(pe, lay, slot)
                pairs_of_sequences(pe, lambda pr: ffn_pair(lay, pr))

        @block.scalar
        def _(act):
            copy = lambda o, i: act.activation(o, i, ACT.Copy)

            def slot(lay, s, t, has_p, has_a):
                T = number(lay, s, t)
                p = t % 2
                if has_p:
                    act.wait_ge(xt_mm, T + 1)
                    act.wait_ge(xl_made, T + 1)
                    act.wait_ge(xsf_made, 3 * T)
                    copy(xsf[0:64, p, 0:P], PS[0:64, 7, 0:P]).then_inc(xsf_made, 1)
                    copy(xsf[64:P, p, 1:P + 1], PS[64:P, 7, 0:P]).then_inc(xsf_made, 1)
                    copy(xsf[64:P, p, 0:1], zeros[64:P, 0, 0:1] if t == 0 else xsf[64:P, 1 - p, P:P + 1]).then_inc(xsf_made, 1)
                    for c in range(2):
                        act.wait_ge(q_mm, T + 1)
                        act.wait_ge(ss_made, 2 * T)
                        act.activation(sq[:, 512 * c:512 * (c + 1)], PS[:, c, :], ACT.Square).then_inc(sq_made, 1)
                if has_a:
                    act.wait_ge(st_mm, T)
                    act.wait_ge(pv_mm, T + 1)
                    for par in range(2):
                        act.activation(pT[:, par, :, :, :].rearrange("p w j q -> p (w j q)"), PS[:, 2 + par, :],
                                       ACT.Exp).then_inc(pt_made, 1)
                if has_p:
                    for c in range(2):
                        act.wait_ge(k_mm, T + 1)
                        act.wait_ge(ss_made, 2 * T + 1)
                        act.activation(sq[:, 512 * c:512 * (c + 1)], PS[:, 4 + c, :], ACT.Square).then_inc(sq_made, 1)
                    act.wait_ge(v_mm, T + 3)
                    act.wait_ge(pv_mm, T + 1)
                    if t:
                        act.wait_ge(vb_in[1 - p], 32 * (lay * (B * 2) + s * 2 + (t - 1) // 2) + 32)
                    else:
                        act.wait_ge(vb_in[1], 32 * (lay * (B * 2) + s * 2))
                    for c in range(2):
                        copy(va[:, p, 8 * c:8 * (c + 1), 0:HB],
                             PS[:, c, :].rearrange("p (h d) -> p h d", h=8)).then_inc(v_made, 1)
                if has_a:
                    for c in range(2):
                        act.wait_ge(ot_mm, 2 * T - 1 + c)
                        act.wait_ge(y_mm, T - 1)
                        copy(oT[:, 4 * c:4 * (c + 1), :],
                             PS[:, (3, 6)[c], :].rearrange("p (j q) -> p j q", j=4)).then_inc(oT_made, 1)
                if has_p:
                    act.wait_ge(qt_mm, T + 1)
                    for c in range(2):
                        copy(qT[:, 4 * c:4 * (c + 1), :], PS[:, c, :].rearrange("p (j q) -> p j q", j=4)).then_inc(qT_made, 1)
                    act.wait_ge(kt_mm, T + 1)
                    for c in range(2):
                        copy(kT[:, p, 4 * c:4 * (c + 1), W:], PS[:, 4 + c, :].rearrange("p (j q) -> p j q", j=4)).then_inc(kT_made, 1)

            def ffn_pair(lay, pr):
                for a in range(2):
                    act.wait_ge(ft_mm, lay * B + pr * 2 + a + 1)
                    copy(fsf[0:64, a, 0:N], PS[0:64, (0, 6)[a], :]).then_inc(fsf_made, 1)
                    copy(fsf[64:P, a, 1:N + 1], PS[64:P, (0, 6)[a], :]).then_inc(fsf_made, 1)
                for a in range(2):
                    act.wait_ge(cen_made, lay * B + pr * 2 + a + 1)
                    act.activation(sqf[:, a, :], cen[:, a, :], ACT.Square).then_inc(sqf_made, 1)
                for a in range(2):
                    for j, (o, w) in enumerate(FC):
                        C = (lay * B + pr * 2 + a) * 3 + j
                        act.wait_ge(g_mm, C + 1)
                        act.wait_ge(h_made, C)
                        act.activation(gel[0:w, (3 * a + j) % 2, :], PS[0:w, 2 + (6 * a + 2 * j) % 4, :], ACT.Gelu,
                                       bias=b1c[0:w, 1, j:j + 1]).then_inc(gel_made, 1)

            act.wait_ge(made, 5)
            copy(credit[:, 7:8], zeros[:, 0, 0:1]).then_inc(gel_made, 1)
            with act.Fori(0, LAYERS) as lay:
                act.wait_ge(raw_in, 16 * lay + 16)
                act.wait_ge(ffn_done, lay * B + B)
                for i in range(3):
                    copy(w_hi[:, INNER * i:INNER * (i + 1)], w_raw[:, INNER * i:INNER * (i + 1)]).then_inc(hi_made, 1)
                attention(act, lay, slot)
                act.wait_ge(ffw_in, FFW_IN * lay + FFW_IN)
                copy(w1_hi[:], w1_raw[:]).then_inc(hi1_made, 1)
                pairs_of_sequences(act, lambda pr: ffn_pair(lay, pr))

        @block.vector
        def _(dve):
            def slot(lay, s, t, has_p, has_a):
                T = number(lay, s, t)
                Ta = T - 1
                sa, ta = before(s, t)
                p = t % 2
                if has_p:
                    dve.wait_ge(xsf_made, 3 * T + 3)
                    dve.wait_ge(v_mm, T + 1)
                    dve.tensor_copy(xh[:, p, :], xsf[:, p, 0:P]).then_inc(xh_made, 1)
                    dve.wait_ge(xh_made, T + 1)
                    dve.tensor_tensor(xl[:, p, :], xsf[:, p, 0:P], xh[:, p, :].bitcast(F32), ALU.subtract).then_inc(xl_made, 1)
                if has_a:
                    dve.wait_ge(s_mm, T)
                    dve.tensor_reduce(m_neg[:].rearrange("p (r j) -> p r j", r=2),
                                      PS[:, 4:6, :].rearrange("p r (j k) -> p r j k", j=PAIRS),
                                      X, ALU.max, negate=True).then_inc(m_made, 1)
                if has_p:
                    for i, (bank, turned) in enumerate(((0, qt_mm), (4, kt_mm))):
                        dve.wait_ge(turned, T)
                        for c in range(2):
                            dve.wait_ge(sq_made, 4 * T + 2 * i + c + 1)
                            src = PS[:, bank + c, :].rearrange("p (h d) -> p h d", h=8)
                            cols = slice(512 * c, 512 * (c + 1))
                            o1 = t1[:, i, cols].rearrange("p (h d) -> p h d", h=8)
                            o2 = t2[:, i, cols].rearrange("p (h d) -> p h d", h=8)
                            dve.tensor_tensor(o1, src, bc(rope[:, 2 * i, t, :], 1, 8), ALU.mult)
                            dve.tensor_tensor(o2[:, :, 0:32], src[:, :, 32:64], bc(rope[:, 2 * i + 1, t, 0:32], 1, 8), ALU.mult)
                            dve.tensor_tensor(o2[:, :, 32:64], src[:, :, 0:32], bc(rope[:, 2 * i + 1, t, 32:64], 1, 8),
                                              ALU.mult).then_inc(t_made, 1)
                        dve.tensor_reduce(ss[:, H * i:H * (i + 1)], sq[:].rearrange("p (h d) -> p h d", h=H),
                                          X, ALU.add).then_inc(ss_made, 1)
                    dve.wait_ge(ss_made, 2 * T + 2)
                    dve.wait_ge(kn_made, T)
                    dve.tensor_scalar(ss[:], ss[:], 1e-24, None, ALU.max).then_inc(rn_chain, 1)
                    dve.wait_ge(rn_chain, T * RN_OPS + 1)
                    rsqrt_steps(dve, rn_chain, T * RN_OPS + 1, rn[:], ss[:], half_ss[:], rn_tmp[:])
                if has_a:
                    dve.wait_ge(pv_mm, T + 2)
                    outs = ((PS[:, 6:8, 0:6 * HB1].rearrange("p b (h e) -> p b h e", e=HB1), 0, 12, 2),
                            (PS[:, 2:3, 0:4 * HB1].rearrange("p b (h e) -> p b h e", e=HB1), 12, 4, 1))
                    for o, h0, nh, nb in outs:
                        dve.reciprocal(rden[:, h0:h0 + nh].rearrange("p (b h) -> p b h", b=nb), o[:, :, :, HB]).then_inc(rden_made, 1)
                    for k, (o, h0, nh, nb) in enumerate(outs):
                        dve.wait_ge(rden_made, 2 * T - 1 + k)
                        dve.tensor_tensor(on[:, h0:h0 + nh, :].rearrange("p (b h) d -> p b h d", b=nb), o[:, :, :, 0:HB],
                                          bc(rden[:, h0:h0 + nh].rearrange("p (b h) -> p b h", b=nb), 3, HB),
                                          ALU.mult).then_inc(on_made, 1)
                    dve.wait_ge(y_mm, T)
                    dve.tensor_tensor(state[:, bass.ds(sa, 1), ta, :], PS[:, 7, 0:D].unsqueeze(1),
                                      xcur[:, ta, :].unsqueeze(1), ALU.add).then_inc(attn_done, 1)

            def ffn_pair(lay, pr):
                for a in range(2):
                    dve.wait_ge(fsf_made, 2 * (lay * B + pr * 2 + a) + 2)
                    dve.wait_ge(mean_mm, lay * B + pr * 2 + a + 1)
                    dve.tensor_tensor(cen[:, a, :], fsf[:, a, 0:N], PS[:, (1, 7)[a], :], ALU.subtract).then_inc(cen_made, 1)
                for a in range(2):
                    c = (lay * B + pr * 2 + a) * RN_OPS
                    dve.wait_ge(var_mm, lay * B + pr * 2 + a + 1)
                    dve.tensor_scalar(var[:, a, :], PS[:, (1, 7)[a], 0:TPS], 1e-5, None, ALU.add).then_inc(f_chain, 1)
                    dve.wait_ge(f_chain, c + 1)
                    rsqrt_steps(dve, f_chain, c + 1, rstd[:, a, :], var[:, a, :], half_v[:, a, :], f_tmp[:, a, :])
                for a in range(2):
                    U = lay * B + pr * 2 + a
                    dve.wait_ge(rb_mm, U + 1)
                    dve.tensor_tensor(cen[:, a, :], cen[:, a, :], PS[:, (1, 7)[a], :], ALU.mult).then_inc(xn_made, 1)
                    dve.wait_ge(xn_made, 2 * U + 1)
                    dve.tensor_scalar(cen[:, a, :], cen[:, a, :], gbc[:, 0:1], gbc[:, 1:2], ALU.mult, ALU.add).then_inc(xn_made, 1)
                    dve.wait_ge(xn_made, 2 * U + 2)
                    dve.tensor_copy(fh[:, a, :], cen[:, a, :]).then_inc(fh_made, 1)
                    dve.wait_ge(fh_made, U + 1)
                    dve.tensor_tensor(fl[:, a, :], cen[:, a, :], fh[:, a, :].bitcast(F32), ALU.subtract).then_inc(fl_made, 1)
                for a in range(2):
                    U = lay * B + pr * 2 + a
                    for j, (o, w) in enumerate(FC):
                        dve.wait_ge(a_mm, 3 * U + j + 1)
                        dve.wait_ge(gel_made, 3 * U + j + 2)
                        dve.scalar_tensor_tensor(hT[0:w, a, j, :], PS[0:w, 2 + (6 * a + 2 * j + 1) % 4, :],
                                                 b1c[0:w, 0, j:j + 1], gel[0:w, (3 * a + j) % 2, :],
                                                 ALU.add, ALU.mult).then_inc(h_made, 1)
                    dve.wait_ge(y2_mm, U + 1)
                    dve.wait_ge(b2_made, U + 1)
                    dve.tensor_tensor(state[:, bass.ds(pr * 2 + a, 1), :, :].rearrange("p a t d -> p (a t) d"),
                                      PS[:, (0, 6)[a], :].rearrange("p (t d) -> p t d", t=TPS),
                                      xf[:, a, :, :], ALU.add).then_inc(ffn_done, 1)

            dve.wait_ge(made, 5)
            for i, (target, n) in enumerate(((xl_made, 2), (v_mm, 2), (pv_mm, 2), (attn_done, 4), (h_made, 1), (ffn_done, B))):
                dve.memset(credit[:, i:i + 1], 0.0).then_inc(target, n)
            with dve.Fori(0, LAYERS) as lay:
                dve.wait_ge(rope_made, 4 * lay + 4)
                for i in range(3):
                    dve.wait_ge(hi_made, 3 * lay + i + 1)
                    cols = slice(INNER * i, INNER * (i + 1))
                    dve.tensor_tensor(w_lo[:, cols], w_raw[:, cols], w_hi[:, cols].bitcast(F32), ALU.subtract).then_inc(lo_made, 1)
                attention(dve, lay, slot)
                dve.wait_ge(hi1_made, lay + 1)
                dve.tensor_tensor(w1_lo[:], w1_raw[:], w1_hi[:].bitcast(F32), ALU.subtract).then_inc(lo1_made, 1)
                pairs_of_sequences(dve, lambda pr: ffn_pair(lay, pr))
            dve.wait_ge(ffn_done, LAYERS * B + B)
            for s in range(B):
                dve.tensor_tensor(total[:, s, :, :], total[:, s, :, :], state[:, s, :, :], ALU.add).then_inc(totaled, 1)


def build(nc, x, Wq, bq, Wk, bk, Wv, bv, Wo, bo, rel_k, rel_v, Wqkv, qs, ks, Wout, ln_g, ln_b,
          W1, b1, W2, b2, const, out, only=None):
    with ExitStack() as ctx:
        sb = lambda n, s, d=F32: ctx.enter_context(nc.sbuf_tensor(n, s, d))
        state = sb("state", [P, B, TPS, D])
        total = sb("total", [P, B, TPS, D])
        rank = {"const": sb("constants", [P, NCONST]), "id_bf": sb("id_bf", [P, P], BF16),
                "mask_bf": sb("mask_bf", [P, C_NEAR - C_MQ], BF16), "mean_w": sb("mean_w", [P, P])}
        norm_and_constants(nc, x, const, state, rank, 1e-5)
        relative_attention(nc, x, Wq, bq, Wk, bk, Wv, bv, Wo, bo, rel_k, rel_v, state, total, rank)
        if only == "A":
            with nc.semaphore("z") as z, nc.Block() as block:
                @block.sync
                def _(sp):
                    sp.dma_start(out.rearrange("s (t p) d -> p (s t) d", p=P), total[:].rearrange("p s t d -> p (s t) d")).then_inc(z, 16)
                    sp.wait_ge(z, 16)
            return
        windowed_layers(nc, Wqkv, qs, ks, Wout, ln_g, ln_b, W1, b1, W2, b2, state, total, rank, out)


_INS = ["x", "W_q", "b_q", "W_k", "b_k", "W_v", "b_v", "W_o", "b_o", "rel_k_table", "rel_v_table"]
_INS = ["L0_attn_" + n for n in _INS] + ["L0_ffn_" + n for n in (
    "Wqkv", "q_scale", "k_scale", "Wo", "ln_g", "ln_b", "W1", "b1", "W2", "b2")]


def kernel(**inputs):
    import concourse.bacc as bacc
    from concourse.bass_utils import run_bass_kernel_spmd

    nc = bacc.Bacc("TRN2", target_bir_lowering=False, num_devices=1)
    arrays, args = {}, []
    for name in _INS + ["const"]:
        a = constants() if name == "const" else np.ascontiguousarray(inputs[name])
        arrays["in_" + name] = a
        args.append(nc.dram_tensor("in_" + name, a.shape, mybir.dt.from_np(a.dtype), kind="ExternalInput").ap())
    args.append(nc.dram_tensor("out_0", (B, N, D), F32, kind="ExternalOutput").ap())
    build(nc, *args)
    return run_bass_kernel_spmd(nc, [arrays], core_ids=[0]).results[0]["out_0"]
```

```python
from contextlib import ExitStack

import numpy as np

import concourse.bass as bass
from concourse import mybir
from concourse.alu_op_type import AluOpType as ALU

F32 = mybir.dt.float32
F32R = mybir.dt.float32r
BF16 = mybir.dt.bfloat16
I32 = mybir.dt.int32
ACT = mybir.ActivationFunctionType
X = mybir.AxisListType.X

P = 128
B, N, D = 8, 512, 128
TPS = N // P
H = 16
HA = D // H
HB = 64
INNER = H * HB
W = 32
NW = P // W
PAIRS = H // 2
LAYERS = 6
FF = int(D * 4 * 2 / 3)
FC = [(0, 128), (128, 128), (256, FF - 256)]
MASKED = -1.0e30
SCALE_A = float(np.float32(1.0) / np.sqrt(np.float32(HA)))
RSQRT_SEED = float(0x5F3759DF)
HB1 = HB + 1

C_ID = 0
C_ROPE = C_ID + P
C_MQ = C_ROPE + 4 * TPS * HB
C_MQ0 = C_MQ + 2 * W
C_FAR = C_MQ0 + 2 * W
C_NEAR = C_FAR + P + 1
NCONST = C_NEAR + H


def constants():
    c = np.zeros((P, NCONST), np.float32)
    c[:, C_ID:C_ID + P] = np.eye(P, dtype=np.float32)
    half = np.arange(0, HB, 2, dtype=np.float32)
    inv_freq = (np.float32(1.0) / np.float32(10000.0) ** (half / np.float32(HB))).astype(np.float32)
    t = np.arange(N, dtype=np.float32)
    freqs = (t[:, None] * inv_freq[None, :]).astype(np.float32)
    base = ((half + np.float32(0.4 * HB)) / np.float32(1.4 * HB)).astype(np.float32)
    power = ((t - N // 2) / np.float32(W // 2)).astype(np.float32)
    scale = (base[None, :] ** power[:, None]).astype(np.float32)
    cos, sin = np.cos(freqs.astype(np.float64)), np.sin(freqs.astype(np.float64))
    q = 8.0 * scale.astype(np.float64)
    k = 1.0 / scale.astype(np.float64)
    tables = []
    for s in (q, k):
        tables += [np.concatenate([cos * s, cos * s], 1), np.concatenate([-sin * s, sin * s], 1)]
    rope = np.stack(tables).astype(np.float32).reshape(4, TPS, P, HB).transpose(2, 0, 1, 3)
    c[:, C_ROPE:C_MQ] = rope.reshape(P, -1)
    r, k2 = np.arange(P)[:, None] % W, np.arange(2 * W)[None, :]
    shut = np.where((k2 < r) | (k2 > r + W), MASKED, 0.0)
    c[:, C_MQ:C_MQ + 2 * W] = shut
    first = (np.arange(P)[:, None] < W) & (k2 < W)
    c[:, C_MQ0:C_MQ0 + 2 * W] = np.where(first, MASKED, shut)
    far = np.arange(P + 1)[None, :] - 1 >= np.arange(P)[:, None] - 1
    c[:, C_FAR:C_FAR + P + 1] = np.where(far, MASKED, 0.0)
    c[0, C_NEAR:C_NEAR + H] = MASKED
    return c


def bc(ap, where, n):
    ap = ap.unsqueeze(where)
    return ap.broadcast_to([n if i == where else m for i, m in enumerate(ap.shape)])


def rsqrt_steps(dve, sem, count, y, x, half_x, tmp):
    def step(instruction):
        nonlocal count
        count = count + 1
        instruction.then_inc(sem, 1)

    step(dve.tensor_scalar(y.bitcast(I32), x.bitcast(I32), 1, None, ALU.arith_shift_right))
    dve.wait_ge(sem, count)
    step(dve.tensor_scalar(y.bitcast(I32), y.bitcast(I32), -1.0, RSQRT_SEED, ALU.mult, ALU.add))
    step(dve.tensor_scalar(half_x, x, -0.5, None, ALU.mult))
    for _ in range(3):
        dve.wait_ge(sem, count)
        step(dve.tensor_tensor(tmp, y, y, ALU.mult))
        dve.wait_ge(sem, count)
        step(dve.tensor_tensor(tmp, tmp, half_x, ALU.mult))
        dve.wait_ge(sem, count)
        step(dve.scalar_tensor_tensor(y, tmp, 1.5, y, ALU.add, ALU.mult))


RSQRT_OPS = 3 + 3 * 3


def norm_and_constants(nc, x, const, state, rank, eps):
    with ExitStack() as ctx:
        sb = lambda n, s, d=F32: ctx.enter_context(nc.sbuf_tensor(n, s, d))
        sem = lambda n: ctx.enter_context(nc.semaphore(n))
        NT = B * TPS
        stats = sb("n_stats", [P, NT, 6])
        mv = sb("n_mv", [P, NT, 2])
        var = sb("n_var", [P, NT])
        half_x = sb("n_half", [P, NT])
        tmp = sb("n_tmp", [P, NT])
        rstd = sb("n_rstd", [P, NT])
        x_in, const_in = sem("n_x_in"), sem("n_const_in")
        const_made, chain, stats_made, mv_made, normed = (
            sem("n_const_made"), sem("n_chain"), sem("n_stats_made"), sem("n_mv_made"), sem("n_normed"))
        tiles = state[:].rearrange("p s t d -> p (s t) d")
        block = ctx.enter_context(nc.Block())

        @block.sync
        def _(sp):
            sp.dma_start(tiles, x.rearrange("s (t p) d -> p (s t) d", p=P)).then_inc(x_in, 16)
            sp.dma_start(rank["const"][:], const).then_inc(const_in, 16)

        @block.gpsimd
        def _(pool):
            pool.memset(rank["mean_w"][:], 1.0 / D).then_inc(const_made, 1)
            pool.wait_ge(const_in, 16)
            pool.tensor_copy(rank["id_bf"][:], rank["const"][:, C_ID:C_ID + P]).then_inc(const_made, 1)
            pool.tensor_copy(rank["mask_bf"][:], rank["const"][:, C_MQ:C_NEAR]).then_inc(const_made, 1)
            pool.wait_ge(const_made, 3)

        @block.vector
        def _(dve):
            dve.wait_ge(x_in, 16)
            for i in range(NT):
                dve.bn_stats(stats[:, i, :], tiles[:, i, :]).then_inc(stats_made, 1)
            for i in range(NT):
                if i == 0:
                    dve.wait_ge(stats_made, NT)
                dve.bn_aggr(mv[:, i, :], stats[:, i, :]).then_inc(mv_made, 1)
            dve.wait_ge(mv_made, NT)
            dve.tensor_scalar(var[:], mv[:, :, 1], eps, None, ALU.add).then_inc(chain, 1)
            dve.wait_ge(chain, 1)
            rsqrt_steps(dve, chain, 1, rstd[:], var[:], half_x[:], tmp[:])
            dve.wait_ge(chain, 1 + RSQRT_OPS)
            for i in range(NT):
                dve.tensor_scalar(tiles[:, i, :], tiles[:, i, :], mv[:, i, 0:1], rstd[:, i:i + 1],
                                  ALU.subtract, ALU.mult).then_inc(normed, 1)
            dve.wait_ge(normed, NT)


def relative_attention(nc, x, Wq, bq, Wk, bk, Wv, bv, Wo, bo, rel_k, rel_v, state, total, rank):
    with ExitStack() as ctx:
        sb = lambda n, s, d=F32: ctx.enter_context(nc.sbuf_tensor(n, s, d))
        sem = lambda n: ctx.enter_context(nc.semaphore(n))
        G = 4
        NG = H // G
        w_pad = sb("a_w_pad", [P, 2, H, 32])
        b_pad = sb("a_b_pad", [P, 2, NG])
        r_pad = sb("a_r_pad", [P, 1])
        w_all = sb("a_w_all", [P, 3 * D])
        wo = sb("a_wo", [P, D])
        bias = sb("a_bias", [P, 4, D])
        rel = sb("a_rel", [P, 2, 3, HA])
        kv_bias = sb("a_kv_bias", [P, 2, 3, D])
        xa = sb("a_xa", [P, TPS, D])
        xo = sb("a_xo", [P, TPS, D])
        xT = sb("a_xT", [P, N + 1])
        qkT = sb("a_qkT", [P, 2, NG, N])
        va = sb("a_va", [P, TPS, H, HA + 1])
        near = sb("a_near", [P, 5, D])
        prod = sb("a_prod", [P, 2, D])
        s01 = sb("a_s01", [P, 2, H])
        sm = sb("a_sm", [P, H])
        far_max = sb("a_far_max", [P, H])
        nm = sb("a_nm", [P, H])
        d01 = sb("a_d01", [P, 2, H])
        p01 = sb("a_p01", [P, 2, H])
        p_sum = sb("a_p_sum", [P, H])
        pv_near = sb("a_pv_near", [P, 2, D])
        probs = sb("a_probs", [P, 4, N])
        probsT = sb("a_probsT", [P, 2, N])
        num = sb("a_num", [P, D])
        den = sb("a_den", [P, H])
        rden = sb("a_rden", [P, H])
        on = sb("a_on", [P, D])
        oT = sb("a_oT", [P, P])
        S = ctx.enter_context(nc.psum_tensor("a_S", [P, 4, 512], F32))
        PT = ctx.enter_context(nc.psum_tensor("a_PT", [P, 2, 512], F32))
        O = ctx.enter_context(nc.psum_tensor("a_O", [P, 512], F32))
        M = ctx.enter_context(nc.psum_tensor("a_M", [P, 512], F32))
        ident = rank["const"][:, C_ID:C_ID + P]
        near_mask = rank["const"][:, C_NEAR:C_NEAR + H]
        far_mask = rank["mask_bf"][:, C_FAR - C_MQ:C_FAR - C_MQ + P + 1]

        par_in, zeroed = sem("a_par_in"), sem("a_zeroed")
        bias_made = sem("a_bias_made")
        xa_in, xo_in = sem("a_xa_in"), sem("a_xo_in")
        seq_done = sem("a_seq_done")
        turned = sem("a_turned")
        xT_ready = sem("a_xT_ready")
        proj = sem("a_proj")
        qkT_ready = sem("a_qkT_ready")
        near_mm = sem("a_near_mm")
        near_ready = sem("a_near_ready")
        prods = sem("a_prods")
        s01_ready = sem("a_s01_ready")
        sm_ready = sem("a_sm_ready")
        scored = sem("a_scored")
        far_maxed = sem("a_far_maxed")
        nm_ready = sem("a_nm_ready")
        exped = sem("a_exped")
        flipped = sem("a_flipped")
        flip_dve, flip_act = sem("a_flip_dve"), sem("a_flip_act")
        summed = sem("a_summed")
        d01_ready, p01_ready = sem("a_d01_ready"), sem("a_p01_ready")
        pool_chain = sem("a_pool_chain")
        fin = sem("a_fin")
        on_T, oT_ready, y_mm = sem("a_on_T"), sem("a_oT_ready"), sem("a_y_mm")
        block = ctx.enter_context(nc.Block())
        NPAIR = TPS * PAIRS

        def region(qt):
            return (0, P, 1) if qt == 0 else (P * qt - 1, P + 1, 0)

        @block.sync
        def _(sp):
            sp.wait_ge(zeroed, 4)
            for i, w in enumerate((Wq, Wk)):
                sp.dma_start(w_pad[:, i, :, 0:HA], w.rearrange("c (h d) -> c h d", h=H)).then_inc(par_in, 16)
            for i, b in enumerate((bq, bk)):
                for g in range(G):
                    sp.dma_start(b_pad[32 * g:32 * g + HA, i, :],
                                 b.rearrange("(n g d) -> g d n", g=G, d=HA)[g],
                                 allow_slow_non_contiguous=True).then_inc(par_in, 16)
            for g in range(G):
                sp.dma_start(r_pad[32 * g:32 * g + HA, :],
                             rel_k[0:1, :].rearrange("a d -> d a"),
                             allow_slow_non_contiguous=True).then_inc(par_in, 16)
            for i, w in enumerate((Wq, Wk, Wv)):
                sp.dma_start(w_all[:, D * i:D * (i + 1)], w).then_inc(par_in, 16)
            sp.dma_start(wo[:], Wo).then_inc(par_in, 16)
            for i, b in enumerate((bq, bk, bv, bo)):
                sp.dma_start(bias[:, i, :], bc(b, 0, P)).then_inc(par_in, 16)
            for i, r in enumerate((rel_k, rel_v)):
                sp.dma_start(rel[:, i, :, :], bc(r[0:3, :], 0, P)).then_inc(par_in, 16)
            with sp.Fori(0, B) as s:
                sp.wait_ge(seq_done, s * TPS)
                sp.dma_start(xa[:], state[:, bass.ds(s, 1), :, :].rearrange("p a t d -> p (a t) d")).then_inc(xa_in, 16)
                sp.dma_start(xo[:], x[bass.ds(s, 1), :, :].rearrange("a (t p) d -> p (a t) d", p=P)).then_inc(xo_in, 16)

        PAR = 16 * (2 + 2 * G + G + 3 + 1 + 4 + 2)

        @block.gpsimd
        def _(pool):
            pool.memset(w_pad[:], 0.0).then_inc(zeroed, 1)
            pool.memset(b_pad[:], 0.0).then_inc(zeroed, 1)
            pool.memset(r_pad[:], 0.0).then_inc(zeroed, 1)
            pool.memset(xT[:, 0:1], 0.0).then_inc(zeroed, 1)
            pool.memset(va[:, :, :, HA:HA + 1], 1.0).then_inc(zeroed, 1)
            pool.wait_ge(par_in, PAR)
            for i in range(2):
                for r in range(3):
                    pool.tensor_tensor(kv_bias[:, i, r, :].rearrange("p (h d) -> p h d", h=H),
                                       bias[:, 1 + i, :].rearrange("p (h d) -> p h d", h=H),
                                       bc(rel[:, i, r, :], 1, H), ALU.add).then_inc(bias_made, 1)
            pool.tensor_tensor(b_pad[:, 1, :], b_pad[:, 1, :], r_pad[:].broadcast_to([P, NG]), ALU.add).then_inc(bias_made, 1)
            with pool.Fori(0, B) as s:
                pool.wait_ge(xo_in, 16 * s + 16)
                pool.tensor_tensor(xo[:], xo[:], bc(bias[:, 3, :], 1, TPS), ALU.add).then_inc(bias_made, 1)
                for qt in range(TPS):
                    u = s * TPS + qt
                    pool.wait_ge(near_ready, 6 * u + 3)
                    pool.wait_ge(s01_ready, 2 * u)
                    pool.tensor_tensor(prod[:, 0, :], near[:, 0, :], near[:, 1, :], ALU.mult).then_inc(prods, 1)
                    pool.tensor_tensor(prod[:, 1, :], near[:, 0, :], near[:, 2, :], ALU.mult).then_inc(prods, 1)
                    pool.wait_ge(near_ready, 6 * u + 6)
                    pool.wait_ge(p01_ready, u + 1)
                    for i in range(2):
                        pool.tensor_tensor(pv_near[:, i, :].rearrange("p (h d) -> p h d", h=H),
                                           near[:, 3 + i, :].rearrange("p (h d) -> p h d", h=H),
                                           bc(p01[:, i, :], 2, HA), ALU.mult).then_inc(pool_chain, 1)
                    pool.tensor_tensor(p_sum[:], p01[:, 0, :], p01[:, 1, :], ALU.add).then_inc(pool_chain, 1)
                    pool.wait_ge(pool_chain, 4 * u + 2)
                    pool.tensor_tensor(pv_near[:, 0, :], pv_near[:, 0, :], pv_near[:, 1, :], ALU.add).then_inc(pool_chain, 1)

        @block.tensor
        def _(pe):
            def scores(s, n):
                qt, pr = divmod(n, PAIRS)
                lo, width, skip = region(qt)
                if n >= 2:
                    pe.wait_ge(exped, 2 * (s * NPAIR + n - 1))
                for j in range(2):
                    h = 2 * pr + j
                    g, r = h // G, 32 * (h % G)
                    bank = S[:, 2 * (n % 2) + j, :]
                    pe.matmul(bank[:, lo:lo + width], rank["id_bf"][:], far_mask[:, skip:],
                              start=True, stop=False, skip_group_check=True)
                    last = pe.matmul(bank[:, 0:P * (qt + 1)], qkT[r:r + 32, 0, g, P * qt:P * (qt + 1)],
                                     qkT[r:r + 32, 1, g, 0:P * (qt + 1)], start=False, stop=True,
                                     skip_group_check=True)
                last.then_inc(scored, 1)

            def weights(s, n):
                qt, pr = divmod(n, PAIRS)
                for j in range(2):
                    pe.wait_ge(exped, 2 * (s * NPAIR + n) + j + 1)
                    pe.wait_ge((flip_dve, flip_act)[j], s * NPAIR + n)
                    for kt in range(qt + 1):
                        last = pe.transpose(PT[:, j, P * kt:P * (kt + 1)],
                                            probs[:, 2 * (n % 2) + j, P * kt:P * (kt + 1)], ident)
                    last.then_inc(flipped, 1)

            def values(s, n):
                qt, pr = divmod(n, PAIRS)
                for j in range(2):
                    h = 2 * pr + j
                    pe.wait_ge((flip_dve, flip_act)[j], s * NPAIR + n + 1)
                    for kt in range(qt + 1):
                        last = pe.matmul(O[:, 9 * h:9 * h + 9], probsT[:, j, P * kt:P * (kt + 1)],
                                         va[:, kt, h, :], start=(kt == 0), stop=(kt == qt),
                                         skip_group_check=True)
                last.then_inc(summed, 1)

            def near_products(s, qt):
                u = s * TPS + qt
                pe.wait_ge(seq_done, u)
                pe.matmul(M[:, 0:3 * D], xT[:, 1 + P * qt:1 + P * (qt + 1)], w_all[:], start=True, stop=True)
                pe.matmul(PT[:, 0, 0:2 * D], xT[:, P * qt:P * (qt + 1)], w_all[:, D:3 * D],
                          start=True, stop=True).then_inc(near_mm, 1)

            def output(s, qt):
                u = s * TPS + qt
                pe.wait_ge(fin, 4 * u + 4)
                pe.transpose(M[:, 0:P], on[:], ident).then_inc(on_T, 1)
                pe.wait_ge(oT_ready, u + 1)
                pe.matmul(M[:, P:2 * P], oT[:], wo[:], start=True, stop=True).then_inc(y_mm, 1)

            pe.wait_ge(bias_made, 7)
            pe.wait_ge(zeroed, 5)
            with pe.Fori(0, B) as s:
                pe.wait_ge(xa_in, 16 * s + 16)
                pe.wait_ge(seq_done, s * TPS)
                for t in range(TPS):
                    last = pe.transpose(M[:, P * t:P * (t + 1)], xa[:, t, :], ident)
                last.then_inc(turned, 1)
                pe.wait_ge(xT_ready, s + 1)
                for i in range(2):
                    for g in range(NG):
                        c = i * NG + g
                        if c >= 2:
                            pe.wait_ge(qkT_ready, 2 * NG * s + c - 1)
                        pe.matmul(S[:, c % 2, :], w_pad[:, i, G * g:G * (g + 1), :].rearrange("p h d -> p (h d)"),
                                  xT[:, 1:N + 1], start=True, stop=True).then_inc(proj, 1)
                pe.wait_ge(qkT_ready, 2 * NG * s + 2 * NG)
                for qt in range(TPS):
                    near_products(s, qt)
                    pe.wait_ge(near_ready, 6 * (s * TPS + qt) + 6)
                    for n in range(qt * PAIRS, (qt + 1) * PAIRS):
                        if n % PAIRS == 0:
                            scores(s, n)
                        if (n + 1) % PAIRS:
                            scores(s, n + 1)
                        weights(s, n)
                        values(s, n)
                    output(s, qt)

        @block.scalar
        def _(act):
            with act.Fori(0, B) as s:
                act.wait_ge(turned, s + 1)
                act.activation(xT[:, 1:N + 1], M[:], ACT.Copy).then_inc(xT_ready, 1)
                for i in range(2):
                    for g in range(NG):
                        c = i * NG + g
                        act.wait_ge(proj, 2 * NG * s + c + 1)
                        act.activation(qkT[:, i, g, :], S[:, c % 2, :], ACT.Identity,
                                       bias=b_pad[:, i, g:g + 1]).then_inc(qkT_ready, 1)
                for qt in range(TPS):
                    u = s * TPS + qt
                    for n in range(qt * PAIRS, (qt + 1) * PAIRS):
                        k = s * NPAIR + n
                        for j in range(2):
                            h = 2 * (n % PAIRS) + j
                            act.wait_ge(nm_ready, k + 1)
                            act.activation(probs[:, 2 * (n % 2) + j, 0:P * (qt + 1)],
                                           S[:, 2 * (n % 2) + j, 0:P * (qt + 1)], ACT.Exp,
                                           bias=nm[:, h:h + 1], scale=SCALE_A).then_inc(exped, 1)
                        act.wait_ge(flipped, 2 * k + 2)
                        if n:
                            act.wait_ge(summed, k)
                        act.activation(probsT[:, 1, 0:P * (qt + 1)], PT[:, 1, 0:P * (qt + 1)],
                                       ACT.Copy).then_inc(flip_act, 1)
                    act.wait_ge(d01_ready, 2 * u + 2)
                    act.activation(p01[:], d01[:], ACT.Exp, scale=1.0).then_inc(p01_ready, 1)
                    act.wait_ge(on_T, u + 1)
                    act.activation(oT[:], M[:, 0:P], ACT.Copy).then_inc(oT_ready, 1)

        @block.vector
        def _(dve):
            with dve.Fori(0, B) as s:
                for qt in range(TPS):
                    u = s * TPS + qt
                    dve.wait_ge(near_mm, u + 1)
                    dve.wait_ge(pool_chain, 4 * u)
                    for out, src, b in ((near[:, 0, :], M[:, 0:D], bias[:, 0, :]),
                                        (near[:, 1, :], M[:, D:2 * D], kv_bias[:, 0, 2, :]),
                                        (near[:, 2, :], PT[:, 0, 0:D], kv_bias[:, 0, 1, :]),
                                        (near[:, 3, :], M[:, 2 * D:3 * D], kv_bias[:, 1, 2, :]),
                                        (near[:, 4, :], PT[:, 0, D:2 * D], kv_bias[:, 1, 1, :])):
                        dve.tensor_tensor(out, src, b, ALU.add).then_inc(near_ready, 1)
                    dve.tensor_tensor(va[:, qt, :, 0:HA], M[:, 2 * D:3 * D].rearrange("p (h d) -> p h d", h=H),
                                      kv_bias[:, 1, 0, :].rearrange("p (h d) -> p h d", h=H),
                                      ALU.add).then_inc(near_ready, 1)
                    for i in range(2):
                        dve.wait_ge(prods, 2 * u + i + 1)
                        dve.tensor_reduce(s01[:, i, :], prod[:, i, :].rearrange("p (h d) -> p h d", h=H),
                                          X, ALU.add).then_inc(s01_ready, 1)
                    dve.wait_ge(s01_ready, 2 * u + 2)
                    c = s * (2 * TPS + 1) + (2 * qt + 1 if qt else 0)
                    if qt == 0:
                        dve.tensor_tensor(s01[:, 1, :], s01[:, 1, :], near_mask, ALU.add).then_inc(sm_ready, 1)
                        dve.wait_ge(sm_ready, c + 1)
                        c = c + 1
                    dve.tensor_tensor(sm[:], s01[:, 0, :], s01[:, 1, :], ALU.max).then_inc(sm_ready, 1)
                    dve.wait_ge(sm_ready, c + 1)
                    dve.tensor_scalar(sm[:], sm[:], -SCALE_A, None, ALU.mult).then_inc(sm_ready, 1)
                    dve.wait_ge(sm_ready, c + 2)

                    def maxima(n):
                        k = s * NPAIR + n
                        h = 2 * (n % PAIRS)
                        dve.wait_ge(scored, k + 1)
                        dve.tensor_reduce(far_max[:, h:h + 2], S[:, 2 * (n % 2):2 * (n % 2) + 2, 0:P * (qt + 1)],
                                          X, ALU.max).then_inc(far_maxed, 1)
                        dve.wait_ge(far_maxed, k + 1)
                        dve.scalar_tensor_tensor(nm[:, h:h + 2], far_max[:, h:h + 2], -SCALE_A, sm[:, h:h + 2],
                                                 ALU.mult, ALU.min).then_inc(nm_ready, 1)

                    def flip(n):
                        k = s * NPAIR + n
                        dve.wait_ge(flipped, 2 * k + 1)
                        if n:
                            dve.wait_ge(summed, k)
                        dve.tensor_copy(probsT[:, 0, 0:P * (qt + 1)],
                                        PT[:, 0, 0:P * (qt + 1)]).then_inc(flip_dve, 1)

                    first = qt * PAIRS
                    maxima(first)
                    for n in range(first, first + PAIRS):
                        if (n + 1) % PAIRS:
                            maxima(n + 1)
                        flip(n)
                    dve.wait_ge(nm_ready, s * NPAIR + first + PAIRS)
                    for i in range(2):
                        dve.scalar_tensor_tensor(d01[:, i, :], s01[:, i, :], SCALE_A, nm[:],
                                                 ALU.mult, ALU.add).then_inc(d01_ready, 1)
                    dve.wait_ge(pool_chain, 4 * u + 4)
                    dve.wait_ge(summed, s * NPAIR + first + PAIRS)
                    o = O[:, 0:9 * H].rearrange("p (h d) -> p h d", h=H)
                    dve.tensor_tensor(den[:], o[:, :, HA], p_sum[:], ALU.add).then_inc(fin, 1)
                    dve.tensor_tensor(num[:].rearrange("p (h d) -> p h d", h=H), o[:, :, 0:HA],
                                      pv_near[:, 0, :].rearrange("p (h d) -> p h d", h=H), ALU.add).then_inc(fin, 1)
                    dve.wait_ge(fin, 4 * u + 2)
                    dve.reciprocal(rden[:], den[:]).then_inc(fin, 1)
                    dve.wait_ge(fin, 4 * u + 3)
                    dve.tensor_tensor(on[:].rearrange("p (h d) -> p h d", h=H),
                                      num[:].rearrange("p (h d) -> p h d", h=H), bc(rden[:], 2, HA),
                                      ALU.mult).then_inc(fin, 1)
                    dve.wait_ge(y_mm, u + 1)
                    dve.wait_ge(bias_made, 7 + 1 + s)
                    dve.tensor_tensor(total[:, bass.ds(s, 1), qt, :],
                                      M[:, P:2 * P].unsqueeze(1),
                                      xo[:, qt, :].unsqueeze(1), ALU.add).then_inc(seq_done, 1)
            dve.wait_ge(seq_done, B * TPS)


def windowed_layers(nc, Wqkv, qs, ks, Wout, ln_g, ln_b, W1, b1, W2, b2, state, total, rank, out):
    with ExitStack() as ctx:
        sb = lambda n, s, d=F32: ctx.enter_context(nc.sbuf_tensor(n, s, d))
        sem = lambda n: ctx.enter_context(nc.semaphore(n))
        w_hi, w_lo = sb("w_hi", [P, 3 * INNER], F32R), sb("w_lo", [P, 3 * INNER], F32R)
        w_out = sb("w_out", [P, PAIRS, D])
        qk_scale = sb("qk_scale", [P, 4, HB])
        rope = sb("rope", [P, 4, TPS, HB])
        w1_raw = sb("w1_raw", [P, 2 * FF])
        w1_hi, w1_lo = sb("w1_hi", [P, 2 * FF], F32R), sb("w1_lo", [P, 2 * FF], F32R)
        w2 = sb("w2", [P, 3, D])
        b1c = sb("b1c", [P, 2, 3])
        gbc = sb("gbc", [P, 2])
        b2r = sb("b2r", [P, D])
        xcur = sb("xcur", [P, TPS, D])
        xsf = sb("xsf", [P, 2, P + 1])
        xh, xl = sb("xh", [P, 2, P], F32R), sb("xl", [P, 2, P], F32R)
        sq = sb("sq", [P, 2, INNER])
        t1 = sb("t1", [P, 2, 2, INNER])
        w_raw = t1[:].rearrange("p a b n -> p (a b n)")[:, 0:3 * INNER]
        t2 = sb("t2", [P, 2, INNER])
        ss = sb("ss", [P, 2 * H])
        rn = sb("rn", [P, 2 * H])
        half_ss, rn_tmp = sb("half_ss", [P, 2 * H]), sb("rn_tmp", [P, 2 * H])
        qT = sb("qT", [P, PAIRS, P])
        kT = sb("kT", [P, 2, PAIRS, W + P])
        va = sb("va", [P, 2, 2, PAIRS, HB1])
        vs = sb("vs", [P, 2, 3, PAIRS, HB1])
        m = sb("m", [P, H])
        shared = sb("shared", [P, 3, INNER])
        e = shared[:, 0, :].rearrange("p (r j k) -> p r j k", r=2, j=PAIRS)
        pw = shared[:, 1, :].rearrange("p (j r k) -> p j r k", j=PAIRS, r=2)
        pT = shared[:, 2, :].rearrange("p (j q) -> p j q", j=PAIRS)
        hT = shared[:].rearrange("p a (b n) -> p (a b) n", b=2).rearrange("p (a j) n -> p a j n", a=2)
        rden = sb("rden", [P, 2, PAIRS])
        on = sb("on", [P, PAIRS, 2, HB])
        oT = sb("oT", [P, PAIRS, P])
        credit = sb("credit", [P, 16])
        zeros = sb("zeros", [P, PAIRS, W])
        xf = sb("xf", [P, 2, TPS, D])
        fsf = sb("fsf", [P, 2, N + 1])
        cen = sb("cen", [P, 2, N])
        sqf = sb("sqf", [P, 2, N])
        var, rstd = sb("f_var", [P, 2, TPS]), sb("f_rstd", [P, 2, TPS])
        half_v, f_tmp = sb("f_half", [P, 2, TPS]), sb("f_tmp", [P, 2, TPS])
        fh, fl = sb("fh", [P, 2, N], F32R), sb("fl", [P, 2, N], F32R)
        gel = sb("gel", [P, 2, N])
        PS = ctx.enter_context(nc.psum_tensor("PS", [P, 8, 512], F32))
        ident = rank["const"][:, C_ID:C_ID + P]
        id_bf, mask_bf, mean_w = rank["id_bf"], rank["mask_bf"], rank["mean_w"]
        mask_q = {t: mask_bf[:, 2 * W * (t == 0):2 * W * (t == 0) + 2 * W] for t in range(TPS)}

        RN_OPS = RSQRT_OPS + 1
        FFW_IN = 16 * (1 + 3 * 3 + 2 + 1)

        VS_IN = 16 * 8

        def placed(par, w):
            return ((0, None, 1, 2), (0, 1, 2, None))[par][w]

        made = sem("made")
        raw_in, wout_in, scale_in, ffw_in = sem("raw_in"), sem("wout_in"), sem("scale_in"), sem("ffw_in")
        x_in = [sem(f"x_in{t}") for t in range(TPS)]
        vs_in = [sem("vs_in0"), sem("vs_in1")]
        xf_in = [sem("xf_in0"), sem("xf_in1")]
        out_done = sem("out_done")
        hi_made, lo_made, rope_made = sem("hi_made"), sem("lo_made"), sem("rope_made")
        hi1_made, lo1_made = sem("hi1_made"), sem("lo1_made")
        xt_mm = sem("xt_mm")
        xsf_made = sem("xsf_made")
        xh_made, xl_made = sem("xh_made"), sem("xl_made")
        q_mm, k_mm, v_mm = sem("q_mm"), sem("k_mm"), sem("v_mm")
        sq_made = sem("sq_made")
        t_made = sem("t_made")
        ss_made = sem("ss_made")
        rn_chain = sem("rn_chain")
        added = sem("added")
        qn_made, kn_made = sem("qn_made"), sem("kn_made")
        carried = sem("carried")
        qt_mm, kt_mm = sem("qt_mm"), sem("kt_mm")
        qT_made, kT_made = sem("qT_made"), sem("kT_made")
        v_made = sem("v_made")
        s_mm = sem("s_mm")
        m_made = sem("m_made")
        e_made = sem("e_made")
        pw_made = sem("pw_made")
        pt_mm, pT_made = sem("pt_mm"), sem("pT_made")
        xf_begun = sem("xf_begun")
        pv_begun = sem("pv_begun")
        pv_mm = sem("pv_mm")
        rden_made, on_made = sem("rden_made"), sem("on_made")
        ot_mm = sem("ot_mm")
        oT_made = sem("oT_made")
        y_mm = sem("y_mm")
        attn_done = sem("attn_done")
        ft_mm, fsf_made, mean_mm, cen_made = sem("ft_mm"), sem("fsf_made"), sem("mean_mm"), sem("cen_made")
        sqf_made, var_mm, f_chain, rb_mm = sem("sqf_made"), sem("var_mm"), sem("f_chain"), sem("rb_mm")
        xn_made, fh_made, fl_made, b2_made = sem("xn_made"), sem("fh_made"), sem("fl_made"), sem("b2_made")
        g_mm, a_mm = sem("g_mm"), sem("a_mm")
        gel_made, h_made = sem("gel_made"), sem("h_made")
        y2_mm = sem("y2_mm")
        ffn_done = sem("ffn_done")
        totaled = sem("totaled")
        block = ctx.enter_context(nc.Block())

        def attention(eng, lay, slot):
            for t in range(TPS):
                slot(lay, 0, t, range(t + 1))
            with eng.Fori(1, B) as s:
                for t in range(TPS):
                    slot(lay, s, t, range(4))
            for t in range(3):
                slot(lay, B, t, range(t + 1, 4))

        def number(lay, s, t):
            return lay * (B * TPS) + s * TPS + t

        def before(s, t, n=1):
            return (s, t - n) if t >= n else (s - 1, t - n + TPS)

        def pairs_of_sequences(eng, body):
            with eng.Fori(0, B // 2) as pr:
                body(pr)

        @block.sync
        def _(sp):
            def load_attention(lay):
                sp.dma_start(w_raw, Wqkv[bass.ds(lay, 1), :, :].rearrange("a c n -> (a c) n")).then_inc(raw_in, 16)
                sp.dma_start(w_out[:], Wout[bass.ds(lay, 1), :, :].rearrange("a (j p) d -> p (a j) d", p=P)).then_inc(wout_in, 16)
                for i, v in enumerate((qs, ks)):
                    v = v[bass.ds(lay, 1), :]
                    wide = v.broadcast_to([P, HB])
                    sp.dma_start(qk_scale[:, 2 * i, :], wide).then_inc(scale_in, 16)
                    sp.dma_start(qk_scale[:, 2 * i + 1, 0:32], wide[:, 32:64]).then_inc(scale_in, 16)
                    sp.dma_start(qk_scale[:, 2 * i + 1, 32:64], wide[:, 0:32]).then_inc(scale_in, 16)

            def load_ffn(lay):
                sp.dma_start(w1_raw[:], W1[bass.ds(lay, 1), :, :].rearrange("a c n -> (a c) n")).then_inc(ffw_in, 16)
                for j, (o, w) in enumerate(FC):
                    sp.dma_start(w2[0:w, j, :], W2[bass.ds(lay, 1), o:o + w, :].rearrange("a c n -> (a c) n")).then_inc(ffw_in, 16)
                    for i in range(2):
                        sp.dma_start(b1c[0:w, i, j:j + 1],
                                     b1[bass.ds(lay, 1), FF * i + o:FF * i + o + w].rearrange("a c -> c a"),
                                     allow_slow_non_contiguous=True).then_inc(ffw_in, 16)
                for i, v in enumerate((ln_g, ln_b)):
                    sp.dma_start(gbc[:, i:i + 1], v[bass.ds(lay, 1), :].rearrange("a c -> c a"),
                                 allow_slow_non_contiguous=True).then_inc(ffw_in, 16)
                sp.dma_start(b2r[:], b2[bass.ds(lay, 1), :].broadcast_to([P, D])).then_inc(ffw_in, 16)

            def layer(lay, prefetch):
                sp.wait_ge(ffn_done, lay * B + B)
                load_ffn(lay)

                def slot(lay, s, t, ages):
                    T = number(lay, s, t)
                    sm, tm = before(s, t)
                    if 0 in ages:
                        if t == 0:
                            sp.wait_ge(ffn_done, lay * B + s + 1)
                        sp.wait_ge(attn_done, T + 1)
                        src = state[:, bass.ds(s, 1), t, :].rearrange("p a d -> p (a d)")
                        sp.dma_start(xcur[:, t, :], src).then_inc(x_in[t], 16)
                    if 1 in ages:
                        sp.wait_ge(v_made, 2 * T)
                        sp.wait_ge(pv_mm, T)
                        now, last = tm % 2, 1 - tm % 2
                        for par in range(2):
                            r = 2 * W * par
                            for to, tile, at, n in [(r, last, P - W, W)] + [(r + W, now, 0, W)]:
                                sp.dma_start(vs[to:to + n, now, 0, :, :], va[at:at + n, tile, par, :, :]).then_inc(vs_in[now], 16)
                            for w in range(1, NW):
                                k = placed(par, w)
                                if k is not None:
                                    sp.dma_start(vs[r:r + 2 * W, now, k, :, :],
                                                 va[W * (w - 1):W * (w + 1), now, par, :, :]).then_inc(vs_in[now], 16)

                attention(sp, lay, slot)
                if prefetch:
                    sp.wait_ge(attn_done, lay * (B * TPS) + B * TPS + TPS)
                    load_attention(lay + 1)

                def ffn(pr):
                    sp.wait_ge(attn_done, lay * (B * TPS) + B * TPS + TPS)
                    sp.sem_inc(xf_begun, 1)
                    for a in range(2):
                        sp.wait_ge(ffn_done, lay * B + pr * 2 + a + B - 1)
                        sp.dma_start(xf[:, a, :, :],
                                     state[:, bass.ds(pr * 2 + a, 1), :, :].rearrange("p a t d -> p (a t) d")
                                     ).then_inc(xf_in[a], 16)
                pairs_of_sequences(sp, ffn)

            sp.wait_ge(made, 5)
            load_attention(0)
            with sp.Fori(0, LAYERS - 1) as lay:
                layer(lay, True)
            layer(LAYERS - 1, False)
            for s in range(B):
                sp.wait_ge(totaled, s + 1)
                sp.dma_start(out[s].rearrange("(t p) d -> p t d", p=P), total[:, s, :, :]).then_inc(out_done, 16)
            sp.wait_ge(out_done, 16 * B)

        @block.gpsimd
        def _(pool):
            pool.memset(zeros[:], 0.0).then_inc(made, 1)
            pool.memset(va[:], 1.0).then_inc(made, 1)
            pool.memset(fsf[:, :, 0:1], 0.0).then_inc(made, 1)
            pool.memset(kT[:], 0.0).then_inc(made, 1)
            pool.memset(b1c[:], 0.0).then_inc(made, 1)

            def layer(lay):
                pool.wait_ge(scale_in, 96 * lay + 96)
                pool.wait_ge(attn_done, lay * (B * TPS) + TPS)
                for i in range(4):
                    pool.tensor_tensor(rope[:, i, :, :],
                                       rank["const"][:, C_ROPE + i * TPS * HB:C_ROPE + (i + 1) * TPS * HB].rearrange("p (t d) -> p t d", t=TPS),
                                       bc(qk_scale[:, i, :], 1, TPS), ALU.mult).then_inc(rope_made, 1)

                def slot(lay, s, t, ages):
                    T = number(lay, s, t)
                    if 0 not in ages:
                        return
                    mine = t1[:, t % 2, :, :]
                    for i in range(2):
                        pool.wait_ge(t_made, 4 * T + 2 * i + 2)
                        pool.tensor_tensor(mine[:, i, :], mine[:, i, :], t2[:, i, :], ALU.add).then_inc(added, 1)
                    pool.wait_ge(kT_made, 2 * T)
                    left = zeros[:] if t == 0 else kT[:, 1 - t % 2, :, P:P + W]
                    pool.tensor_tensor(kT[:, t % 2, :, 0:W], left, zeros[:], ALU.add).then_inc(carried, 1)
                    pool.wait_ge(rn_chain, (T + 1) * RN_OPS)
                    for i, done in enumerate((qn_made, kn_made)):
                        pool.wait_ge(added, 2 * T + i + 1)
                        h = mine[:, i, :].rearrange("p (h d) -> p h d", h=H)
                        pool.tensor_tensor(h, h, bc(rn[:, H * i:H * (i + 1)], 2, HB), ALU.mult).then_inc(done, 1)
                attention(pool, lay, slot)

                def ffn(pr):
                    pool.wait_ge(ffw_in, FFW_IN * lay + FFW_IN)
                    for a in range(2):
                        pool.wait_ge(ft_mm, lay * B + pr * 2 + a + 1)
                        pool.tensor_tensor(xf[:, a, :, :], xf[:, a, :, :], bc(b2r[:], 1, TPS), ALU.add).then_inc(b2_made, 1)
                pairs_of_sequences(pool, ffn)

            with pool.Fori(0, LAYERS) as lay:
                layer(lay)

        @block.tensor
        def _(pe):
            def split_matmul(out, hi, lo, w_hi, w_lo):
                pe.matmul(out, hi, w_hi, start=True, stop=False)
                pe.matmul(out, lo, w_hi, start=False, stop=False)
                return pe.matmul(out, hi, w_lo, start=False, stop=True)

            def project(i, bank, t, done):
                for c in range(2):
                    cols = slice(INNER * i + 512 * c, INNER * i + 512 * (c + 1))
                    last = split_matmul(PS[:, bank + c, :], xh[:, t % 2, :], xl[:, t % 2, :], w_hi[:, cols], w_lo[:, cols])
                last.then_inc(done, 1)

            def turn_tile(i, bank, t, done):
                for j in range(PAIRS):
                    last = pe.transpose(PS[:, bank + j // 4, P * (j % 4):P * (j % 4 + 1)],
                                        t1[:, t % 2, i, P * j:P * (j + 1)], ident)
                last.then_inc(done, 1)

            def score_pairs(t, pairs):
                for pair in pairs:
                    for par in range(2):
                        rows = slice(HB * par, HB * (par + 1))
                        for w in range(NW):
                            last = pe.matmul(PS[W * w:W * (w + 1), 6 + par, 2 * W * pair:2 * W * (pair + 1)],
                                             qT[rows, pair, W * w:W * (w + 1)],
                                             kT[rows, t % 2, pair, W * w:W * (w + 2)],
                                             start=False, stop=True, skip_group_check=True)
                return last

            def slot(lay, s, t, ages):
                T = number(lay, s, t)
                (s1, tile1), (s2, tile2) = before(s, t, 1), before(s, t, 2)
                if 0 in ages:
                    if 3 not in ages:
                        pe.wait_ge(t_made, 4 * T)
                    pe.wait_ge(x_in[t], 16 * (lay * B + s) + 16)
                    pe.transpose(PS[:, 3, 0:P], xcur[:, t, :], ident).then_inc(xt_mm, 1)
                if 3 in ages:
                    pe.wait_ge(oT_made, 2 * T)
                    for pair in range(PAIRS):
                        last = pe.matmul(PS[:, 4, 0:D], oT[:, pair, :], w_out[:, pair, :],
                                         start=(pair == 0), stop=(pair == PAIRS - 1))
                    last.then_inc(y_mm, 1)
                if 0 in ages:
                    pe.wait_ge(xl_made, T + 3)
                    project(0, 0, t, q_mm)
                    project(1, 2, t, k_mm)
                if 1 in ages:
                    pe.wait_ge(v_made, 2 * T)
                    pe.wait_ge(attn_done, T + 2)
                    pe.wait_ge(qn_made, T)
                    turn_tile(0, 4, tile1, qt_mm)
                    if 2 in ages:
                        pe.wait_ge(e_made, 2 * (T - 1))
                    pe.wait_ge(kn_made, T)
                    turn_tile(1, 6, tile1, kt_mm)
                if 2 in ages:
                    if 0 in ages:
                        pe.wait_ge(t_made, 4 * T + 2)
                    for c in range(2):
                        pe.wait_ge(pw_made, 2 * (T - 2) + c + 1)
                        for j in range(4):
                            last = pe.transpose(PS[:, c, P * j:P * (j + 1)],
                                                pw[:, 4 * c + j, :, :].rearrange("p r k -> p (r k)"), ident)
                        last.then_inc(pt_mm, 1)
                if 0 in ages:
                    if 1 in ages:
                        pe.wait_ge(qT_made, 2 * T)
                    project(2, 4, t, v_mm)
                if 2 in ages:
                    if 0 in ages:
                        pe.wait_ge(t_made, 4 * T + 4)
                    pe.wait_ge(vs_in[tile2 % 2], VS_IN * (lay * (B * 2) + s2 * 2 + tile2 // 2) + VS_IN)
                    pe.wait_ge(pT_made, 2 * (T - 1))
                    pe.sem_inc(pv_begun, 1)
                    for h in range(H):
                        par, pair = h % 2, h // 2
                        bank, at = 2 * (pair // 7) + par, HB1 * (pair % 7)
                        rows = slice(2 * W * par, 2 * W * (par + 1))
                        for w in range(NW):
                            k = placed(par, w)
                            v = va[rows, tile2 % 2, par, pair, :] if k is None else vs[rows, tile2 % 2, k, pair, :]
                            last = pe.matmul(PS[W * w:W * (w + 1), bank, at:at + HB1],
                                             pT[rows, pair, W * w:W * (w + 1)], v, start=True, stop=True,
                                             skip_group_check=True)
                    last.then_inc(pv_mm, 1)
                if 1 in ages:
                    pe.wait_ge(qT_made, 2 * T)
                    pe.wait_ge(kT_made, 2 * T)
                    pe.wait_ge(carried, T)
                    for par in range(2):
                        pe.matmul(PS[:, 6 + par, :], id_bf[:], bc(mask_q[tile1], 1, PAIRS),
                                  start=True, stop=False, skip_group_check=True)
                    score_pairs(tile1, range(0, PAIRS // 2))
                if 2 in ages:
                    if 0 in ages:
                        pe.wait_ge(v_made, 2 * T + 2)
                    pe.wait_ge(on_made, 2 * T)
                    for c in range(2):
                        for j in range(4):
                            last = pe.transpose(PS[:, 4 + c, P * j:P * (j + 1)],
                                                on[:, 4 * c + j, :, :].rearrange("p r d -> p (r d)"), ident)
                        last.then_inc(ot_mm, 1)
                if 1 in ages:
                    score_pairs(tile1, range(PAIRS // 2, PAIRS)).then_inc(s_mm, 1)

            def ffn_pair(lay, pr):
                pe.wait_ge(attn_done, lay * (B * TPS) + B * TPS + TPS)
                pe.wait_ge(hi1_made, lay + 1)
                pe.wait_ge(lo1_made, lay + 1)
                for a in range(2):
                    U = lay * B + pr * 2 + a
                    first = (0, 6)[a]
                    pe.wait_ge(xf_in[a], 16 * (lay * (B // 2) + pr) + 16)
                    pe.wait_ge(ffn_done, U + B - 1)
                    for t in range(TPS):
                        last = pe.transpose(PS[:, first, P * t:P * (t + 1)], xf[:, a, t, :], ident)
                    last.then_inc(ft_mm, 1)
                for a in range(2):
                    pe.wait_ge(fsf_made, 2 * (lay * B + pr * 2 + a) + 2)
                    pe.matmul(PS[:, (1, 7)[a], :], mean_w[:], fsf[:, a, 0:N], start=True, stop=True).then_inc(mean_mm, 1)
                for a in range(2):
                    pe.wait_ge(sqf_made, lay * B + pr * 2 + a + 1)
                    for t in range(TPS):
                        last = pe.matmul(PS[:, (1, 7)[a], t:t + 1], sqf[:, a, P * t:P * (t + 1)], mean_w[:, 0:1],
                                         start=True, stop=True, skip_group_check=True)
                    last.then_inc(var_mm, 1)
                for a in range(2):
                    pe.wait_ge(f_chain, (lay * B + pr * 2 + a + 1) * RN_OPS)
                    for t in range(TPS):
                        last = pe.matmul(PS[:, (1, 7)[a], P * t:P * (t + 1)], rstd[:, a, t:t + 1].broadcast_to([P, P]),
                                         ident, start=True, stop=True, skip_group_check=True)
                    last.then_inc(rb_mm, 1)
                pe.wait_ge(ffw_in, FFW_IN * lay + FFW_IN)
                for a in range(2):
                    U = lay * B + pr * 2 + a
                    pe.wait_ge(fl_made, U + 1)
                    for j, (o, w) in enumerate(FC):
                        for i, (sem_read, done) in enumerate(((gel_made, g_mm), (h_made, a_mm))):
                            bank = 2 + (6 * a + 2 * j + i) % 4
                            pe.wait_ge(sem_read, 3 * U + j)
                            cols = slice(FF * (1 - i) + o, FF * (1 - i) + o + w)
                            split_matmul(PS[0:w, bank, :], w1_hi[:, cols], w1_lo[:, cols], fh[:, a, :], fl[:, a, :]).then_inc(done, 1)
                    pe.wait_ge(h_made, 3 * U + 4)
                    for t in range(TPS):
                        for j, (o, w) in enumerate(FC):
                            last = pe.matmul(PS[:, (0, 6)[a], P * t:P * (t + 1)], hT[0:w, a, j, P * t:P * (t + 1)],
                                             w2[0:w, j, :], start=(j == 0), stop=(j == 2), skip_group_check=True)
                    last.then_inc(y2_mm, 1)

            pe.wait_ge(made, 5)
            with pe.Fori(0, LAYERS) as lay:
                pe.wait_ge(ffn_done, lay * B + B)
                pe.wait_ge(hi_made, 3 * lay + 3)
                pe.wait_ge(lo_made, 3 * lay + 3)
                pe.wait_ge(wout_in, 16 * lay + 16)

                attention(pe, lay, slot)
                pairs_of_sequences(pe, lambda pr: ffn_pair(lay, pr))

        @block.scalar
        def _(act):
            copy = lambda o, i: act.activation(o, i, ACT.Copy)

            def slot(lay, s, t, ages):
                T = number(lay, s, t)
                p = t % 2
                if 0 in ages:
                    act.wait_ge(xt_mm, T + 1)
                    act.wait_ge(xl_made, T + 1)
                    act.wait_ge(xsf_made, 3 * T)
                    copy(xsf[0:64, p, 0:P], PS[0:64, 3, 0:P]).then_inc(xsf_made, 1)
                    copy(xsf[64:P, p, 1:P + 1], PS[64:P, 3, 0:P]).then_inc(xsf_made, 1)
                    copy(xsf[64:P, p, 0:1], zeros[64:P, 0, 0:1] if t == 0 else xsf[64:P, 1 - p, P:P + 1]).then_inc(xsf_made, 1)
                    act.wait_ge(ss_made, 2 * T)
                    act.wait_ge(q_mm, T + 1)
                    for c in range(2):
                        act.activation(sq[:, 0, 512 * c:512 * (c + 1)], PS[:, c, :], ACT.Square).then_inc(sq_made, 1)
                if 2 in ages:
                    act.wait_ge(pt_mm, 2 * (T - 2))
                    for c in range(2):
                        act.wait_ge(e_made, 2 * (T - 2) + c + 1)
                        act.activation(pw[:, 4 * c:4 * (c + 1), :, :], e[:, :, 4 * c:4 * (c + 1), :].rearrange("p r j k -> p j r k"),
                                       ACT.Exp).then_inc(pw_made, 1)
                if 0 in ages:
                    act.wait_ge(k_mm, T + 1)
                    for c in range(2):
                        act.activation(sq[:, 1, 512 * c:512 * (c + 1)], PS[:, 2 + c, :], ACT.Square).then_inc(sq_made, 1)
                if 1 in ages:
                    act.wait_ge(qt_mm, T + 1)
                    for c in range(2):
                        copy(qT[:, 4 * c:4 * (c + 1), :], PS[:, 4 + c, :].rearrange("p (j q) -> p j q", j=4)).then_inc(qT_made, 1)
                    act.wait_ge(kt_mm, T + 1)
                    for c in range(2):
                        copy(kT[:, 1 - p, 4 * c:4 * (c + 1), W:], PS[:, 6 + c, :].rearrange("p (j q) -> p j q", j=4)).then_inc(kT_made, 1)
                if 2 in ages:
                    act.wait_ge(pv_mm, T)
                    for c in range(2):
                        act.wait_ge(pt_mm, 2 * (T - 2) + c + 1)
                        copy(pT[:, 4 * c:4 * (c + 1), :], PS[:, c, :].rearrange("p (j q) -> p j q", j=4)).then_inc(pT_made, 1)
                if 0 in ages:
                    act.wait_ge(v_mm, T + 3)
                    act.wait_ge(pv_mm, T + 1)
                    if t:
                        act.wait_ge(vs_in[1 - p], VS_IN * (lay * (B * 2) + s * 2 + (t - 1) // 2) + VS_IN)
                    else:
                        act.wait_ge(vs_in[1], VS_IN * (lay * (B * 2) + s * 2))
                    for c in range(2):
                        copy(va[:, p, :, 4 * c:4 * (c + 1), 0:HB],
                             PS[:, 4 + c, :].rearrange("p (j r d) -> p r j d", j=4, r=2)).then_inc(v_made, 1)
                if 2 in ages:
                    for c in range(2):
                        act.wait_ge(ot_mm, 2 * T - 1 + c)
                        act.wait_ge(y_mm, T)
                        copy(oT[:, 4 * c:4 * (c + 1), :],
                             PS[:, 4 + c, :].rearrange("p (j q) -> p j q", j=4)).then_inc(oT_made, 1)

            def ffn_pair(lay, pr):
                for a in range(2):
                    act.wait_ge(ft_mm, lay * B + pr * 2 + a + 1)
                    copy(fsf[0:64, a, 0:N], PS[0:64, (0, 6)[a], :]).then_inc(fsf_made, 1)
                    copy(fsf[64:P, a, 1:N + 1], PS[64:P, (0, 6)[a], :]).then_inc(fsf_made, 1)
                for a in range(2):
                    act.wait_ge(cen_made, lay * B + pr * 2 + a + 1)
                    act.activation(sqf[:, a, :], cen[:, a, :], ACT.Square).then_inc(sqf_made, 1)
                for a in range(2):
                    for j, (o, w) in enumerate(FC):
                        C = (lay * B + pr * 2 + a) * 3 + j
                        act.wait_ge(g_mm, C + 1)
                        act.wait_ge(h_made, C)
                        act.activation(gel[0:w, (3 * a + j) % 2, :], PS[0:w, 2 + (6 * a + 2 * j) % 4, :], ACT.Gelu,
                                       bias=b1c[0:w, 1, j:j + 1]).then_inc(gel_made, 1)

            act.wait_ge(made, 5)
            copy(credit[:, 15:16], zeros[:, 0, 0:1]).then_inc(gel_made, 1)
            with act.Fori(0, LAYERS) as lay:
                act.wait_ge(raw_in, 16 * lay + 16)
                act.wait_ge(ffn_done, lay * B + B)
                for i in range(3):
                    copy(w_hi[:, INNER * i:INNER * (i + 1)], w_raw[:, INNER * i:INNER * (i + 1)]).then_inc(hi_made, 1)
                attention(act, lay, slot)
                act.wait_ge(ffw_in, FFW_IN * lay + FFW_IN)
                copy(w1_hi[:], w1_raw[:]).then_inc(hi1_made, 1)
                pairs_of_sequences(act, lambda pr: ffn_pair(lay, pr))

        @block.vector
        def _(dve):
            def slot(lay, s, t, ages):
                T = number(lay, s, t)
                s3, tile3 = before(s, t, 3)
                p = t % 2
                if 0 in ages:
                    dve.wait_ge(xsf_made, 3 * T + 3)
                    dve.wait_ge(v_mm, T + 1)
                    dve.tensor_copy(xh[:, p, :], xsf[:, p, 0:P]).then_inc(xh_made, 1)
                    dve.wait_ge(xh_made, T + 1)
                    dve.tensor_tensor(xl[:, p, :], xsf[:, p, 0:P], xh[:, p, :].bitcast(F32), ALU.subtract).then_inc(xl_made, 1)
                if 2 in ages:
                    scores = PS[:, 6:8, :].rearrange("p r (j k) -> p r j k", j=PAIRS)
                    dve.wait_ge(s_mm, T - 1)
                    dve.tensor_reduce(m[:].rearrange("p (r j) -> p r j", r=2), scores, X, ALU.max).then_inc(m_made, 1)
                    dve.wait_ge(m_made, T - 1)
                    dve.wait_ge(pw_made, 2 * (T - 2))
                    for c in range(2):
                        pairs = slice(4 * c, 4 * (c + 1))
                        dve.tensor_tensor(e[:, :, pairs, :], scores[:, :, pairs, :],
                                          bc(m[:].rearrange("p (r j) -> p r j", r=2)[:, :, pairs], 3, 2 * W),
                                          ALU.subtract).then_inc(e_made, 1)
                if 3 in ages:
                    dve.wait_ge(y_mm, T)
                    dve.tensor_tensor(state[:, bass.ds(s3, 1), tile3, :], PS[:, 4, 0:D].unsqueeze(1),
                                      xcur[:, tile3, :].unsqueeze(1), ALU.add).then_inc(attn_done, 1)
                if 0 in ages:
                    dve.wait_ge(kt_mm, T)
                    dve.wait_ge(added, 2 * T)
                    for i in range(2):
                        for c in range(2):
                            dve.wait_ge(sq_made, 4 * T + 2 * i + c + 1)
                            src = PS[:, 2 * i + c, :].rearrange("p (h d) -> p h d", h=8)
                            cols = slice(512 * c, 512 * (c + 1))
                            o1 = t1[:, p, i, cols].rearrange("p (h d) -> p h d", h=8)
                            o2 = t2[:, i, cols].rearrange("p (h d) -> p h d", h=8)
                            dve.tensor_tensor(o1, src, bc(rope[:, 2 * i, t, :], 1, 8), ALU.mult)
                            dve.tensor_tensor(o2[:, :, 0:32], src[:, :, 32:64], bc(rope[:, 2 * i + 1, t, 0:32], 1, 8), ALU.mult)
                            dve.tensor_tensor(o2[:, :, 32:64], src[:, :, 0:32], bc(rope[:, 2 * i + 1, t, 32:64], 1, 8),
                                              ALU.mult).then_inc(t_made, 1)
                    for i in range(2):
                        dve.tensor_reduce(ss[:, H * i:H * (i + 1)], sq[:, i, :].rearrange("p (h d) -> p h d", h=H),
                                          X, ALU.add).then_inc(ss_made, 1)
                if 2 in ages:
                    dve.wait_ge(pv_mm, T + 1)
                    dve.wait_ge(ot_mm, 2 * T - 2)
                    outs = [(PS[:, bk:bk + 2, 0:nj * HB1].rearrange("p r (j e) -> p r j e", e=HB1), slice(j0, j0 + nj))
                            for bk, j0, nj in ((0, 0, 7), (2, 7, 1))]
                    for o, j in outs:
                        dve.reciprocal(rden[:, :, j], o[:, :, :, HB]).then_inc(rden_made, 1)
                    for k, (o, j) in enumerate(outs):
                        dve.wait_ge(rden_made, 2 * (T - 2) + k + 1)
                        dve.tensor_tensor(on[:, j, :, :].rearrange("p j r d -> p r j d"), o[:, :, :, 0:HB],
                                          bc(rden[:, :, j], 3, HB), ALU.mult).then_inc(on_made, 1)
                if 0 in ages:
                    dve.wait_ge(ss_made, 2 * T + 2)
                    dve.wait_ge(kn_made, T)
                    dve.tensor_scalar(ss[:], ss[:], 1e-24, None, ALU.max).then_inc(rn_chain, 1)
                    dve.wait_ge(rn_chain, T * RN_OPS + 1)
                    rsqrt_steps(dve, rn_chain, T * RN_OPS + 1, rn[:], ss[:], half_ss[:], rn_tmp[:])

            def ffn_pair(lay, pr):
                for a in range(2):
                    dve.wait_ge(fsf_made, 2 * (lay * B + pr * 2 + a) + 2)
                    dve.wait_ge(mean_mm, lay * B + pr * 2 + a + 1)
                    dve.tensor_tensor(cen[:, a, :], fsf[:, a, 0:N], PS[:, (1, 7)[a], :], ALU.subtract).then_inc(cen_made, 1)
                for a in range(2):
                    c = (lay * B + pr * 2 + a) * RN_OPS
                    dve.wait_ge(var_mm, lay * B + pr * 2 + a + 1)
                    dve.tensor_scalar(var[:, a, :], PS[:, (1, 7)[a], 0:TPS], 1e-5, None, ALU.add).then_inc(f_chain, 1)
                    dve.wait_ge(f_chain, c + 1)
                    rsqrt_steps(dve, f_chain, c + 1, rstd[:, a, :], var[:, a, :], half_v[:, a, :], f_tmp[:, a, :])
                for a in range(2):
                    U = lay * B + pr * 2 + a
                    dve.wait_ge(rb_mm, U + 1)
                    dve.tensor_tensor(cen[:, a, :], cen[:, a, :], PS[:, (1, 7)[a], :], ALU.mult).then_inc(xn_made, 1)
                    dve.wait_ge(xn_made, 2 * U + 1)
                    dve.tensor_scalar(cen[:, a, :], cen[:, a, :], gbc[:, 0:1], gbc[:, 1:2], ALU.mult, ALU.add).then_inc(xn_made, 1)
                    dve.wait_ge(xn_made, 2 * U + 2)
                    dve.tensor_copy(fh[:, a, :], cen[:, a, :]).then_inc(fh_made, 1)
                    dve.wait_ge(fh_made, U + 1)
                    dve.tensor_tensor(fl[:, a, :], cen[:, a, :], fh[:, a, :].bitcast(F32), ALU.subtract).then_inc(fl_made, 1)
                for a in range(2):
                    U = lay * B + pr * 2 + a
                    for j, (o, w) in enumerate(FC):
                        dve.wait_ge(a_mm, 3 * U + j + 1)
                        dve.wait_ge(gel_made, 3 * U + j + 2)
                        dve.scalar_tensor_tensor(hT[0:w, a, j, :], PS[0:w, 2 + (6 * a + 2 * j + 1) % 4, :],
                                                 b1c[0:w, 0, j:j + 1], gel[0:w, (3 * a + j) % 2, :],
                                                 ALU.add, ALU.mult).then_inc(h_made, 1)
                    dve.wait_ge(y2_mm, U + 1)
                    dve.wait_ge(b2_made, U + 1)
                    dve.tensor_tensor(state[:, bass.ds(pr * 2 + a, 1), :, :].rearrange("p a t d -> p (a t) d"),
                                      PS[:, (0, 6)[a], :].rearrange("p (t d) -> p t d", t=TPS),
                                      xf[:, a, :, :], ALU.add).then_inc(ffn_done, 1)

            dve.wait_ge(made, 5)
            for i, (target, n) in enumerate(((xl_made, 2), (v_mm, 2), (pv_mm, 2), (attn_done, 4), (h_made, 1), (ffn_done, B),
                                         (oT_made, 4), (on_made, 2), (y_mm, 2), (ot_mm, 2), (qt_mm, 1), (kt_mm, 1))):
                dve.memset(credit[:, i:i + 1], 0.0).then_inc(target, n)
            with dve.Fori(0, LAYERS) as lay:
                dve.wait_ge(rope_made, 4 * lay + 4)
                for i in range(3):
                    dve.wait_ge(hi_made, 3 * lay + i + 1)
                    cols = slice(INNER * i, INNER * (i + 1))
                    dve.tensor_tensor(w_lo[:, cols], w_raw[:, cols], w_hi[:, cols].bitcast(F32), ALU.subtract).then_inc(lo_made, 1)
                attention(dve, lay, slot)
                dve.wait_ge(hi1_made, lay + 1)
                dve.tensor_tensor(w1_lo[:], w1_raw[:], w1_hi[:].bitcast(F32), ALU.subtract).then_inc(lo1_made, 1)
                pairs_of_sequences(dve, lambda pr: ffn_pair(lay, pr))
            dve.wait_ge(ffn_done, LAYERS * B + B)
            for s in range(B):
                dve.tensor_tensor(total[:, s, :, :], total[:, s, :, :], state[:, s, :, :], ALU.add).then_inc(totaled, 1)


def build(nc, x, Wq, bq, Wk, bk, Wv, bv, Wo, bo, rel_k, rel_v, Wqkv, qs, ks, Wout, ln_g, ln_b,
          W1, b1, W2, b2, const, out, only=None):
    with ExitStack() as ctx:
        sb = lambda n, s, d=F32: ctx.enter_context(nc.sbuf_tensor(n, s, d))
        state = sb("state", [P, B, TPS, D])
        total = sb("total", [P, B, TPS, D])
        rank = {"const": sb("constants", [P, NCONST]), "id_bf": sb("id_bf", [P, P], BF16),
                "mask_bf": sb("mask_bf", [P, C_NEAR - C_MQ], BF16), "mean_w": sb("mean_w", [P, P])}
        norm_and_constants(nc, x, const, state, rank, 1e-5)
        relative_attention(nc, x, Wq, bq, Wk, bk, Wv, bv, Wo, bo, rel_k, rel_v, state, total, rank)
        if only == "A":
            with nc.semaphore("z") as z, nc.Block() as block:
                @block.sync
                def _(sp):
                    sp.dma_start(out.rearrange("s (t p) d -> p (s t) d", p=P), total[:].rearrange("p s t d -> p (s t) d")).then_inc(z, 16)
                    sp.wait_ge(z, 16)
            return
        windowed_layers(nc, Wqkv, qs, ks, Wout, ln_g, ln_b, W1, b1, W2, b2, state, total, rank, out)


_INS = ["x", "W_q", "b_q", "W_k", "b_k", "W_v", "b_v", "W_o", "b_o", "rel_k_table", "rel_v_table"]
_INS = ["L0_attn_" + n for n in _INS] + ["L0_ffn_" + n for n in (
    "Wqkv", "q_scale", "k_scale", "Wo", "ln_g", "ln_b", "W1", "b1", "W2", "b2")]


def kernel(**inputs):
    import concourse.bacc as bacc
    from concourse.bass_utils import run_bass_kernel_spmd

    nc = bacc.Bacc("TRN2", target_bir_lowering=False, num_devices=1)
    arrays, args = {}, []
    for name in _INS + ["const"]:
        a = constants() if name == "const" else np.ascontiguousarray(inputs[name])
        arrays["in_" + name] = a
        args.append(nc.dram_tensor("in_" + name, a.shape, mybir.dt.from_np(a.dtype), kind="ExternalInput").ap())
    args.append(nc.dram_tensor("out_0", (B, N, D), F32, kind="ExternalOutput").ap())
    build(nc, *args)
    return run_bass_kernel_spmd(nc, [arrays], core_ids=[0]).results[0]["out_0"]
```

```python
from contextlib import ExitStack

import numpy as np

import concourse.bass as bass
from concourse import mybir
from concourse.alu_op_type import AluOpType as ALU

F32 = mybir.dt.float32
F32R = mybir.dt.float32r
BF16 = mybir.dt.bfloat16
I32 = mybir.dt.int32
ACT = mybir.ActivationFunctionType
X = mybir.AxisListType.X

P = 128
B, N, D = 8, 512, 128
TPS = N // P
H = 16
HA = D // H
HB = 64
INNER = H * HB
W = 32
NW = P // W
PAIRS = H // 2
LAYERS = 6
FF = int(D * 4 * 2 / 3)
FC = [(0, 128), (128, 128), (256, FF - 256)]
MASKED = -1.0e30
SCALE_A = float(np.float32(1.0) / np.sqrt(np.float32(HA)))
RSQRT_SEED = float(0x5F3759DF)
HB1 = HB + 1

C_ID = 0
C_ROPE = C_ID + P
C_MQ = C_ROPE + 4 * TPS * HB
C_MQ0 = C_MQ + 2 * W
C_FAR = C_MQ0 + 2 * W
C_NEAR = C_FAR + P + 1
C_PART = C_NEAR + H
NCONST = C_PART + 4


def constants():
    c = np.zeros((P, NCONST), np.float32)
    c[:, C_ID:C_ID + P] = np.eye(P, dtype=np.float32)
    half = np.arange(0, HB, 2, dtype=np.float32)
    inv_freq = (np.float32(1.0) / np.float32(10000.0) ** (half / np.float32(HB))).astype(np.float32)
    t = np.arange(N, dtype=np.float32)
    freqs = (t[:, None] * inv_freq[None, :]).astype(np.float32)
    base = ((half + np.float32(0.4 * HB)) / np.float32(1.4 * HB)).astype(np.float32)
    power = ((t - N // 2) / np.float32(W // 2)).astype(np.float32)
    scale = (base[None, :] ** power[:, None]).astype(np.float32)
    cos, sin = np.cos(freqs.astype(np.float64)), np.sin(freqs.astype(np.float64))
    q = 8.0 * scale.astype(np.float64)
    k = 1.0 / scale.astype(np.float64)
    tables = []
    for s in (q, k):
        tables += [np.concatenate([cos * s, cos * s], 1), np.concatenate([-sin * s, sin * s], 1)]
    rope = np.stack(tables).astype(np.float32).reshape(4, TPS, P, HB).transpose(2, 0, 1, 3)
    c[:, C_ROPE:C_MQ] = rope.reshape(P, -1)
    r, k2 = np.arange(P)[:, None] % W, np.arange(2 * W)[None, :]
    shut = np.where((k2 < r) | (k2 > r + W), MASKED, 0.0)
    c[:, C_MQ:C_MQ + 2 * W] = shut
    first = (np.arange(P)[:, None] < W) & (k2 < W)
    c[:, C_MQ0:C_MQ0 + 2 * W] = np.where(first, MASKED, shut)
    far = np.arange(P + 1)[None, :] - 1 >= np.arange(P)[:, None] - 1
    c[:, C_FAR:C_FAR + P + 1] = np.where(far, MASKED, 0.0)
    c[0, C_NEAR:C_NEAR + H] = MASKED
    copy = np.arange(P) // HA % 4
    for i, low in enumerate((copy % 2, copy // 2)):
        c[:, C_PART + i] = low
        c[:, C_PART + 2 + i] = 1 - 2 * low
    return c


def bc(ap, where, n):
    ap = ap.unsqueeze(where)
    return ap.broadcast_to([n if i == where else m for i, m in enumerate(ap.shape)])


def rsqrt_steps(dve, sem, count, y, x, half_x, tmp):
    def step(instruction):
        nonlocal count
        count = count + 1
        instruction.then_inc(sem, 1)

    step(dve.tensor_scalar(y.bitcast(I32), x.bitcast(I32), 1, None, ALU.arith_shift_right))
    dve.wait_ge(sem, count)
    step(dve.tensor_scalar(y.bitcast(I32), y.bitcast(I32), -1.0, RSQRT_SEED, ALU.mult, ALU.add))
    step(dve.tensor_scalar(half_x, x, -0.5, None, ALU.mult))
    for _ in range(3):
        dve.wait_ge(sem, count)
        step(dve.tensor_tensor(tmp, y, y, ALU.mult))
        dve.wait_ge(sem, count)
        step(dve.tensor_tensor(tmp, tmp, half_x, ALU.mult))
        dve.wait_ge(sem, count)
        step(dve.scalar_tensor_tensor(y, tmp, 1.5, y, ALU.add, ALU.mult))


RSQRT_OPS = 3 + 3 * 3


def norm_and_constants(nc, x, const, state, rank, eps, load_next):
    with ExitStack() as ctx:
        sb = lambda n, s, d=F32: ctx.enter_context(nc.sbuf_tensor(n, s, d))
        sem = lambda n: ctx.enter_context(nc.semaphore(n))
        NT = B * TPS
        stats = sb("n_stats", [P, NT, 6])
        mv = sb("n_mv", [P, NT, 2])
        var = sb("n_var", [P, NT])
        half_x = sb("n_half", [P, NT])
        tmp = sb("n_tmp", [P, NT])
        rstd = sb("n_rstd", [P, NT])
        x_in, const_in = [sem(f"n_x_in{s}") for s in range(B)], sem("n_const_in")
        const_made, chain, stats_made, mv_made, normed = (
            sem("n_const_made"), sem("n_chain"), sem("n_stats_made"), sem("n_mv_made"), sem("n_normed"))
        tiles = state[:].rearrange("p s t d -> p (s t) d")
        block = ctx.enter_context(nc.Block())

        @block.sync
        def _(sp):
            for s in range(B):
                sp.dma_start(state[:, s, :, :], x[s].rearrange("(t p) d -> p t d", p=P)).then_inc(x_in[s], 16)
            sp.dma_start(rank["const"][:], const).then_inc(const_in, 16)
            load_next(sp)

        @block.gpsimd
        def _(pool):
            pool.memset(rank["mean_w"][:], 1.0 / D).then_inc(const_made, 1)
            pool.wait_ge(const_in, 16)
            pool.tensor_copy(rank["id_bf"][:], rank["const"][:, C_ID:C_ID + P]).then_inc(const_made, 1)
            pool.tensor_copy(rank["mask_bf"][:], rank["const"][:, C_MQ:C_NEAR]).then_inc(const_made, 1)
            pool.wait_ge(const_made, 3)

        @block.vector
        def _(dve):
            for i in range(NT):
                if i % TPS == 0:
                    dve.wait_ge(x_in[i // TPS], 16)
                dve.bn_stats(stats[:, i, :], tiles[:, i, :]).then_inc(stats_made, 1)
            for i in range(NT):
                if i == 0:
                    dve.wait_ge(stats_made, NT)
                dve.bn_aggr(mv[:, i, :], stats[:, i, :]).then_inc(mv_made, 1)
            dve.wait_ge(mv_made, NT)
            dve.tensor_scalar(var[:], mv[:, :, 1], eps, None, ALU.add).then_inc(chain, 1)
            dve.wait_ge(chain, 1)
            rsqrt_steps(dve, chain, 1, rstd[:], var[:], half_x[:], tmp[:])
            dve.wait_ge(chain, 1 + RSQRT_OPS)
            for i in range(NT):
                dve.tensor_scalar(tiles[:, i, :], tiles[:, i, :], mv[:, i, 0:1], rstd[:, i:i + 1],
                                  ALU.subtract, ALU.mult).then_inc(normed, 1)
            dve.wait_ge(normed, NT)


def relative_attention(nc, x, const, Wq, bq, Wk, bk, Wv, bv, Wo, bo, rel_k, rel_v, state, total, rank):
    with ExitStack() as ctx:
        sb = lambda n, s, d=F32: ctx.enter_context(nc.sbuf_tensor(n, s, d))
        sem = lambda n: ctx.enter_context(nc.semaphore(n))
        G = 4
        NG = H // G
        w_pad = sb("a_w_pad", [P, 2, H, 4, HA])
        b_pad = sb("a_b_pad", [P, 2, NG])
        b_low = sb("a_b_low", [P, 2, NG])
        r_pad = sb("a_r_pad", [P, 1])
        w_all = sb("a_w_all", [P, 3 * D])
        wo = sb("a_wo", [P, D])
        bias = sb("a_bias", [P, 4, D])
        rel = sb("a_rel", [P, 2, 3, HA])
        kv_bias = sb("a_kv_bias", [P, 2, 3, D])
        xa = sb("a_xa", [P, TPS, D])
        xo = sb("a_xo", [P, TPS, D])
        xT = sb("a_xT", [P, N + 1])
        qkT = sb("a_qkT", [P, 2, NG, N], F32R)
        high = sb("a_high", [P, 2, N], F32R)
        lowT = sb("a_lowT", [P, 2, N])
        va = sb("a_va", [P, TPS, H, 32])
        sumsT = sb("a_sumsT", [P, NG, P])
        near = sb("a_near", [P, 5, TPS, D])
        prod = sb("a_prod", [P, 2, TPS, D])
        s01 = sb("a_s01", [P, 2, TPS, H])
        sm = sb("a_sm", [P, TPS, H])
        far_max = sb("a_far_max", [P, 2, H])
        nm = sb("a_nm", [P, 2, H])
        d01 = sb("a_d01", [P, 2, H])
        p01 = sb("a_p01", [P, 2, H])
        p_sum = sb("a_p_sum", [P, H])
        pv_near = sb("a_pv_near", [P, 2, D])
        probs = sb("a_probs", [P, 4, N])
        probsT = sb("a_probsT", [P, 2, 2, N])
        num = sb("a_num", [P, D])
        den = sb("a_den", [P, H])
        rden = sb("a_rden", [P, H])
        on = sb("a_on", [P, D])
        oT = sb("a_oT", [P, P])
        S = ctx.enter_context(nc.psum_tensor("a_S", [P, 4, 512], F32))
        PT = ctx.enter_context(nc.psum_tensor("a_PT", [P, 2, 512], F32))
        O = ctx.enter_context(nc.psum_tensor("a_O", [P, NG, P], F32))
        M = ctx.enter_context(nc.psum_tensor("a_M", [P, 512], F32))
        SUMS, TURNED, Y = slice(0, 9 * H), slice(160, 160 + P), slice(288, 288 + D)
        ident = rank["const"][:, C_ID:C_ID + P]
        part = rank["const"][:, C_PART:C_PART + 4]
        near_mask = rank["const"][:, C_NEAR:C_NEAR + H]
        far_mask = rank["mask_bf"][:, C_FAR - C_MQ:C_FAR - C_MQ + P + 1]

        par_in, zeroed = sem("a_par_in"), sem("a_zeroed")
        bias_made = sem("a_bias_made")
        xa_in, xo_in = sem("a_xa_in"), sem("a_xo_in")
        seq_done = sem("a_seq_done")
        turned = sem("a_turned")
        xT_ready = sem("a_xT_ready")
        proj = sem("a_proj")
        split_ready = sem("a_split_ready")
        qkT_ready = sem("a_qkT_ready")
        near_mm = sem("a_near_mm")
        near_ready = sem("a_near_ready")
        prods = sem("a_prods")
        s01_ready = sem("a_s01_ready")
        sm_ready = sem("a_sm_ready")
        scored = sem("a_scored")
        far_maxed = sem("a_far_maxed")
        nm_ready = sem("a_nm_ready")
        exped = sem("a_exped")
        flipped = sem("a_flipped")
        flip_dve, flip_act = sem("a_flip_dve"), sem("a_flip_act")
        summed = sem("a_summed")
        sums_out, sums_turned = sem("a_sums_out"), sem("a_sums_turned")
        d01_ready, p01_ready = sem("a_d01_ready"), sem("a_p01_ready")
        pool_chain = sem("a_pool_chain")
        fin = sem("a_fin")
        on_T, oT_ready, y_mm = sem("a_on_T"), sem("a_oT_ready"), sem("a_y_mm")

        def load_parameters(sp):
            for r in range(4):
                for i, w in enumerate((Wq, Wk)):
                    sp.dma_start(w_pad[:, i, :, r, :], w.rearrange("c (h d) -> c h d", h=H)).then_inc(par_in, 16)
                for g in range(G):
                    rows = slice(32 * g + HA * r, 32 * g + HA * (r + 1))
                    for i, b in enumerate((bq, bk)):
                        sp.dma_start(b_pad[rows, i, :], b.rearrange("(n g d) -> g d n", g=G, d=HA)[g],
                                     allow_slow_non_contiguous=True).then_inc(par_in, 16)
                    sp.dma_start(r_pad[rows, :], rel_k[0:1, :].rearrange("a d -> d a"),
                                 allow_slow_non_contiguous=True).then_inc(par_in, 16)
            for i, w in enumerate((Wq, Wk, Wv)):
                sp.dma_start(w_all[:, D * i:D * (i + 1)], w).then_inc(par_in, 16)
            sp.dma_start(wo[:], Wo).then_inc(par_in, 16)
            for i, b in enumerate((bq, bk, bv, bo)):
                sp.dma_start(bias[:, i, :], bc(b, 0, P)).then_inc(par_in, 16)
            for i, r in enumerate((rel_k, rel_v)):
                sp.dma_start(rel[:, i, :, :], bc(r[0:3, :], 0, P)).then_inc(par_in, 16)

        norm_and_constants(nc, x, const, state, rank, 1e-5, load_parameters)
        block = ctx.enter_context(nc.Block())
        NPAIR = TPS * PAIRS

        def region(qt):
            return (0, P, 1) if qt == 0 else (P * qt - 1, P + 1, 0)

        @block.sync
        def _(sp):
            def load_xa(s):
                sp.dma_start(xa[:], state[:, bass.ds(s, 1), :, :].rearrange("p a t d -> p (a t) d")).then_inc(xa_in, 16)

            def load_xo(s):
                sp.dma_start(xo[:], x[bass.ds(s, 1), :, :].rearrange("a (t p) d -> p (a t) d", p=P)).then_inc(xo_in, 16)

            load_xa(0)
            load_xo(0)
            with sp.Fori(1, B) as s:
                sp.wait_ge(turned, s)
                load_xa(s)
                sp.wait_ge(seq_done, s * TPS + 1)
                load_xo(s)

        PAR = 16 * (4 * (2 + 3 * G) + 3 + 1 + 4 + 2)

        @block.gpsimd
        def _(pool):
            pool.memset(xT[:, 0:1], 0.0).then_inc(zeroed, 1)
            pool.memset(va[:, :, :, HA:HA + 1], 1.0).then_inc(zeroed, 1)
            pool.memset(va[:, :, :, HA + 1:], 0.0).then_inc(zeroed, 1)
            pool.wait_ge(par_in, PAR)
            for i in range(2):
                for r in range(3):
                    pool.tensor_tensor(kv_bias[:, i, r, :].rearrange("p (h d) -> p h d", h=H),
                                       bias[:, 1 + i, :].rearrange("p (h d) -> p h d", h=H),
                                       bc(rel[:, i, r, :], 1, H), ALU.add).then_inc(bias_made, 1)
            pool.tensor_tensor(b_pad[:, 1, :], b_pad[:, 1, :], r_pad[:].broadcast_to([P, NG]), ALU.add).then_inc(bias_made, 1)
            pool.wait_ge(bias_made, 7)
            pool.tensor_tensor(b_low[:], b_pad[:], bc(part[:, 0:2], 2, NG), ALU.mult).then_inc(bias_made, 1)
            with pool.Fori(0, B) as s:
                pool.wait_ge(xo_in, 16 * s + 16)
                pool.tensor_tensor(xo[:], xo[:], bc(bias[:, 3, :], 1, TPS), ALU.add).then_inc(bias_made, 1)
                pool.wait_ge(near_ready, 6 * TPS * (s + 1))
                for i in range(2):
                    pool.tensor_tensor(prod[:, i, :, :], near[:, 0, :, :], near[:, 1 + i, :, :], ALU.mult).then_inc(prods, 1)
                for qt in range(TPS):
                    u = s * TPS + qt
                    pool.wait_ge(p01_ready, u + 1)
                    for i in range(2):
                        pool.tensor_tensor(pv_near[:, i, :].rearrange("p (h d) -> p h d", h=H),
                                           near[:, 3 + i, qt, :].rearrange("p (h d) -> p h d", h=H),
                                           bc(p01[:, i, :], 2, HA), ALU.mult).then_inc(pool_chain, 1)
                    pool.tensor_tensor(p_sum[:], p01[:, 0, :], p01[:, 1, :], ALU.add).then_inc(pool_chain, 1)
                    pool.wait_ge(pool_chain, 4 * u + 2)
                    pool.tensor_tensor(pv_near[:, 0, :], pv_near[:, 0, :], pv_near[:, 1, :], ALU.add).then_inc(pool_chain, 1)

        @block.tensor
        def _(pe):
            def near_products(s, qt):
                if qt >= 2:
                    pe.wait_ge(near_ready, 6 * (s * TPS + qt - 1))
                pe.matmul(S[:, 2 + qt % 2, 0:3 * D], xT[:, 1 + P * qt:1 + P * (qt + 1)], w_all[:], start=True, stop=True)
                pe.matmul(PT[:, qt % 2, 0:2 * D], xT[:, P * qt:P * (qt + 1)], w_all[:, D:3 * D],
                          start=True, stop=True).then_inc(near_mm, 1)

            def scores(s, n):
                qt, pr = divmod(n, PAIRS)
                lo, width, skip = region(qt)
                if n >= 2:
                    pe.wait_ge(exped, 2 * (s * NPAIR + n - 1))
                for j in range(2):
                    pe.matmul(S[:, 2 * (n % 2) + j, lo:lo + width], rank["id_bf"][:], far_mask[:, skip:],
                              start=True, stop=False, skip_group_check=True)
                for j in range(2):
                    h = 2 * pr + j
                    g, r = h // G, 32 * (h % G)
                    last = pe.matmul(S[:, 2 * (n % 2) + j, 0:P * (qt + 1)], qkT[r:r + 32, 0, g, P * qt:P * (qt + 1)],
                                     qkT[r:r + 32, 1, g, 0:P * (qt + 1)], start=False, stop=True,
                                     skip_group_check=True)
                last.then_inc(scored, 1)

            def turn_weights(s, n):
                qt = n // PAIRS
                for j in range(2):
                    pe.wait_ge(exped, 2 * (s * NPAIR + n) + j + 1)
                    if n:
                        pe.wait_ge((flip_dve, flip_act)[j], s * NPAIR + n)
                    for kt in range(qt + 1):
                        last = pe.transpose(PT[:, j, P * kt:P * (kt + 1)],
                                            probs[:, 2 * (n % 2) + j, P * kt:P * (kt + 1)], ident)
                    last.then_inc(flipped, 1)

            def values(s, n):
                qt, pr = divmod(n, PAIRS)
                if qt and pr == 0:
                    pe.wait_ge(sums_out, s * TPS + qt)
                for j in range(2):
                    pe.wait_ge((flip_dve, flip_act)[j], s * NPAIR + n + 1)
                for kt in range(qt + 1):
                    for j in range(2):
                        h = 2 * pr + j
                        r = 32 * (h % G)
                        last = pe.matmul(O[r:r + 32, h // G, :], va[:, kt, h, :],
                                         probsT[:, n % 2, j, P * kt:P * (kt + 1)], start=(kt == 0), stop=(kt == qt),
                                         skip_group_check=True)
                last.then_inc(summed, 1)

            def turn_sums(s, qt):
                u = s * TPS + qt
                pe.wait_ge(sums_out, u + 1)
                pe.wait_ge(seq_done, u + 1)
                keep = ident.rearrange("p (h c) -> p h c", h=G)[:, :, 0:HA + 1]
                for g in range(NG):
                    last = pe.matmul(M[:, 36 * g:36 * (g + 1)], sumsT[:, g, :], keep, start=True, stop=True,
                                     skip_group_check=True)
                last.then_inc(sums_turned, 1)

            def turn_output(s, qt):
                pe.wait_ge(fin, 4 * (s * TPS + qt) + 4)
                pe.transpose(M[:, TURNED], on[:], ident).then_inc(on_T, 1)

            def project_output(s, qt):
                pe.wait_ge(oT_ready, s * TPS + qt + 1)
                pe.matmul(M[:, Y], oT[:], wo[:], start=True, stop=True).then_inc(y_mm, 1)

            pe.wait_ge(bias_made, 8)
            pe.wait_ge(zeroed, 3)
            with pe.Fori(0, B) as s:
                pe.wait_ge(xa_in, 16 * s + 16)
                for t in range(TPS):
                    last = pe.transpose(PT[:, 0, P * t:P * (t + 1)], xa[:, t, :], ident)
                last.then_inc(turned, 1)
                pe.wait_ge(xT_ready, s + 1)
                for i in range(2):
                    for g in range(NG):
                        c = i * NG + g
                        if 1 <= c <= TPS:
                            near_products(s, c - 1)
                        if c >= 2:
                            pe.wait_ge(split_ready, 2 * (2 * NG * s + c - 1))
                        pe.matmul(S[:, c % 2, :], w_pad[:, i, G * g:G * (g + 1), :, :].rearrange("p h r d -> p (h r d)"),
                                  xT[:, 1:N + 1], start=True, stop=True).then_inc(proj, 1)
                pe.wait_ge(qkT_ready, 2 * NG * s + 2 * NG)
                pe.wait_ge(near_ready, 6 * TPS * (s + 1))
                scores(s, 0)
                scores(s, 1)
                for n in range(NPAIR):
                    qt, at = divmod(n, PAIRS)
                    turn_weights(s, n)
                    if n + 2 < NPAIR:
                        scores(s, n + 2)
                    if n:
                        values(s, n - 1)
                    if qt and at == 1:
                        turn_sums(s, qt - 1)
                    if qt and at == 3:
                        turn_output(s, qt - 1)
                    if qt and at == 4:
                        project_output(s, qt - 1)
                values(s, NPAIR - 1)
                turn_sums(s, TPS - 1)
                turn_output(s, TPS - 1)
                project_output(s, TPS - 1)

        @block.scalar
        def _(act):
            def weights(s, n):
                k = s * NPAIR + n
                qt, pr = divmod(n, PAIRS)
                act.wait_ge(nm_ready, k + 1)
                if n >= 2:
                    act.wait_ge(flipped, 2 * (k - 1))
                for j in range(2):
                    h = 2 * pr + j
                    act.activation(probs[:, 2 * (n % 2) + j, 0:P * (qt + 1)],
                                   S[:, 2 * (n % 2) + j, 0:P * (qt + 1)], ACT.Exp,
                                   bias=nm[:, qt % 2, h:h + 1], scale=SCALE_A).then_inc(exped, 1)

            def turn_output(s, qt):
                act.wait_ge(on_T, s * TPS + qt + 1)
                act.activation(oT[:], M[:, TURNED], ACT.Copy).then_inc(oT_ready, 1)

            def copy_sums(s, qt):
                act.wait_ge(summed, s * NPAIR + (qt + 1) * PAIRS)
                act.activation(sumsT[:], O[:], ACT.Copy).then_inc(sums_out, 1)

            with act.Fori(0, B) as s:
                act.wait_ge(turned, s + 1)
                act.activation(xT[:, 1:N + 1], PT[:, 0, :], ACT.Copy).then_inc(xT_ready, 1)
                for i in range(2):
                    for g in range(NG):
                        c = i * NG + g
                        act.wait_ge(proj, 2 * NG * s + c + 1)
                        if c >= 2:
                            act.wait_ge(qkT_ready, 2 * NG * s + c - 1)
                        act.activation(high[:, c % 2, :], S[:, c % 2, :], ACT.Identity,
                                       bias=b_pad[:, i, g:g + 1]).then_inc(split_ready, 1)
                        act.activation(lowT[:, c % 2, :], S[:, c % 2, :], ACT.Identity,
                                       bias=b_low[:, i, g:g + 1], scale=part[:, i:i + 1]).then_inc(split_ready, 1)
                weights(s, 0)
                for n in range(NPAIR):
                    k = s * NPAIR + n
                    qt, at = divmod(n, PAIRS)
                    if n + 1 < NPAIR:
                        weights(s, n + 1)
                    act.wait_ge(flipped, 2 * k + 2)
                    if n >= 2:
                        act.wait_ge(summed, k - 1)
                    act.activation(probsT[:, n % 2, 1, 0:P * (qt + 1)], PT[:, 1, 0:P * (qt + 1)],
                                   ACT.Copy).then_inc(flip_act, 1)
                    if qt and at == 0:
                        copy_sums(s, qt - 1)
                    if qt and at == 3:
                        turn_output(s, qt - 1)
                    if at == PAIRS - 1:
                        act.wait_ge(d01_ready, 2 * (s * TPS + qt) + 2)
                        act.activation(p01[:], d01[:], ACT.Exp, scale=1.0).then_inc(p01_ready, 1)
                copy_sums(s, TPS - 1)
                turn_output(s, TPS - 1)

        @block.vector
        def _(dve):
            def maxima(s, n):
                k = s * NPAIR + n
                qt, pr = divmod(n, PAIRS)
                hs = slice(2 * pr, 2 * pr + 2)
                dve.wait_ge(scored, k + 1)
                dve.tensor_reduce(far_max[:, qt % 2, hs], S[:, 2 * (n % 2):2 * (n % 2) + 2, 0:P * (qt + 1)],
                                  X, ALU.max).then_inc(far_maxed, 1)
                dve.wait_ge(far_maxed, k + 1)
                dve.scalar_tensor_tensor(nm[:, qt % 2, hs], far_max[:, qt % 2, hs], -SCALE_A, sm[:, qt, hs],
                                         ALU.mult, ALU.min).then_inc(nm_ready, 1)

            def normalize(s, qt):
                u = s * TPS + qt
                dve.wait_ge(pool_chain, 4 * u + 4)
                dve.wait_ge(sums_turned, u + 1)
                o = M[:, SUMS].rearrange("p (h d) -> p h d", h=H)
                dve.tensor_tensor(den[:], o[:, :, HA], p_sum[:], ALU.add).then_inc(fin, 1)
                dve.tensor_tensor(num[:].rearrange("p (h d) -> p h d", h=H), o[:, :, 0:HA],
                                  pv_near[:, 0, :].rearrange("p (h d) -> p h d", h=H), ALU.add).then_inc(fin, 1)
                dve.wait_ge(fin, 4 * u + 2)
                dve.reciprocal(rden[:], den[:]).then_inc(fin, 1)
                dve.wait_ge(fin, 4 * u + 3)
                dve.tensor_tensor(on[:].rearrange("p (h d) -> p h d", h=H),
                                  num[:].rearrange("p (h d) -> p h d", h=H), bc(rden[:], 2, HA),
                                  ALU.mult).then_inc(fin, 1)

            def add_output(s, qt):
                dve.wait_ge(y_mm, s * TPS + qt + 1)
                if qt == 0:
                    dve.wait_ge(bias_made, 8 + 1 + s)
                dve.tensor_tensor(total[:, bass.ds(s, 1), qt, :], M[:, Y].unsqueeze(1),
                                  xo[:, qt, :].unsqueeze(1), ALU.add).then_inc(seq_done, 1)

            def near_biases(s, qt):
                dve.wait_ge(near_mm, s * TPS + qt + 1)
                a, b = S[:, 2 + qt % 2, :], PT[:, qt % 2, :]
                for i, src, bia in ((0, a[:, 0:D], bias[:, 0, :]),
                                    (1, a[:, D:2 * D], kv_bias[:, 0, 2, :]),
                                    (2, b[:, 0:D], kv_bias[:, 0, 1, :]),
                                    (3, a[:, 2 * D:3 * D], kv_bias[:, 1, 2, :]),
                                    (4, b[:, D:2 * D], kv_bias[:, 1, 1, :])):
                    dve.tensor_tensor(near[:, i, qt, :], src, bia, ALU.add).then_inc(near_ready, 1)
                dve.tensor_tensor(va[:, qt, :, 0:HA], a[:, 2 * D:3 * D].rearrange("p (h d) -> p h d", h=H),
                                  kv_bias[:, 1, 0, :].rearrange("p (h d) -> p h d", h=H),
                                  ALU.add).then_inc(near_ready, 1)

            def join_parts(s, c):
                i, g = divmod(c, NG)
                dve.wait_ge(split_ready, 2 * (2 * NG * s + c + 1))
                dve.scalar_tensor_tensor(qkT[:, i, g, :], high[:, c % 2, :].bitcast(F32), part[:, 2 + i:3 + i], lowT[:, c % 2, :],
                                         ALU.mult, ALU.add).then_inc(qkT_ready, 1)

            dve.memset(rden[:], 0.0).then_inc(seq_done, 1)
            with dve.Fori(0, B) as s:
                for c in range(2 * NG):
                    if 1 <= c <= TPS:
                        near_biases(s, c - 1)
                    join_parts(s, c)
                for i in range(2):
                    dve.wait_ge(prods, 2 * s + i + 1)
                    dve.tensor_reduce(s01[:, i, :, :], prod[:, i, :, :].rearrange("p t (h d) -> p t h d", h=H),
                                      X, ALU.add).then_inc(s01_ready, 1)
                dve.wait_ge(s01_ready, 2 * s + 2)
                dve.tensor_tensor(s01[:, 1, 0, :], s01[:, 1, 0, :], near_mask, ALU.add).then_inc(sm_ready, 1)
                dve.wait_ge(sm_ready, 3 * s + 1)
                dve.tensor_tensor(sm[:], s01[:, 0, :, :], s01[:, 1, :, :], ALU.max).then_inc(sm_ready, 1)
                dve.wait_ge(sm_ready, 3 * s + 2)
                dve.tensor_scalar(sm[:], sm[:], -SCALE_A, None, ALU.mult).then_inc(sm_ready, 1)
                dve.wait_ge(sm_ready, 3 * s + 3)
                maxima(s, 0)
                for n in range(NPAIR):
                    k = s * NPAIR + n
                    qt, at = divmod(n, PAIRS)
                    if n + 1 < NPAIR:
                        maxima(s, n + 1)
                    dve.wait_ge(flipped, 2 * k + 1)
                    if n >= 2:
                        dve.wait_ge(summed, k - 1)
                    dve.tensor_copy(probsT[:, n % 2, 0, 0:P * (qt + 1)], PT[:, 0, 0:P * (qt + 1)]).then_inc(flip_dve, 1)
                    if qt and at == 2:
                        normalize(s, qt - 1)
                    if qt and at == 5:
                        add_output(s, qt - 1)
                    if at == PAIRS - 1:
                        dve.wait_ge(nm_ready, s * NPAIR + n + 1)
                        for i in range(2):
                            dve.scalar_tensor_tensor(d01[:, i, :], s01[:, i, qt, :], SCALE_A, nm[:, qt % 2, :],
                                                     ALU.mult, ALU.add).then_inc(d01_ready, 1)
                normalize(s, TPS - 1)
                add_output(s, TPS - 1)
            dve.wait_ge(seq_done, B * TPS + 1)


def windowed_layers(nc, Wqkv, qs, ks, Wout, ln_g, ln_b, W1, b1, W2, b2, state, total, rank, out):
    with ExitStack() as ctx:
        sb = lambda n, s, d=F32: ctx.enter_context(nc.sbuf_tensor(n, s, d))
        sem = lambda n: ctx.enter_context(nc.semaphore(n))
        w_hi, w_lo = sb("w_hi", [P, 3 * INNER], F32R), sb("w_lo", [P, 3 * INNER], F32R)
        w_out = sb("w_out", [P, PAIRS, D])
        qk_scale = sb("qk_scale", [P, 4, HB])
        rope = sb("rope", [P, 4, TPS, HB])
        w1_raw = sb("w1_raw", [P, 2 * FF])
        w1_hi, w1_lo = sb("w1_hi", [P, 2 * FF], F32R), sb("w1_lo", [P, 2 * FF], F32R)
        w2 = sb("w2", [P, 3, D])
        b1c = sb("b1c", [P, 2, 3])
        gbc = sb("gbc", [P, 2])
        b2r = sb("b2r", [P, D])
        xcur = sb("xcur", [P, TPS, D])
        xsf = sb("xsf", [P, 2, P + 1])
        xh, xl = sb("xh", [P, 2, P], F32R), sb("xl", [P, 2, P], F32R)
        sq = sb("sq", [P, 2, INNER])
        t1 = sb("t1", [P, 2, 2, INNER])
        w_raw = t1[:].rearrange("p a b n -> p (a b n)")[:, 0:3 * INNER]
        t2 = sb("t2", [P, 2, INNER])
        ss = sb("ss", [P, 2 * H])
        rn = sb("rn", [P, 2 * H])
        half_ss, rn_tmp = sb("half_ss", [P, 2 * H]), sb("rn_tmp", [P, 2 * H])
        qT = sb("qT", [P, PAIRS, P])
        kT = sb("kT", [P, 2, PAIRS, 2, W + P])
        va = sb("va", [P, 2, 2, PAIRS, HB1])
        vs = sb("vs", [P, 2, 3, PAIRS, HB1])
        m = sb("m", [P, H])
        shared = sb("shared", [P, 3, INNER])
        e = shared[:, 0, :].rearrange("p (h k) -> p h k", h=H)
        pw = shared[:, 1, :].rearrange("p (h k) -> p h k", h=H)
        pT = shared[:, 2, :].rearrange("p (j q) -> p j q", j=PAIRS)
        hT = shared[:].rearrange("p a (b n) -> p (a b) n", b=2).rearrange("p (a j) n -> p a j n", a=2)
        rden = sb("rden", [P, 2, PAIRS])
        on = sb("on", [P, PAIRS, 2, HB])
        oT = sb("oT", [P, PAIRS, P])
        credit = sb("credit", [P, 16])
        zeros = sb("zeros", [P, PAIRS, W])
        xf = sb("xf", [P, 2, TPS, D])
        fsf = sb("fsf", [P, 2, N + 1])
        cen, sqf = t2[:, 0, :].rearrange("p (a n) -> p a n", a=2), t2[:, 1, :].rearrange("p (a n) -> p a n", a=2)
        var, rstd = sb("f_var", [P, 2 * TPS]), sb("f_rstd", [P, 2 * TPS])
        half_v, f_tmp = sb("f_half", [P, 2 * TPS]), sb("f_tmp", [P, 2 * TPS])
        fh, fl = sb("fh", [P, 2, N], F32R), sb("fl", [P, 2, N], F32R)
        gel = sq[:, 0, :].rearrange("p (a n) -> p a n", a=2)
        xr = sq[:, 1, :].rearrange("p (a t d) -> p a t d", a=2, t=TPS)
        PS = ctx.enter_context(nc.psum_tensor("PS", [P, 8, 512], F32))
        ident = rank["const"][:, C_ID:C_ID + P]
        id_bf, mask_bf, mean_w = rank["id_bf"], rank["mask_bf"], rank["mean_w"]
        mask_q = {t: mask_bf[:, 2 * W * (t == 0):2 * W * (t == 0) + 2 * W] for t in range(TPS)}

        RN_OPS = RSQRT_OPS + 1
        FFW_IN = 16 * (1 + 3 * 3 + 2 + 1)

        VS_IN = 16 * 8

        def placed(par, w):
            return ((0, None, 1, 2), (0, 1, 2, None))[par][w]

        made = sem("made")
        raw_in, wout_in, scale_in, ffw_in = sem("raw_in"), sem("wout_in"), sem("scale_in"), sem("ffw_in")
        x_in = [sem(f"x_in{t}") for t in range(TPS)]
        vs_in = [sem("vs_in0"), sem("vs_in1")]
        xf_in = [sem("xf_in0"), sem("xf_in1")]
        xr_in = [sem("xr_in0"), sem("xr_in1")]
        out_done = sem("out_done")
        hi_made, lo_made, rope_made = sem("hi_made"), sem("lo_made"), sem("rope_made")
        hi1_made, lo1_made = sem("hi1_made"), sem("lo1_made")
        xt_mm = sem("xt_mm")
        xsf_made = sem("xsf_made")
        xh_made, xl_made = sem("xh_made"), sem("xl_made")
        q_mm, k_mm, v_mm = sem("q_mm"), sem("k_mm"), sem("v_mm")
        sq_made = sem("sq_made")
        t_made = sem("t_made")
        ss_made = sem("ss_made")
        rn_chain = sem("rn_chain")
        added = sem("added")
        qn_made, kn_made = sem("qn_made"), sem("kn_made")
        carried = sem("carried")
        qt_mm, kt_mm = sem("qt_mm"), sem("kt_mm")
        qT_made, kT_made = sem("qT_made"), sem("kT_made")
        v_made = sem("v_made")
        s_mm = sem("s_mm")
        m_made = sem("m_made")
        e_made = sem("e_made")
        pw_made = sem("pw_made")
        pt_mm, pT_made = sem("pt_mm"), sem("pT_made")
        xf_begun = sem("xf_begun")
        pv_begun = sem("pv_begun")
        pv_half = sem("pv_half")
        pv_mm = sem("pv_mm")
        rden_made, on_made = sem("rden_made"), sem("on_made")
        ot_mm = sem("ot_mm")
        oT_made = sem("oT_made")
        y_mm = sem("y_mm")
        attn_done = sem("attn_done")
        ft_mm, fsf_made, mean_mm, cen_made = sem("ft_mm"), sem("fsf_made"), sem("mean_mm"), sem("cen_made")
        sqf_made, var_mm, f_chain, rb_mm = sem("sqf_made"), sem("var_mm"), sem("f_chain"), sem("rb_mm")
        xn_made, fh_made, fl_made, b2_made = sem("xn_made"), sem("fh_made"), sem("fl_made"), sem("b2_made")
        g_mm, a_mm = sem("g_mm"), sem("a_mm")
        gel_made, h_made = sem("gel_made"), sem("h_made")
        y2_mm = sem("y2_mm")
        ffn_done = sem("ffn_done")
        totaled = sem("totaled")
        block = ctx.enter_context(nc.Block())

        def attention(eng, lay, slot):
            for t in range(TPS):
                slot(lay, 0, t, range(t + 1))
            with eng.Fori(1, B) as s:
                for t in range(TPS):
                    slot(lay, s, t, range(4))
            for t in range(3):
                slot(lay, B, t, range(t + 1, 4))

        def number(lay, s, t):
            return lay * (B * TPS) + s * TPS + t

        def before(s, t, n=1):
            return (s, t - n) if t >= n else (s - 1, t - n + TPS)

        def feed_forward(eng, step):
            with eng.Fori(0, B // 2 - 1) as i:
                step(i, i + 1)
            step(B // 2 - 1, None)

        @block.sync
        def _(sp):
            def load_attention(lay):
                sp.dma_start(w_raw, Wqkv[bass.ds(lay, 1), :, :].rearrange("a c n -> (a c) n")).then_inc(raw_in, 16)
                sp.dma_start(w_out[:], Wout[bass.ds(lay, 1), :, :].rearrange("a (j p) d -> p (a j) d", p=P)).then_inc(wout_in, 16)
                for i, v in enumerate((qs, ks)):
                    v = v[bass.ds(lay, 1), :]
                    wide = v.broadcast_to([P, HB])
                    sp.dma_start(qk_scale[:, 2 * i, :], wide).then_inc(scale_in, 16)
                    sp.dma_start(qk_scale[:, 2 * i + 1, 0:32], wide[:, 32:64]).then_inc(scale_in, 16)
                    sp.dma_start(qk_scale[:, 2 * i + 1, 32:64], wide[:, 0:32]).then_inc(scale_in, 16)

            def load_ffn(lay):
                sp.dma_start(w1_raw[:], W1[bass.ds(lay, 1), :, :].rearrange("a c n -> (a c) n")).then_inc(ffw_in, 16)
                for j, (o, w) in enumerate(FC):
                    sp.dma_start(w2[0:w, j, :], W2[bass.ds(lay, 1), o:o + w, :].rearrange("a c n -> (a c) n")).then_inc(ffw_in, 16)
                    for i in range(2):
                        sp.dma_start(b1c[0:w, i, j:j + 1],
                                     b1[bass.ds(lay, 1), FF * i + o:FF * i + o + w].rearrange("a c -> c a"),
                                     allow_slow_non_contiguous=True).then_inc(ffw_in, 16)
                for i, v in enumerate((ln_g, ln_b)):
                    sp.dma_start(gbc[:, i:i + 1], v[bass.ds(lay, 1), :].rearrange("a c -> c a"),
                                 allow_slow_non_contiguous=True).then_inc(ffw_in, 16)
                sp.dma_start(b2r[:], b2[bass.ds(lay, 1), :].broadcast_to([P, D])).then_inc(ffw_in, 16)

            def layer(lay, prefetch):
                def source(i, a):
                    return state[:, bass.ds(i * 2 + a, 1), :, :].rearrange("p a t d -> p (a t) d")

                def load(i):
                    sp.sem_inc(xf_begun, 1)
                    for a in range(2):
                        sp.wait_ge(ft_mm, lay * B + i * 2 + a + 1)
                        sp.dma_start(xf[:, a, :, :], source(i, a)).then_inc(xf_in[a], 16)

                def slot(lay, s, t, ages):
                    T = number(lay, s, t)
                    sm, tm = before(s, t)
                    if 0 in ages:
                        if t == 0:
                            sp.wait_ge(ffn_done, lay * B + s + 1)
                        sp.wait_ge(attn_done, T + 1)
                        src = state[:, bass.ds(s, 1), t, :].rearrange("p a d -> p (a d)")
                        sp.dma_start(xcur[:, t, :], src).then_inc(x_in[t], 16)
                    if 1 in ages:
                        sp.wait_ge(v_made, 2 * T)
                        sp.wait_ge(pv_mm, T)
                        now, last = tm % 2, 1 - tm % 2
                        for par in range(2):
                            r = 2 * W * par
                            for to, tile, at, n in [(r, last, P - W, W)] + [(r + W, now, 0, W)]:
                                sp.dma_start(vs[to:to + n, now, 0, :, :], va[at:at + n, tile, par, :, :]).then_inc(vs_in[now], 16)
                            for w in range(1, NW):
                                k = placed(par, w)
                                if k is not None:
                                    sp.dma_start(vs[r:r + 2 * W, now, k, :, :],
                                                 va[W * (w - 1):W * (w + 1), now, par, :, :]).then_inc(vs_in[now], 16)
                    if list(ages) == [0, 1, 2]:
                        sp.wait_ge(ffn_done, lay * B + B)
                        load_ffn(lay)

                attention(sp, lay, slot)
                sp.wait_ge(attn_done, lay * (B * TPS) + 2 * TPS + TPS)
                load(0)
                if prefetch:
                    sp.wait_ge(attn_done, lay * (B * TPS) + B * TPS + TPS)
                    load_attention(lay + 1)

                def step(old, new):
                    if new is not None:
                        load(new)
                    for a in range(2):
                        sp.wait_ge(ffn_done, lay * B + old * 2 + a + B - 1)
                        sp.dma_start(xr[:, a, :, :], source(old, a)).then_inc(xr_in[a], 16)

                sp.wait_ge(attn_done, lay * (B * TPS) + B * TPS + TPS)
                sp.sem_inc(xf_begun, 1)
                feed_forward(sp, step)

            sp.wait_ge(made, 5)
            load_attention(0)
            with sp.Fori(0, LAYERS - 1) as lay:
                layer(lay, True)
            layer(LAYERS - 1, False)
            for s in range(B):
                sp.wait_ge(totaled, s + 1)
                sp.dma_start(out[s].rearrange("(t p) d -> p t d", p=P), total[:, s, :, :]).then_inc(out_done, 16)
            sp.wait_ge(out_done, 16 * B)

        @block.gpsimd
        def _(pool):
            pool.memset(zeros[:], 0.0).then_inc(made, 1)
            pool.memset(va[:], 1.0).then_inc(made, 1)
            pool.memset(fsf[:, :, 0:1], 0.0).then_inc(made, 1)
            pool.memset(kT[:], 0.0).then_inc(made, 1)
            pool.memset(b1c[:], 0.0).then_inc(made, 1)

            def layer(lay):
                pool.wait_ge(scale_in, 96 * lay + 96)
                pool.wait_ge(attn_done, lay * (B * TPS) + TPS)
                for i in range(4):
                    pool.tensor_tensor(rope[:, i, :, :],
                                       rank["const"][:, C_ROPE + i * TPS * HB:C_ROPE + (i + 1) * TPS * HB].rearrange("p (t d) -> p t d", t=TPS),
                                       bc(qk_scale[:, i, :], 1, TPS), ALU.mult).then_inc(rope_made, 1)

                def slot(lay, s, t, ages):
                    T = number(lay, s, t)
                    if 0 not in ages:
                        return
                    mine = t1[:, t % 2, :, :]
                    for i in range(2):
                        pool.wait_ge(t_made, 4 * T + 2 * i + 2)
                        pool.tensor_tensor(mine[:, i, :], mine[:, i, :], t2[:, i, :], ALU.add).then_inc(added, 1)
                    if 1 in ages:
                        pool.wait_ge(kT_made, 4 * T)
                    none = bc(zeros[:], 2, 2)
                    left = none if t == 0 else kT[:, 1 - t % 2, :, :, P:P + W]
                    pool.tensor_tensor(kT[:, t % 2, :, :, 0:W], left, none, ALU.add).then_inc(carried, 1)
                    pool.wait_ge(rn_chain, (T + 1) * RN_OPS)
                    for i, done in enumerate((qn_made, kn_made)):
                        pool.wait_ge(added, 2 * T + i + 1)
                        h = mine[:, i, :].rearrange("p (h d) -> p h d", h=H)
                        pool.tensor_tensor(h, h, bc(rn[:, H * i:H * (i + 1)], 2, HB), ALU.mult).then_inc(done, 1)
                attention(pool, lay, slot)

                def norm(i):
                    for a in range(2):
                        pool.wait_ge(cen_made, lay * B + i * 2 + a + 1)
                        pool.tensor_tensor(sqf[:, a, :], cen[:, a, :], cen[:, a, :], ALU.mult).then_inc(sqf_made, 1)

                def step(old, new):
                    if new is not None:
                        norm(new)
                    pool.wait_ge(ffw_in, FFW_IN * lay + FFW_IN)
                    for a in range(2):
                        pool.wait_ge(xr_in[a], 16 * (lay * (B // 2) + old) + 16)
                        pool.tensor_tensor(xr[:, a, :, :], xr[:, a, :, :], bc(b2r[:], 1, TPS), ALU.add).then_inc(b2_made, 1)

                norm(0)
                feed_forward(pool, step)

            with pool.Fori(0, LAYERS) as lay:
                layer(lay)

        @block.tensor
        def _(pe):
            def split_matmul(out, hi, lo, w_hi, w_lo):
                pe.matmul(out, hi, w_hi, start=True, stop=False)
                pe.matmul(out, lo, w_hi, start=False, stop=False)
                return pe.matmul(out, hi, w_lo, start=False, stop=True)

            def project(lay, T, i, bank, t, done, first):
                if first:
                    pe.wait_ge(lo_made, 3 * lay + i + 1)
                for c in range(2):
                    if i == 2 and not first:
                        pe.wait_ge(qT_made, 2 * T)
                    cols = slice(INNER * i + 512 * c, INNER * i + 512 * (c + 1))
                    last = split_matmul(PS[:, bank + c, :], xh[:, t % 2, :], xl[:, t % 2, :], w_hi[:, cols], w_lo[:, cols])
                last.then_inc(done, 1)

            def turn_tile(i, bank, t, done):
                for j in range(PAIRS):
                    last = pe.transpose(PS[:, bank + j // 4, P * (j % 4):P * (j % 4 + 1)],
                                        t1[:, t % 2, i, P * j:P * (j + 1)], ident)
                last.then_inc(done, 1)

            def mask_scores(t, bank):
                pe.matmul(PS[:, bank, :], id_bf[:], bc(mask_q[t], 1, PAIRS),
                          start=True, stop=False, skip_group_check=True)

            def score_pairs(t, pairs):
                for pair in pairs:
                    for w in range(NW):
                        last = pe.matmul(PS[W * w:W * (w + 1), 6 + pair // 4, P * (pair % 4):P * (pair % 4 + 1)],
                                         qT[:, pair, W * w:W * (w + 1)],
                                         kT[:, t % 2, pair, :, W * w:W * (w + 2)],
                                         start=False, stop=True, skip_group_check=True)
                return last

            def slot(lay, s, t, ages):
                T = number(lay, s, t)
                (s1, tile1), (s2, tile2) = before(s, t, 1), before(s, t, 2)
                if 0 in ages:
                    if 1 in ages and 3 not in ages:
                        pe.wait_ge(t_made, 4 * T)
                    pe.wait_ge(x_in[t], 16 * (lay * B + s) + 16)
                    pe.transpose(PS[:, 3, 0:P], xcur[:, t, :], ident).then_inc(xt_mm, 1)
                if 3 in ages:
                    pe.wait_ge(oT_made, 2 * T)
                    for pair in range(PAIRS):
                        last = pe.matmul(PS[:, 4, 0:D], oT[:, pair, :], w_out[:, pair, :],
                                         start=(pair == 0), stop=(pair == PAIRS - 1))
                    last.then_inc(y_mm, 1)
                if list(ages) == [3]:
                    for a in range(2):
                        variance(lay, 0, a, 6)
                if 0 in ages:
                    pe.wait_ge(xl_made, T + 3)
                    project(lay, T, 0, 0, t, q_mm, 1 not in ages)
                    project(lay, T, 1, 2, t, k_mm, 1 not in ages)
                if 1 in ages:
                    pe.wait_ge(v_made, 2 * T)
                    pe.wait_ge(attn_done, T + 2)
                    pe.wait_ge(qn_made, T)
                    turn_tile(0, 4, tile1, qt_mm)
                    if 2 in ages:
                        pe.wait_ge(e_made, 2 * (T - 1))
                    pe.wait_ge(kn_made, T)
                    turn_tile(1, 6, tile1, kt_mm)
                if 0 in ages:
                    project(lay, T, 2, 4, t, v_mm, 1 not in ages)
                if 2 in ages:
                    if 0 in ages:
                        pe.wait_ge(t_made, 4 * T + 2)
                    for c in range(2):
                        pe.wait_ge(pw_made, 2 * (T - 2) + c + 1)
                        for j in range(4):
                            last = pe.transpose(PS[:, c, P * j:P * (j + 1)],
                                                pw[:, 8 * c + 2 * j:8 * c + 2 * j + 2, :].rearrange("p r k -> p (r k)"), ident)
                        last.then_inc(pt_mm, 1)
                if list(ages) == [2, 3]:
                    for a in range(2):
                        turn(lay, 0, a, 6 + a)
                if 1 in ages:
                    pe.wait_ge(qT_made, 2 * T)
                    pe.wait_ge(kT_made, 4 * T)
                    pe.wait_ge(carried, T)
                    mask_scores(tile1, 6)
                    mask_scores(tile1, 7)
                    score_pairs(tile1, range(0, 2))
                if 2 in ages:
                    pe.wait_ge(vs_in[tile2 % 2], VS_IN * (lay * (B * 2) + s2 * 2 + tile2 // 2) + VS_IN)
                    pe.wait_ge(pT_made, 2 * (T - 1))
                    pe.sem_inc(pv_begun, 1)
                    for c, done in enumerate((pv_half, pv_mm)):
                        if c == 1 and 0 in ages:
                            pe.wait_ge(t_made, 4 * T + 4)
                            pe.sem_inc(pv_begun, 1)
                        for pair in range(4 * c, 4 * (c + 1)):
                            for par in range(2):
                                rows = slice(2 * W * par, 2 * W * (par + 1))
                                for w in range(NW):
                                    k = placed(par, w)
                                    v = va[rows, tile2 % 2, par, pair, :] if k is None else vs[rows, tile2 % 2, k, pair, :]
                                    last = pe.matmul(PS[W * w:W * (w + 1), 2 * c + par, HB1 * (pair % 4):HB1 * (pair % 4 + 1)],
                                                     pT[rows, pair, W * w:W * (w + 1)], v, start=True, stop=True,
                                                     skip_group_check=True)
                        last.then_inc(done, 1)
                if list(ages) == [2, 3]:
                    for a in range(2):
                        mean(lay, 0, a, 6 + a)
                if 1 in ages:
                    score_pairs(tile1, range(2, 5))
                if 2 in ages:
                    for c in range(2):
                        if 0 in ages:
                            pe.wait_ge(v_made, 2 * T + 1 + c)
                        pe.wait_ge(on_made, 2 * T - 1 + c)
                        for j in range(4):
                            last = pe.transpose(PS[:, 4 + c, P * j:P * (j + 1)],
                                                on[:, 4 * c + j, :, :].rearrange("p r d -> p (r d)"), ident)
                        last.then_inc(ot_mm, 1)
                if 1 in ages:
                    score_pairs(tile1, range(5, PAIRS)).then_inc(s_mm, 1)

            def turn(lay, i, a, bank):
                pe.wait_ge(xf_in[a], 16 * (lay * (B // 2) + i) + 16)
                pe.wait_ge(ffn_done, lay * B + i * 2 + a + B - 3)
                for t in range(TPS):
                    last = pe.transpose(PS[:, bank, P * t:P * (t + 1)], xf[:, a, t, :], ident)
                last.then_inc(ft_mm, 1)

            def mean(lay, i, a, bank):
                pe.wait_ge(fsf_made, 2 * (lay * B + i * 2 + a) + 2)
                pe.matmul(PS[:, bank, :], mean_w[:], fsf[:, a, 0:N], start=True, stop=True).then_inc(mean_mm, 1)

            def variance(lay, i, a, bank):
                pe.wait_ge(sqf_made, lay * B + i * 2 + a + 1)
                for t in range(TPS):
                    last = pe.matmul(PS[:, bank, TPS * a + t:TPS * a + t + 1], sqf[:, a, P * t:P * (t + 1)], mean_w[:, 0:1],
                                     start=True, stop=True, skip_group_check=True)
                last.then_inc(var_mm, 1)

            def spread(lay, i, a, bank):
                pe.wait_ge(f_chain, (lay * (B // 2) + i + 1) * RN_OPS)
                for t in range(TPS):
                    last = pe.matmul(PS[:, bank, P * t:P * (t + 1)], rstd[:, TPS * a + t:TPS * a + t + 1].broadcast_to([P, P]),
                                     ident, start=True, stop=True, skip_group_check=True)
                last.then_inc(rb_mm, 1)

            def feed(lay):
                def hidden(i, a, j):
                    U = lay * B + i * 2 + a
                    o, w = FC[j]
                    if j == 0:
                        pe.wait_ge(fl_made, U + 1)
                    for k, (sem_read, done) in enumerate(((gel_made, g_mm), (h_made, a_mm))):
                        bank = 2 + (6 * a + 2 * j + k) % 4
                        pe.wait_ge(sem_read, 3 * U + j + 1)
                        cols = slice(FF * (1 - k) + o, FF * (1 - k) + o + w)
                        split_matmul(PS[0:w, bank, :], w1_hi[:, cols], w1_lo[:, cols], fh[:, a, :], fl[:, a, :]).then_inc(done, 1)

                def output(i, a):
                    pe.wait_ge(h_made, 3 * (lay * B + i * 2 + a) + 5)
                    for t in range(TPS):
                        for j, (o, w) in enumerate(FC):
                            last = pe.matmul(PS[:, (0, 6)[a], P * t:P * (t + 1)], hT[0:w, a, j, P * t:P * (t + 1)],
                                             w2[0:w, j, :], start=(j == 0), stop=(j == 2), skip_group_check=True)
                    last.then_inc(y2_mm, 1)

                def step(old, new):
                    def both(stage, banks):
                        if new is not None:
                            for a in range(2):
                                stage(lay, new, a, banks[a])

                    both(turn, (0, 6))
                    hidden(old, 0, 0)
                    hidden(old, 0, 1)
                    pe.wait_ge(fl_made, lay * B + old * 2 + 2)
                    both(mean, (1, 7))
                    hidden(old, 0, 2)
                    hidden(old, 1, 0)
                    both(variance, (1, 1))
                    output(old, 0)
                    hidden(old, 1, 1)
                    hidden(old, 1, 2)
                    both(spread, (1, 7))
                    output(old, 1)

                pe.wait_ge(attn_done, lay * (B * TPS) + B * TPS + TPS)
                pe.wait_ge(hi1_made, lay + 1)
                pe.wait_ge(lo1_made, lay + 1)
                pe.wait_ge(ffw_in, FFW_IN * lay + FFW_IN)
                for a in range(2):
                    spread(lay, 0, a, (1, 7)[a])
                feed_forward(pe, step)

            pe.wait_ge(made, 5)
            with pe.Fori(0, LAYERS) as lay:
                pe.wait_ge(ffn_done, lay * B + B)
                pe.wait_ge(wout_in, 16 * lay + 16)

                attention(pe, lay, slot)
                feed(lay)

        @block.scalar
        def _(act):
            copy = lambda o, i: act.activation(o, i, ACT.Copy)

            def shift(lay, i, banks):
                for a in range(2):
                    act.wait_ge(ft_mm, lay * B + i * 2 + a + 3)
                    copy(fsf[0:64, a, 0:N], PS[0:64, banks[a], :]).then_inc(fsf_made, 1)
                    copy(fsf[64:P, a, 1:N + 1], PS[64:P, banks[a], :]).then_inc(fsf_made, 1)

            def slot(lay, s, t, ages):
                T = number(lay, s, t)
                p = t % 2
                if 0 in ages:
                    act.wait_ge(xt_mm, T + 1)
                    act.wait_ge(xl_made, T + 1)
                    if 1 in ages:
                        act.wait_ge(xsf_made, 3 * T)
                    copy(xsf[0:64, p, 0:P], PS[0:64, 3, 0:P]).then_inc(xsf_made, 1)
                    copy(xsf[64:P, p, 1:P + 1], PS[64:P, 3, 0:P]).then_inc(xsf_made, 1)
                    copy(xsf[64:P, p, 0:1], zeros[64:P, 0, 0:1] if t == 0 else xsf[64:P, 1 - p, P:P + 1]).then_inc(xsf_made, 1)
                    if 1 in ages:
                        act.wait_ge(ss_made, 2 * T)
                    act.wait_ge(q_mm, T + 1)
                    for c in range(2):
                        act.activation(sq[:, 0, 512 * c:512 * (c + 1)], PS[:, c, :], ACT.Square).then_inc(sq_made, 1)
                if 2 in ages:
                    if 3 in ages:
                        act.wait_ge(pt_mm, 2 * (T - 2))
                    for c in range(2):
                        act.wait_ge(e_made, 2 * (T - 2) + c + 1)
                        act.activation(pw[:, 8 * c:8 * (c + 1), :], e[:, 8 * c:8 * (c + 1), :], ACT.Exp).then_inc(pw_made, 1)
                if 1 in ages:
                    act.wait_ge(qt_mm, T + 1)
                    for c in range(2):
                        copy(qT[:, 4 * c:4 * (c + 1), :], PS[:, 4 + c, :].rearrange("p (j q) -> p j q", j=4)).then_inc(qT_made, 1)
                if 0 in ages:
                    act.wait_ge(k_mm, T + 1)
                    for c in range(2):
                        act.activation(sq[:, 1, 512 * c:512 * (c + 1)], PS[:, 2 + c, :], ACT.Square).then_inc(sq_made, 1)
                if 1 in ages:
                    act.wait_ge(kt_mm, T + 1)
                    for c in range(2):
                        for par in range(2):
                            rows = slice(HB * par, HB * (par + 1))
                            copy(kT[rows, 1 - p, 4 * c:4 * (c + 1), par, W:],
                                 PS[rows, 6 + c, :].rearrange("p (j q) -> p j q", j=4)).then_inc(kT_made, 1)
                if 2 in ages:
                    act.wait_ge(pv_mm, T)
                    for c in range(2):
                        act.wait_ge(pt_mm, 2 * (T - 2) + c + 1)
                        copy(pT[:, 4 * c:4 * (c + 1), :], PS[:, c, :].rearrange("p (j q) -> p j q", j=4)).then_inc(pT_made, 1)
                if 0 in ages:
                    act.wait_ge(v_mm, T + 3)
                    act.wait_ge(pv_mm, T + 1)
                    if t:
                        act.wait_ge(vs_in[1 - p], VS_IN * (lay * (B * 2) + s * 2 + (t - 1) // 2) + VS_IN)
                    elif 1 in ages:
                        act.wait_ge(vs_in[1], VS_IN * (lay * (B * 2) + s * 2))
                    for c in range(2):
                        copy(va[:, p, :, 4 * c:4 * (c + 1), 0:HB],
                             PS[:, 4 + c, :].rearrange("p (j r d) -> p r j d", j=4, r=2)).then_inc(v_made, 1)
                if list(ages) == [2, 3]:
                    shift(lay, 0, (6, 7))
                if 2 in ages:
                    for c in range(2):
                        act.wait_ge(ot_mm, 2 * T - 1 + c)
                        act.wait_ge(y_mm, T)
                        copy(oT[:, 4 * c:4 * (c + 1), :],
                             PS[:, 4 + c, :].rearrange("p (j q) -> p j q", j=4)).then_inc(oT_made, 1)

            def feed(lay):
                def step(old, new):
                    if new is not None:
                        shift(lay, new, (0, 6))
                    for a in range(2):
                        for j, (o, w) in enumerate(FC):
                            C = (lay * B + old * 2 + a) * 3 + j
                            act.wait_ge(g_mm, C + 1)
                            act.wait_ge(h_made, C + 1)
                            act.activation(gel[0:w, (3 * a + j) % 2, :], PS[0:w, 2 + (6 * a + 2 * j) % 4, :], ACT.Gelu,
                                           bias=b1c[0:w, 1, j:j + 1]).then_inc(gel_made, 1)

                feed_forward(act, step)

            act.wait_ge(made, 5)
            copy(credit[:, 15:16], zeros[:, 0, 0:1]).then_inc(gel_made, 2)
            with act.Fori(0, LAYERS) as lay:
                act.wait_ge(raw_in, 16 * lay + 16)
                for i in range(3):
                    copy(w_hi[:, INNER * i:INNER * (i + 1)], w_raw[:, INNER * i:INNER * (i + 1)]).then_inc(hi_made, 1)
                attention(act, lay, slot)
                act.wait_ge(ffw_in, FFW_IN * lay + FFW_IN)
                copy(w1_hi[:], w1_raw[:]).then_inc(hi1_made, 1)
                feed(lay)

        @block.vector
        def _(dve):
            def center(lay, i, a, bank):
                U = lay * B + i * 2 + a
                dve.wait_ge(fsf_made, 2 * U + 2)
                dve.wait_ge(mean_mm, U + 1)
                dve.tensor_tensor(cen[:, a, :], fsf[:, a, 0:N], PS[:, bank, :], ALU.subtract).then_inc(cen_made, 1)

            def deviations(lay, i, bank):
                V = lay * (B // 2) + i
                dve.wait_ge(var_mm, lay * B + i * 2 + 2)
                dve.tensor_scalar(var[:], PS[:, bank, 0:2 * TPS], 1e-5, None, ALU.add).then_inc(f_chain, 1)
                dve.wait_ge(f_chain, V * RN_OPS + 1)
                rsqrt_steps(dve, f_chain, V * RN_OPS + 1, rstd[:], var[:], half_v[:], f_tmp[:])

            def norm(lay, i, a, bank):
                U = lay * B + i * 2 + a
                dve.wait_ge(rb_mm, U + 1)
                dve.wait_ge(ffw_in, FFW_IN * lay + FFW_IN)
                dve.tensor_tensor(cen[:, a, :], cen[:, a, :], PS[:, bank, :], ALU.mult).then_inc(xn_made, 1)
                dve.wait_ge(xn_made, 2 * U + 1)
                dve.tensor_scalar(cen[:, a, :], cen[:, a, :], gbc[:, 0:1], gbc[:, 1:2], ALU.mult, ALU.add).then_inc(xn_made, 1)
                dve.wait_ge(xn_made, 2 * U + 2)
                dve.tensor_copy(fh[:, a, :], cen[:, a, :]).then_inc(fh_made, 1)
                dve.wait_ge(fh_made, U + 1)
                dve.tensor_tensor(fl[:, a, :], cen[:, a, :], fh[:, a, :].bitcast(F32), ALU.subtract).then_inc(fl_made, 1)

            def slot(lay, s, t, ages):
                T = number(lay, s, t)
                s3, tile3 = before(s, t, 3)
                p = t % 2
                if 0 in ages:
                    dve.wait_ge(xsf_made, 3 * T + 3)
                    dve.wait_ge(v_mm, T + 1)
                    dve.tensor_copy(xh[:, p, :], xsf[:, p, 0:P]).then_inc(xh_made, 1)
                    dve.wait_ge(xh_made, T + 1)
                    dve.tensor_tensor(xl[:, p, :], xsf[:, p, 0:P], xh[:, p, :].bitcast(F32), ALU.subtract).then_inc(xl_made, 1)
                if 2 in ages:
                    dve.wait_ge(s_mm, T - 1)
                    dve.tensor_reduce(m[:], PS[:, 6:8, :].rearrange("p b (h k) -> p (b h) k", h=8), X, ALU.max).then_inc(m_made, 1)
                    dve.wait_ge(m_made, T - 1)
                    if 3 in ages:
                        dve.wait_ge(pw_made, 2 * (T - 2))
                    for c in range(2):
                        hs = slice(8 * c, 8 * (c + 1))
                        dve.tensor_tensor(e[:, hs, :], PS[:, 6 + c, :].rearrange("p (h k) -> p h k", h=8),
                                          bc(m[:, hs], 2, 2 * W), ALU.subtract).then_inc(e_made, 1)
                if 3 in ages:
                    dve.wait_ge(y_mm, T)
                    dve.tensor_tensor(state[:, bass.ds(s3, 1), tile3, :], PS[:, 4, 0:D].unsqueeze(1),
                                      xcur[:, tile3, :].unsqueeze(1), ALU.add).then_inc(attn_done, 1)
                if 0 in ages:
                    if 1 in ages:
                        dve.wait_ge(kt_mm, T)
                        dve.wait_ge(added, 2 * T)
                    for i in range(2):
                        for c in range(2):
                            dve.wait_ge(sq_made, 4 * T + 2 * i + c + 1)
                            src = PS[:, 2 * i + c, :].rearrange("p (h d) -> p h d", h=8)
                            cols = slice(512 * c, 512 * (c + 1))
                            o1 = t1[:, p, i, cols].rearrange("p (h d) -> p h d", h=8)
                            o2 = t2[:, i, cols].rearrange("p (h d) -> p h d", h=8)
                            dve.tensor_tensor(o1, src, bc(rope[:, 2 * i, t, :], 1, 8), ALU.mult)
                            dve.tensor_tensor(o2[:, :, 0:32], src[:, :, 32:64], bc(rope[:, 2 * i + 1, t, 0:32], 1, 8), ALU.mult)
                            dve.tensor_tensor(o2[:, :, 32:64], src[:, :, 0:32], bc(rope[:, 2 * i + 1, t, 32:64], 1, 8),
                                              ALU.mult).then_inc(t_made, 1)
                    for i in range(2):
                        dve.tensor_reduce(ss[:, H * i:H * (i + 1)], sq[:, i, :].rearrange("p (h d) -> p h d", h=H),
                                          X, ALU.add).then_inc(ss_made, 1)
                if 2 in ages:
                    for c in range(2):
                        if c == 0:
                            dve.wait_ge(pv_half, T - 1)
                            dve.wait_ge(ot_mm, 2 * T - 2)
                        else:
                            dve.wait_ge(pv_mm, T + 1)
                        o = PS[:, 2 * c:2 * c + 2, 0:4 * HB1].rearrange("p r (j e) -> p r j e", e=HB1)
                        pairs = slice(4 * c, 4 * (c + 1))
                        dve.reciprocal(rden[:, :, pairs], o[:, :, :, HB]).then_inc(rden_made, 1)
                        dve.wait_ge(rden_made, 2 * (T - 2) + c + 1)
                        dve.tensor_tensor(on[:, pairs, :, :].rearrange("p j r d -> p r j d"), o[:, :, :, 0:HB],
                                          bc(rden[:, :, pairs], 3, HB), ALU.mult).then_inc(on_made, 1)
                if list(ages) == [2, 3]:
                    for a in range(2):
                        center(lay, 0, a, 6 + a)
                if 0 in ages:
                    dve.wait_ge(ss_made, 2 * T + 2)
                    if 1 in ages:
                        dve.wait_ge(kn_made, T)
                    dve.tensor_scalar(ss[:], ss[:], 1e-24, None, ALU.max).then_inc(rn_chain, 1)
                    dve.wait_ge(rn_chain, T * RN_OPS + 1)
                    rsqrt_steps(dve, rn_chain, T * RN_OPS + 1, rn[:], ss[:], half_ss[:], rn_tmp[:])

            def feed(lay):
                def hidden(i, a, j):
                    U = lay * B + i * 2 + a
                    o, w = FC[j]
                    dve.wait_ge(a_mm, 3 * U + j + 1)
                    dve.wait_ge(gel_made, 3 * U + j + 3)
                    dve.scalar_tensor_tensor(hT[0:w, a, j, :], PS[0:w, 2 + (6 * a + 2 * j + 1) % 4, :],
                                             b1c[0:w, 0, j:j + 1], gel[0:w, (3 * a + j) % 2, :],
                                             ALU.add, ALU.mult).then_inc(h_made, 1)

                def finish(i, a):
                    U = lay * B + i * 2 + a
                    dve.wait_ge(y2_mm, U + 1)
                    dve.wait_ge(b2_made, U + 1)
                    dve.tensor_tensor(state[:, bass.ds(i * 2 + a, 1), :, :].rearrange("p a t d -> p (a t) d"),
                                      PS[:, (0, 6)[a], :].rearrange("p (t d) -> p t d", t=TPS),
                                      xr[:, a, :, :], ALU.add).then_inc(ffn_done, 1)

                def step(old, new):
                    hidden(old, 0, 0)
                    hidden(old, 0, 1)
                    if new is not None:
                        center(lay, new, 0, 1)
                        center(lay, new, 1, 7)
                    hidden(old, 0, 2)
                    hidden(old, 1, 0)
                    if new is not None:
                        deviations(lay, new, 1)
                    finish(old, 0)
                    hidden(old, 1, 1)
                    hidden(old, 1, 2)
                    if new is not None:
                        norm(lay, new, 0, 1)
                        norm(lay, new, 1, 7)
                    finish(old, 1)

                feed_forward(dve, step)

            dve.wait_ge(made, 5)
            for i, (target, n) in enumerate(((xl_made, 2), (v_mm, 2), (pv_mm, 2), (attn_done, 4), (h_made, 2), (ffn_done, B),
                                         (oT_made, 4), (on_made, 2), (y_mm, 2), (ot_mm, 2), (qt_mm, 1), (kt_mm, 1),
                                         (ft_mm, 2))):
                dve.memset(credit[:, i:i + 1], 0.0).then_inc(target, n)
            with dve.Fori(0, LAYERS) as lay:
                dve.wait_ge(rope_made, 4 * lay + 4)
                for i in range(3):
                    dve.wait_ge(hi_made, 3 * lay + i + 1)
                    cols = slice(INNER * i, INNER * (i + 1))
                    dve.tensor_tensor(w_lo[:, cols], w_raw[:, cols], w_hi[:, cols].bitcast(F32), ALU.subtract).then_inc(lo_made, 1)
                attention(dve, lay, slot)
                deviations(lay, 0, 6)
                dve.wait_ge(hi1_made, lay + 1)
                dve.tensor_tensor(w1_lo[:], w1_raw[:], w1_hi[:].bitcast(F32), ALU.subtract).then_inc(lo1_made, 1)
                for a in range(2):
                    norm(lay, 0, a, (1, 7)[a])
                feed(lay)
            dve.wait_ge(ffn_done, LAYERS * B + B)
            for s in range(B):
                dve.tensor_tensor(total[:, s, :, :], total[:, s, :, :], state[:, s, :, :], ALU.add).then_inc(totaled, 1)


def build(nc, x, Wq, bq, Wk, bk, Wv, bv, Wo, bo, rel_k, rel_v, Wqkv, qs, ks, Wout, ln_g, ln_b,
          W1, b1, W2, b2, const, out):
    with ExitStack() as ctx:
        sb = lambda n, s, d=F32: ctx.enter_context(nc.sbuf_tensor(n, s, d))
        state = sb("state", [P, B, TPS, D])
        total = sb("total", [P, B, TPS, D])
        rank = {"const": sb("constants", [P, NCONST]), "id_bf": sb("id_bf", [P, P], BF16),
                "mask_bf": sb("mask_bf", [P, C_NEAR - C_MQ], BF16), "mean_w": sb("mean_w", [P, P])}
        relative_attention(nc, x, const, Wq, bq, Wk, bk, Wv, bv, Wo, bo, rel_k, rel_v, state, total, rank)
        windowed_layers(nc, Wqkv, qs, ks, Wout, ln_g, ln_b, W1, b1, W2, b2, state, total, rank, out)


_INS = ["x", "W_q", "b_q", "W_k", "b_k", "W_v", "b_v", "W_o", "b_o", "rel_k_table", "rel_v_table"]
_INS = ["L0_attn_" + n for n in _INS] + ["L0_ffn_" + n for n in (
    "Wqkv", "q_scale", "k_scale", "Wo", "ln_g", "ln_b", "W1", "b1", "W2", "b2")]


def kernel(**inputs):
    import concourse.bacc as bacc
    from concourse.bass_utils import run_bass_kernel_spmd

    nc = bacc.Bacc("TRN2", target_bir_lowering=False, num_devices=1)
    arrays, args = {}, []
    for name in _INS + ["const"]:
        a = constants() if name == "const" else np.ascontiguousarray(inputs[name])
        arrays["in_" + name] = a
        args.append(nc.dram_tensor("in_" + name, a.shape, mybir.dt.from_np(a.dtype), kind="ExternalInput").ap())
    args.append(nc.dram_tensor("out_0", (B, N, D), F32, kind="ExternalOutput").ap())
    build(nc, *args)
    return run_bass_kernel_spmd(nc, [arrays], core_ids=[0]).results[0]["out_0"]
```
